# Optimizing a Trainium2 kernel written in Bass

```python
import numpy as np
import jax
import jax.numpy as jnp

def _softmax(x, axis=-1):
    return jax.nn.softmax(x, axis=axis)

def _gelu(x):
    return jax.nn.gelu(x, approximate=True)

def _silu(x):
    return jax.nn.silu(x)

def _sigmoid(x):
    return jax.nn.sigmoid(x)

def _layernorm(x, axis=-1, eps=1e-05):
    m = jnp.mean(x, axis=axis, keepdims=True)
    v = jnp.var(x, axis=axis, keepdims=True)
    return (x - m) / jnp.sqrt(v + eps)

def _scatter_add(tgt, idx, src, axis=0):
    return tgt.at[idx].add(src)

def _segment_sum(src, seg, n):
    return jax.ops.segment_sum(src, seg, n)
kernel_name = 'mk_gnn_preln_d2_gnn_r8_11ff59'

def setup_inputs(seed: int=0):
    np.random.seed(seed)
    _w = jnp.asarray

    def _rec_inputs():
        import jax
        import jax.numpy as jnp
        _gk = jax.random.key(seed)
        x = -0.000202 + 1 * jax.random.normal(jax.random.fold_in(_gk, 1), (12500, 128), jnp.float32)
        src = jax.random.randint(jax.random.fold_in(_gk, 2), (200000,), 0, 12500, jnp.int32)
        dst = jnp.minimum((12500 * jax.random.uniform(jax.random.fold_in(_gk, 3), (200000,)) ** 2.0).astype(jnp.int32), 99999)
        _o = jnp.argsort(dst, stable=True)
        src = src[_o]
        dst = dst[_o]
        return (x, src, dst)
    x, src, dst = _rec_inputs()

    def _L0_gnn_setup():
        import jax, jax.numpy as jnp
        import numpy as np
        N = 6250
        E = 100000
        HID = 128
        NH = 8
        HD = 16
        FFN = 512
        EPS = 1e-05

        def _layer_norm(x, g, b):
            m = jnp.mean(x, axis=-1, keepdims=True)
            v = jnp.mean((x - m) ** 2, axis=-1, keepdims=True)
            return (x - m) * jax.lax.rsqrt(v + EPS) * g + b

        def _gnn_layer(x, edge_index, Wq, bq, Wk, bk, Wv, bv, Wo, bo, g1, b1, g2, b2, W1, bf1, W2, bf2):
            n = x.shape[0]
            residual = x
            h = _layer_norm(x, g1, b1)
            q = (h @ Wq + bq).reshape(n, NH, HD)
            k = (h @ Wk + bk).reshape(n, NH, HD)
            v = (h @ Wv + bv).reshape(n, NH, HD)
            src, dst = (edge_index[0], edge_index[1])
            deg = jax.ops.segment_sum(jnp.ones(src.shape, x.dtype), dst, num_segments=n)
            loops = jnp.arange(n, dtype=src.dtype)
            s_all = jnp.concatenate([src, loops])
            d_all = jnp.concatenate([dst, loops])
            e = jnp.sum(q[d_all] * k[s_all], axis=-1) / np.sqrt(HD).astype(np.float32)
            m = jax.lax.stop_gradient(jax.ops.segment_max(e, d_all, num_segments=n))
            p = jnp.exp(e - m[d_all])
            z = jax.ops.segment_sum(p, d_all, num_segments=n)
            alpha = p / z[d_all]
            agg = jax.ops.segment_sum(alpha[:, :, None] * v[s_all], d_all, num_segments=n)
            agg = jnp.where(deg[:, None, None] > 0, agg, jnp.zeros_like(agg))
            att = agg.reshape(n, NH * HD) @ Wo + bo
            x = residual + att
            residual = x
            h = _layer_norm(x, g2, b2)
            ffn = jax.nn.gelu(h @ W1 + bf1, approximate=False) @ W2 + bf2
            return residual + ffn
        key = jax.random.key(seed)
        ks = jax.random.split(key, 12)
        s = 0.02
        d = {}
        d['x'] = jax.random.normal(ks[0], (N, HID), jnp.float32)
        d['edge_index'] = jax.random.randint(ks[1], (2, E), 0, N, dtype=jnp.int32)
        d['Wq'] = jax.random.normal(ks[2], (HID, NH * HD), jnp.float32) * s
        d['bq'] = jnp.zeros((NH * HD,), jnp.float32)
        d['Wk'] = jax.random.normal(ks[3], (HID, NH * HD), jnp.float32) * s
        d['bk'] = jnp.zeros((NH * HD,), jnp.float32)
        d['Wv'] = jax.random.normal(ks[4], (HID, NH * HD), jnp.float32) * s
        d['bv'] = jnp.zeros((NH * HD,), jnp.float32)
        d['Wo'] = jax.random.normal(ks[5], (NH * HD, HID), jnp.float32) * s
        d['bo'] = jnp.zeros((HID,), jnp.float32)
        d['g1'] = jnp.ones((HID,), jnp.float32)
        d['b1'] = jnp.zeros((HID,), jnp.float32)
        d['g2'] = jnp.ones((HID,), jnp.float32)
        d['b2'] = jnp.zeros((HID,), jnp.float32)
        d['W1'] = jax.random.normal(ks[6], (HID, FFN), jnp.float32) * s
        d['bf1'] = jnp.zeros((FFN,), jnp.float32)
        d['W2'] = jax.random.normal(ks[7], (FFN, HID), jnp.float32) * s
        d['bf2'] = jnp.zeros((HID,), jnp.float32)
        return d
    _L0_gnn_all = _L0_gnn_setup()
    _L0_gnn_in = {k: v for k, v in _L0_gnn_all.items() if k in ('Wq', 'bq', 'Wk', 'bk', 'Wv', 'bv', 'Wo', 'bo', 'g1', 'b1', 'g2', 'b2', 'W1', 'bf1', 'W2', 'bf2')}
    del _L0_gnn_all

    def _L1_gnn_setup():
        import jax, jax.numpy as jnp
        import numpy as np
        N_NODES = 12500
        N_EDGES = 400000
        D = 128
        key = jax.random.key(seed)
        k_feat, k_src, k_dst, k_w1, k_w2 = jax.random.split(key, 5)
        feat = jax.random.normal(k_feat, (N_NODES, D), dtype=jnp.float32)
        src = jax.random.randint(k_src, (N_EDGES,), 0, N_NODES, dtype=jnp.int32)
        dst = jax.random.randint(k_dst, (N_EDGES,), 0, N_NODES, dtype=jnp.int32)
        eps = jnp.zeros((1,), dtype=jnp.float32)
        s1 = 1.0 / np.sqrt(D)
        W1 = jax.random.normal(k_w1, (D, D), dtype=jnp.float32) * s1
        b1 = jnp.zeros((D,), dtype=jnp.float32)
        W2 = jax.random.normal(k_w2, (D, D), dtype=jnp.float32) * s1
        b2 = jnp.zeros((D,), dtype=jnp.float32)
        return {'feat': feat, 'src': src, 'dst': dst, 'eps': eps, 'W1': W1, 'b1': b1, 'W2': W2, 'b2': b2}
    _L1_gnn_all = _L1_gnn_setup()
    _L1_gnn_in = {k: v for k, v in _L1_gnn_all.items() if k in ('eps', 'W1', 'b1', 'W2', 'b2')}
    del _L1_gnn_all
    return {'x': x, 'src': src, 'dst': dst, 'L0_gnn_Wq': _L0_gnn_in['Wq'], 'L0_gnn_bq': _L0_gnn_in['bq'], 'L0_gnn_Wk': _L0_gnn_in['Wk'], 'L0_gnn_bk': _L0_gnn_in['bk'], 'L0_gnn_Wv': _L0_gnn_in['Wv'], 'L0_gnn_bv': _L0_gnn_in['bv'], 'L0_gnn_Wo': _L0_gnn_in['Wo'], 'L0_gnn_bo': _L0_gnn_in['bo'], 'L0_gnn_g1': _L0_gnn_in['g1'], 'L0_gnn_b1': _L0_gnn_in['b1'], 'L0_gnn_g2': _L0_gnn_in['g2'], 'L0_gnn_b2': _L0_gnn_in['b2'], 'L0_gnn_W1': _L0_gnn_in['W1'], 'L0_gnn_bf1': _L0_gnn_in['bf1'], 'L0_gnn_W2': _L0_gnn_in['W2'], 'L0_gnn_bf2': _L0_gnn_in['bf2'], 'L1_gnn_eps': _L1_gnn_in['eps'], 'L1_gnn_W1': _L1_gnn_in['W1'], 'L1_gnn_b1': _L1_gnn_in['b1'], 'L1_gnn_W2': _L1_gnn_in['W2'], 'L1_gnn_b2': _L1_gnn_in['b2']}

def reference(x, src, dst, L0_gnn_Wq, L0_gnn_bq, L0_gnn_Wk, L0_gnn_bk, L0_gnn_Wv, L0_gnn_bv, L0_gnn_Wo, L0_gnn_bo, L0_gnn_g1, L0_gnn_b1, L0_gnn_g2, L0_gnn_b2, L0_gnn_W1, L0_gnn_bf1, L0_gnn_W2, L0_gnn_bf2, L1_gnn_eps, L1_gnn_W1, L1_gnn_b1, L1_gnn_W2, L1_gnn_b2):
    import jax
    import jax.numpy as jnp

    def _L0_gnn_ref(x, edge_index, Wq, bq, Wk, bk, Wv, bv, Wo, bo, g1, b1, g2, b2, W1, bf1, W2, bf2):
        import jax, jax.numpy as jnp
        import numpy as np
        N = 6250
        E = 100000
        HID = 128
        NH = 8
        HD = 16
        FFN = 512
        EPS = 1e-05

        def _layer_norm(x, g, b):
            m = jnp.mean(x, axis=-1, keepdims=True)
            v = jnp.mean((x - m) ** 2, axis=-1, keepdims=True)
            return (x - m) * jax.lax.rsqrt(v + EPS) * g + b

        def _gnn_layer(x, edge_index, Wq, bq, Wk, bk, Wv, bv, Wo, bo, g1, b1, g2, b2, W1, bf1, W2, bf2):
            n = x.shape[0]
            residual = x
            h = _layer_norm(x, g1, b1)
            q = (h @ Wq + bq).reshape(n, NH, HD)
            k = (h @ Wk + bk).reshape(n, NH, HD)
            v = (h @ Wv + bv).reshape(n, NH, HD)
            src, dst = (edge_index[0], edge_index[1])
            deg = jax.ops.segment_sum(jnp.ones(src.shape, x.dtype), dst, num_segments=n)
            loops = jnp.arange(n, dtype=src.dtype)
            s_all = jnp.concatenate([src, loops])
            d_all = jnp.concatenate([dst, loops])
            e = jnp.sum(q[d_all] * k[s_all], axis=-1) / np.sqrt(HD).astype(np.float32)
            m = jax.lax.stop_gradient(jax.ops.segment_max(e, d_all, num_segments=n))
            p = jnp.exp(e - m[d_all])
            z = jax.ops.segment_sum(p, d_all, num_segments=n)
            alpha = p / z[d_all]
            agg = jax.ops.segment_sum(alpha[:, :, None] * v[s_all], d_all, num_segments=n)
            agg = jnp.where(deg[:, None, None] > 0, agg, jnp.zeros_like(agg))
            att = agg.reshape(n, NH * HD) @ Wo + bo
            x = residual + att
            residual = x
            h = _layer_norm(x, g2, b2)
            ffn = jax.nn.gelu(h @ W1 + bf1, approximate=False) @ W2 + bf2
            return residual + ffn
        return _gnn_layer(x, edge_index, Wq, bq, Wk, bk, Wv, bv, Wo, bo, g1, b1, g2, b2, W1, bf1, W2, bf2)

    def _L1_gnn_ref(feat, src, dst, eps, W1, b1, W2, b2):
        import jax, jax.numpy as jnp
        import numpy as np
        N_NODES = 12500
        N_EDGES = 400000
        D = 128
        msgs = feat[src]
        neigh = jax.ops.segment_sum(msgs, dst, num_segments=feat.shape[0])
        h = (1.0 + eps[0]) * feat + neigh
        h = jax.nn.relu(h @ W1 + b1)
        out = h @ W2 + b2
        return out
    edge_index = jnp.stack([src, dst])
    h = jnp.maximum(_layernorm(x, axis=-1), 0.0)
    x = x + _L0_gnn_ref(h, edge_index, L0_gnn_Wq, L0_gnn_bq, L0_gnn_Wk, L0_gnn_bk, L0_gnn_Wv, L0_gnn_bv, L0_gnn_Wo, L0_gnn_bo, L0_gnn_g1, L0_gnn_b1, L0_gnn_g2, L0_gnn_b2, L0_gnn_W1, L0_gnn_bf1, L0_gnn_W2, L0_gnn_bf2)
    h = jnp.maximum(_layernorm(x, axis=-1), 0.0)
    x = x + _L1_gnn_ref(h, src, dst, L1_gnn_eps, L1_gnn_W1, L1_gnn_b1, L1_gnn_W2, L1_gnn_b2)
    return x

_drawn_inputs = setup_inputs


def setup_inputs(seed=0):
    import zlib

    import numpy as np

    out = dict(_drawn_inputs(seed))
    spreads = {'L0_gnn_bq': (0.0, 0.8),
     'L0_gnn_bk': (0.0, 2.0),
     'L0_gnn_bv': (0.0, 0.716),
     'L0_gnn_bo': (0.0, 0.38),
     'L0_gnn_g1': (1.0, 0.6),
     'L0_gnn_b1': (0.0, 0.8),
     'L0_gnn_g2': (1.0, 0.6),
     'L0_gnn_b2': (0.0, 0.8),
     'L0_gnn_bf1': (0.0, 0.512),
     'L0_gnn_bf2': (0.0, 0.298),
     'L1_gnn_b1': (0.0, 0.8),
     'L1_gnn_b2': (0.0, 0.699)}
    factors = {'L0_gnn_Wq': 8.0,
     'L0_gnn_Wk': 8.0,
     'L0_gnn_Wv': 8.0,
     'L0_gnn_Wo': 5.447,
     'L0_gnn_W1': 5.56,
     'L0_gnn_W2': 3.247}
    for name, (base, spread) in spreads.items():
        noise = np.random.default_rng([zlib.crc32(name.encode()), seed]).standard_normal(out[name].shape)
        drawn = base * np.exp(spread * noise) if base else spread * noise
        out[name] = jnp.asarray(drawn.astype(out[name].dtype))
    for name, factor in factors.items():
        out[name] = (out[name] * factor).astype(out[name].dtype)
    return out
```

```python
import concourse.bass as bass
from concourse import mybir
from contextlib import ExitStack

F32 = mybir.dt.float32
I32 = mybir.dt.int32
ALU = mybir.AluOpType
ACT = mybir.ActivationFunctionType
AX = mybir.AxisListType

P = 128
N = 12500
E = 200000
HID = 128
NH = 8
HD = HID // NH
FFN = 512
FC = FFN // P
LN_EPS = 1e-5

NODE_COLS = -(-N // P)
NP = P * NODE_COLS
FULL = N // NODE_COLS
REST = N - FULL * NODE_COLS
G = 7
PAIRS = NODE_COLS // (2 * G)
GW = G * HID
HALF = GW // 2

B = 16
BATCHES = -(-E // (P * B))
STEPS = B * BATCHES
EP = P * STEPS
EFULL = E // STEPS
EREST = E - EFULL * STEPS
BPAIRS = BATCHES // 2
SAMPLE = 32
SAMPLES = STEPS // SAMPLE
BLOCKS = EP // SAMPLE

HS = HD + 1
SW = NH * HS
RW = SW + NH
BIG = 1e30
NOWHERE = float(1 << 21)
SCALE = 1.0 / HD ** 0.5

ARENA = 28800
WEIGHTS = 24
PREP_DIAG, PREP_ALL = 6, 18
FIRSTS_SET, STARTS_SET, PLACED = 3, 7, 14

assert NODE_COLS % (2 * G) == 0 and BATCHES % 2 == 0 and STEPS % SAMPLE == 0


class Carve:

    def __init__(self, tensor):
        self.tensor, self.at = tensor, 0

    def take(self, *shape):
        n = 1
        for s in shape:
            n *= s
        part = self.tensor[:, self.at:self.at + n]
        self.at += n
        assert self.at <= ARENA, self.at
        if len(shape) == 1:
            return part
        names = "abc"[:len(shape)]
        return part.rearrange(f"p ({' '.join(names)}) -> p {' '.join(names)}", **dict(zip(names[1:], shape[1:])))

    def two(self, *shape):
        return [self.take(*shape) for _ in range(2)]


def spread(ap, n):
    return ap.unsqueeze(2).to_broadcast([ap.shape[0], ap.shape[1], n])


def repeat(eng, count, body, peel=1):
    for i in range(peel):
        body(i, i == 0)
    with eng.Fori(peel, count) as i:
        body(i, False)


def build(nc, a, out):
    ctx = ExitStack()
    with ctx:
        def sb(name, shape, dt=F32):
            return ctx.enter_context(nc.sbuf_tensor(name, shape, dt))

        def sem(name):
            return ctx.enter_context(nc.semaphore(name))

        def sem2(name):
            return [sem(f"{name}{k}") for k in range(2)]

        def dram(name, shape, dt=F32):
            return nc.dram_tensor(name, shape, dt).ap()

        q_tab = dram("q_tab", [NP, HID])
        kv_tab = dram("kv_tab", [NP, 2 * HID])
        h0_tab = dram("h0_tab", [NP, HID])
        h2_tab = dram("h2_tab", [NP, HID])
        q_edges = dram("q_edges", [EP + B, HID])
        states0 = dram("states0", [EP, RW])
        states1 = dram("states1", [EP, HID])
        dst_tab = dram("dst_tab", [EP // SAMPLE, SAMPLE], I32)
        last_tab = dram("last_tab", [NP + 1, 1], I32)

        def by_node(tab):
            return tab.rearrange("(p j) f -> p j f", j=NODE_COLS)

        def by_step(tab):
            return tab.rearrange("(p t) f -> p t f", t=STEPS)

        nodes = sb("nodes", [P, NODE_COLS, HID])
        src_all = sb("src_all", [P, STEPS + 2 * B], I32)
        keep = sb("keep", [P, STEPS + B])
        pen = sb("pen", [P, STEPS + B])
        ident = sb("ident", [P, P])
        ones = sb("ones", [P, P])
        earlier = sb("earlier", [P, P])
        same_dst = sb("same_dst", [P, P])
        same_pen = sb("same_pen", [P, P])
        has_edges = sb("has_edges", [P, NODE_COLS])
        start_i = sb("start_i", [P, NODE_COLS], I32)
        sum_i = sb("sum_i", [P, NODE_COLS + 2 * G], I32)
        patch_i = sb("patch_i", [P, 2], I32)
        chunk_start = sb("chunk_start", [P, 1], I32)
        first_i = sb("first_i", [P, 2], I32)
        q_first = sb("q_first", [P, HID])
        idx = [sb(f"idx{k}", [P, B], I32) for k in range(2)]
        eps_t = sb("eps_t", [P, 1])
        eps1 = sb("eps1", [P, 1])
        wqkv = sb("wqkv", [P, 3 * HID])
        bqkv = sb("bqkv", [1, 3 * HID])
        wo = sb("wo", [P, HID])
        bo = sb("bo", [P, HID])
        cols = sb("cols", [P, 4])
        w1 = sb("w1", [P, FFN])
        bf1 = sb("bf1", [P, FC])
        w2 = sb("w2", [P, FC, HID])
        bf2 = sb("bf2", [P, HID])
        gw1 = sb("gw1", [P, HID])
        gb1 = sb("gb1", [P, 1])
        gw2 = sb("gw2", [P, HID])
        gb2 = sb("gb2", [P, HID])
        arena = sb("arena", [P, ARENA])
        ps = ctx.enter_context(nc.psum_tensor("ps", [P, 8, 512], F32))

        def two_banks(b):
            flat = ps[:, b:b + 2, :].rearrange("p a b -> p (a b)")
            return flat[:, 0:GW], [flat[:, j * HID:(j + 1) * HID] for j in range(G)]

        def halves(b):
            return ps[:, b:b + 2, 0:HALF]

        LN_STEPS = ("own", "centred", "square", "var", "std", "out")

        class Norm:
            def __init__(self, tag, carve):
                self.s = {n: sem(f"{tag}_{n}") for n in LN_STEPS}
                self.sum, self.mean, self.rstd = carve.take(G), carve.take(G), carve.take(G)
                self.cen, self.sq = carve.take(G, HID), carve.take(G, HID)

        def norm_dve(dve, ln, n, x):
            nc.vector.tensor_reduce(ln.sum, x, AX.X, ALU.add).then_inc(ln.s["own"], 1)
            dve.wait_ge(ln.s["own"], n * 3 - 2)
            nc.vector.tensor_scalar_mul(ln.mean, ln.sum, -1.0 / HID).then_inc(ln.s["own"], 1)
            dve.wait_ge(ln.s["own"], n * 3 - 1)
            nc.vector.tensor_tensor(ln.cen, x, spread(ln.mean, HID), ALU.add).then_inc(ln.s["centred"], 1)
            dve.wait_ge(ln.s["square"], n)
            nc.vector.tensor_reduce(ln.sum, ln.sq, AX.X, ALU.add).then_inc(ln.s["var"], 1)
            dve.wait_ge(ln.s["std"], n)
            nc.vector.reciprocal(ln.rstd, ln.mean).then_inc(ln.s["own"], 1)
            dve.wait_ge(ln.s["own"], n * 3)

        def norm_act(act, ln, n):
            act.wait_ge(ln.s["centred"], n)
            nc.scalar.activation(ln.sq, ln.cen, ACT.Square).then_inc(ln.s["square"], 1)
            act.wait_ge(ln.s["var"], n)
            nc.scalar.activation(ln.mean, ln.sum, ACT.Sqrt, bias=eps_t[:], scale=1.0 / HID).then_inc(ln.s["std"], 1)

        def relu_norm(ln, to):
            return nc.vector.scalar_tensor_tensor(to, ln.cen, 0.0, spread(ln.rstd, HID), ALU.max, ALU.mult)

        cA = Carve(arena)
        zeros = cA.take(B, HID)
        dst_all = cA.take(STEPS).bitcast(I32)
        dst_f = cA.take(STEPS)
        last_row = cA.take(P)
        diag = cA.take(P)
        step_back = cA.take(P)
        back_one = cA.take(P)
        samples = cA.take(SAMPLES + 1)
        deltas = cA.take(SAMPLES + 1)
        row_node_i = cA.take(P).bitcast(I32)
        row_node = cA.take(P)
        node_i = cA.take(NODE_COLS).bitcast(I32)
        node_f = cA.take(NODE_COLS)
        col_i = cA.take(NODE_COLS).bitcast(I32)
        first_less_j = cA.take(NODE_COLS)
        block_f = cA.take(NODE_COLS)
        last_f = cA.take(NODE_COLS)
        last_i = cA.take(NODE_COLS).bitcast(I32)
        before_i = cA.take(NODE_COLS).bitcast(I32)
        before_f = cA.take(NODE_COLS)
        start_f = cA.take(NODE_COLS)
        minus1 = cA.take(1).bitcast(I32)
        chunk_i = cA.take(1).bitcast(I32)
        patch_raw = cA.take(1).bitcast(I32)
        patch_f = cA.take(4)
        starts_ge = cA.two(G, P)
        cmp2 = cA.take(G, SAMPLES)
        cnt2 = cA.take(G)
        blk2 = cA.take(G)
        look = cA.two(G, SAMPLE)
        cmp3 = cA.take(G, SAMPLE)
        cnt3 = cA.take(G)
        lnA = [Norm(f"lnA{t}", cA) for t in range(2)]
        h0_b = cA.two(G, HID)
        hn_b = cA.two(G, HID)
        hnT = cA.two(GW)
        kv_b = cA.two(G, 2 * HID)
        qs_b = cA.two(G, HID)

        memset_done = sem("memset_done")
        consts = sem("consts")
        masks = sem("masks")
        edges_in = sem("edges_in")
        x_in = sem("x_in")
        weights_in = sem("weights_in")
        q_zeroed = sem("q_zeroed")
        prep = sem("prep")
        sample_delta = sem("sample_delta")
        last_rows = sem("last_rows")
        dst_tab_in = sem("dst_tab_in")
        starts = sem("starts")
        sample_row = sem("sample_row")
        search_s = sem("search_s")
        block_idx = sem("block_idx")
        look_in = sem2("look_in")
        count_s = sem("count_s")
        last_s = sem("last_s")
        turns = sem("turns")
        hn_T = sem("hn_T")
        hnT_set = sem("hnT_set")
        qkv_ps = sem("qkv_ps")
        q_set = sem("q_set")
        kv_set = sem("kv_set")
        h0_stored, q_stored, kv_stored = sem2("h0_stored"), sem2("q_stored"), sem2("kv_stored")
        last_set = sem("last_set")
        last_stored = sem("last_stored")
        before_in = sem("before_in")
        place = sem("place")
        patch_in = sem("patch_in")
        qs_copied = sem("qs_copied")
        qs_out = sem2("qs_out")
        q_first_in = sem("q_first_in")
        q_first_out = sem("q_first_out")

        CW = B + 1
        cB = Carve(arena)
        kvb = cB.two(B, 2 * HID)
        qb = cB.two(B, HID)
        stb = cB.two(B, RW)
        score = cB.take(NH, CW)
        run_max = cB.take(NH * CW)
        top = cB.take(NH, CW)
        dif = cB.take(NH, CW)
        penb = cB.two(NH * CW + 1)
        keepb = cB.two(B)
        rescale = cB.take(NH)
        carried = cB.take(SW)
        no_q = cB.take(HID)
        diag8 = cB.take(NH, P)
        masked = cB.take(NH, P)
        carry_max = cB.take(NH)
        weight = cB.take(NH, P)
        weightT = cB.take(NH, P)
        carry = cB.take(NH, HS)
        patch_row = cB.take(RW)
        patch_top = cB.take(NH)
        patch_low = cB.take(2, NH)
        patch_w = cB.take(2, NH)
        patch_add = cB.take(NH, HS)

        edge_ready = sem("edge_ready")
        idx_set = sem("idx_set")
        gates_set = sem("gates_set")
        q_in, kv_in, states_out = sem2("q_in"), sem2("kv_in"), sem2("states_out")
        q_filled = sem("q_filled")
        prod_s, dif_s = sem("prod_s"), sem("dif_s")
        scan_s = sem("scan_s")
        probs_s, rescale_s, top_out = sem("probs_s"), sem("rescale_s"), sem("top_out")
        weighed_s, carried_s = sem("weighed_s"), sem("carried_s")
        state_s = sem("state_s")
        chunk_s = sem("chunk_s")
        tops_ps, weight_s, weightT_ps, weightT_s, carry_ps = (sem(n) for n in (
            "tops_ps", "weight_s", "weightT_ps", "weightT_s", "carry_ps"))
        patch_row_in, patch_exp, patch_done, patch_out = (sem(n) for n in (
            "patch_row_in", "patch_exp", "patch_done", "patch_out"))

        cC = Carve(arena)
        sg = cC.two(G, RW)
        qg = cC.two(G, HID)
        kvg = cC.two(G, 2 * HID)
        h0g = cC.two(G, HID)
        self_e = cC.two(G, NH)
        top_c = cC.two(G, NH)
        low_c = cC.two(2, G * NH)
        w_c = cC.two(2, G * NH)
        rden = cC.two(G, NH)
        xT = cC.two(GW)
        gT = cC.two(FC, GW)
        xb = cC.two(G, HID)
        hn2 = cC.two(G, HID)
        h2b = cC.two(G, HID)
        lnC = [Norm(f"lnC{t}", cC) for t in range(2)]

        sum_idx = sem("sum_idx")
        sg_in, ng_in = sem2("sg_in"), sem2("ng_in")
        attend_s = sem("attend_s")
        low1_s, w_cs, num_s, agg_s = (sem(n) for n in ("low1_s", "w_cs", "num_s", "agg_s"))
        (aggT_ps, aggT_s, att_ps, h0bo_s, x1_s, hnT2_ps, hnT2_s, ff1_ps, gelu_s, ff2_ps, xsum_s, x2_s) = (
            sem(n) for n in ("aggT_ps", "aggT_s", "att_ps", "h0bo_s", "x1_s", "hnT2_ps", "hnT2_s", "ff1_ps", "gelu_s",
                             "ff2_ps", "xsum_s", "x2_s"))
        h2_stored = sem2("h2_stored")

        cD = Carve(arena)
        rows = cD.two(B, HID)
        keepd = cD.two(B)
        sameT = cD.take(P)
        patch_row1 = cD.take(HID)
        idx1_set, keep1_set = sem("idx1_set"), sem("keep1_set")
        rows_in, sums_out = sem2("rows_in"), sem2("sums_out")
        sum_s = sem("sum_s")
        sameT_ps, sameT_s, carry1_ps, row1_in, row1_s, row1_out = (sem(n) for n in (
            "sameT_ps", "sameT_s", "carry1_ps", "row1_in", "row1_s", "row1_out"))

        cE = Carve(arena)
        ng = cE.two(G, HID)
        hg = cE.two(G, HID)
        hT = cE.two(GW)
        rT = cE.two(GW)
        end_idx, eps_set = sem("end_idx"), sem("eps_set")
        nsum_in, h2_in = sem2("nsum_in"), sem2("h2_in")
        masked_s, h_s, hT_ps, hT_s, mlp1_ps, relu_s, mlp2_ps, xb2_s, out_s = (sem(n) for n in (
            "masked_s", "h_s", "hT_ps", "hT_s", "mlp1_ps", "relu_s", "mlp2_ps", "xb2_s", "out_s"))
        out_stored = sem("out_stored")

        x_full = a["x"][0:FULL * NODE_COLS, :].rearrange("(p j) f -> p j f", j=NODE_COLS)
        x_rest = a["x"][FULL * NODE_COLS:N, :].rearrange("(p j) f -> p j f", p=1)
        LAST = (BATCHES - 1) % 2
        BW = 16 * B
        GWAIT = 16 * G

        def settle(eng):
            eng.sem_inc(turns, 1)

        block = ctx.enter_context(nc.Block())

        @block.sync
        def _(sp):
            sp.wait_ge(memset_done, 4)
            for to, frm in ((dst_all, a["dst"]), (src_all, a["src"])):
                sp.dma_start(to[0:EFULL, 0:STEPS], frm[0:EFULL * STEPS].rearrange("(p t) -> p t", t=STEPS))\
                    .then_inc(edges_in, 16)
                sp.dma_start(to[EFULL:EFULL + 1, 0:EREST], frm[EFULL * STEPS:E].rearrange("(p t) -> p t", p=1))\
                    .then_inc(edges_in, 16)
            sp.dma_start(nodes[0:FULL, :, :], x_full).then_inc(x_in, 16)
            sp.dma_start(nodes[FULL:FULL + 1, 0:REST, :], x_rest).then_inc(x_in, 16)
            sp.wait_ge(edges_in, 64)
            sp.dma_start(dst_tab.rearrange("(p b) s -> p (b s)", p=P), dst_all).then_inc(dst_tab_in, 16)

            with sp.Fori(0, BATCHES) as n:
                sp.dma_start(by_step(q_edges[0:EP, :])[:, bass.ds(n * B, B), :], zeros).then_inc(q_zeroed, 16)
            sp.dma_start(q_edges[EP:EP + B, :], zeros[0:B, 0, :]).then_inc(q_zeroed, 16)

            q_now = by_step(q_edges[0:EP, :])
            q_next = by_step(q_edges[B:EP + B, :])
            sp.wait_ge(q_first_out, 16)
            sp.wait_ge(edge_ready, 1)
            sp.dma_start(qb[0], q_now[:, 0:B, :]).then_inc(q_in[0], 16)

            def batch_b(i, first):
                for k in range(2):
                    n = i * 2 + k
                    sp.wait_ge(q_filled, n * B + 1)
                    settle(sp)
                    sp.dma_start(qb[1 - k], q_next[:, bass.ds(n * B, B), :]).then_inc(q_in[1 - k], 16)
                    sp.wait_ge(state_s, n * B + B)
                    settle(sp)
                    sp.wait_ge(top_out, n + 1)
                    settle(sp)
                    sp.dma_start(by_step(states0)[:, bass.ds(n * B, B), :], stb[k]).then_inc(states_out[k], 16)
            repeat(sp, BPAIRS, batch_b)

            sp.dma_start(nodes[0:FULL, :, :], x_full).then_inc(x_in, 16)
            sp.dma_start(nodes[FULL:FULL + 1, 0:REST, :], x_rest).then_inc(x_in, 16)
            sp.wait_ge(patch_out, 16)

            def group_c(i, first):
                for k in range(2):
                    g = (i * 2 + k) * G
                    if not first:
                        sp.wait_ge(x2_s, i * 2 + k - 1)
                        settle(sp)
                    for to, tab in ((qg, q_tab), (kvg, kv_tab), (h0g, h0_tab)):
                        sp.dma_start(to[k], by_node(tab)[:, bass.ds(g, G), :]).then_inc(ng_in[k], 16)
            repeat(sp, PAIRS, group_c)

            def batch_d(i, first):
                for k in range(2):
                    n = i * 2 + k
                    sp.wait_ge(sum_s, n * B + B + 1)
                    settle(sp)
                    sp.dma_start(by_step(states1)[:, bass.ds(n * B, B), :], rows[k]).then_inc(sums_out[k], 16)
            repeat(sp, BPAIRS, batch_d)

            sp.wait_ge(row1_out, 16)

            def group_e(i, first):
                for k in range(2):
                    g = (i * 2 + k) * G
                    if not first:
                        sp.wait_ge(hT_ps, i * 2 + k - 1)
                        settle(sp)
                    sp.dma_start(hg[k], by_node(h2_tab)[:, bass.ds(g, G), :]).then_inc(h2_in[k], 16)
            repeat(sp, PAIRS, group_e)
            for half in range(2):
                j0, j1 = half * PAIRS * G, (half + 1) * PAIRS * G
                sp.wait_ge(out_s, (half + 1) * PAIRS)
                sp.dma_start(out[0:FULL * NODE_COLS, :].rearrange("(p j) f -> p j f", j=NODE_COLS)[:, j0:j1, :],
                             nodes[0:FULL, j0:j1, :]).then_inc(out_stored, 16)
            sp.dma_start(out[FULL * NODE_COLS:N, :].rearrange("(p j) f -> p j f", p=1),
                         nodes[FULL:FULL + 1, 0:REST, :]).then_inc(out_stored, 16)
            sp.wait_ge(out_stored, 48)

        @block.gpsimd
        def _(pool):
            def gather(to, tab, at, done):
                pool.indirect_dma_start(to, None, tab, bass.IndirectOffsetOnAxis(ap=at, axis=0)).then_inc(done, 16)

            def scatter(tab, at, frm, done):
                pool.indirect_dma_start(tab, bass.IndirectOffsetOnAxis(ap=at, axis=0), frm, None,
                                        bounds_check=EP - 1, oob_is_err=False).then_inc(done, 16)

            nc.gpsimd.memset(ident[:], 0.0).then_inc(consts, 1)
            nc.gpsimd.memset(back_one, 0.0).then_inc(consts, 1)
            nc.gpsimd.memset(earlier[:], 1.0).then_inc(consts, 1)
            nc.gpsimd.memset(ones[:], 1.0).then_inc(consts, 1)
            nc.gpsimd.memset(eps_t[:], LN_EPS).then_inc(consts, 1)
            nc.gpsimd.memset(minus1, -1).then_inc(consts, 1)
            nc.gpsimd.iota(node_i, [[1, NODE_COLS]], base=0, channel_multiplier=NODE_COLS).then_inc(consts, 1)
            nc.gpsimd.iota(col_i, [[1, NODE_COLS]], base=0, channel_multiplier=0).then_inc(consts, 1)
            nc.gpsimd.iota(row_node_i, [[NODE_COLS, P]], base=0, channel_multiplier=0).then_inc(consts, 1)
            nc.gpsimd.iota(chunk_i, [[1, 1]], base=0, channel_multiplier=1).then_inc(consts, 1)
            nc.gpsimd.iota(chunk_start[:], [[1, 1]], base=0, channel_multiplier=STEPS).then_inc(consts, 1)
            pool.wait_ge(consts, 11)
            nc.gpsimd.affine_select(out=ident[:], in_=ident[:], compare_op=ALU.not_equal, fill=1.0, base=0,
                                    pattern=[[-1, P]], channel_multiplier=1).then_inc(masks, 1)
            nc.gpsimd.affine_select(out=back_one, in_=back_one, compare_op=ALU.not_equal, fill=1.0, base=1,
                                    pattern=[[-1, P]], channel_multiplier=1).then_inc(masks, 1)
            nc.gpsimd.affine_select(out=earlier[:], in_=earlier[:], compare_op=ALU.is_gt, fill=0.0, base=0,
                                    pattern=[[-1, P]], channel_multiplier=1).then_inc(masks, 1)

            def weight_in(to, frm):
                pool.dma_start(to, frm).then_inc(weights_in, 16)

            def column(name):
                return a[name].rearrange("(p o) -> p o", o=1)

            for t, name in enumerate(("g1", "b1", "g2", "b2")):
                weight_in(cols[:, t:t + 1], column("L0_gnn_" + name))
            for t, name in enumerate("qkv"):
                weight_in(wqkv[:, t * HID:(t + 1) * HID], a["L0_gnn_W" + name])
                weight_in(bqkv[:, t * HID:(t + 1) * HID], a["L0_gnn_b" + name].rearrange("(o f) -> o f", o=1))
            weight_in(wo[:], a["L0_gnn_Wo"])
            weight_in(w1[:], a["L0_gnn_W1"])
            weight_in(w2[:], a["L0_gnn_W2"].rearrange("(c p) f -> p c f", p=P))
            for c in range(FC):
                weight_in(bf1[:, c:c + 1], a["L0_gnn_bf1"][c * P:(c + 1) * P].rearrange("(p o) -> p o", o=1))
            for to, name in ((bo, "L0_gnn_bo"), (bf2, "L0_gnn_bf2"), (gb2, "L1_gnn_b2"), (eps1, "L1_gnn_eps")):
                weight_in(to[:], a[name].partition_broadcast(P))
            weight_in(gw1[:], a["L1_gnn_W1"])
            weight_in(gw2[:], a["L1_gnn_W2"])
            weight_in(gb1[:], column("L1_gnn_b1"))

            pool.wait_ge(dst_tab_in, 16)

            def search(i, first):
                for k in range(2):
                    pool.wait_ge(block_idx, i * 2 + k + 1)
                    settle(pool)
                    for j in range(G):
                        gather(look[k][:, j, :].bitcast(I32), dst_tab, idx[k][:, j:j + 1], look_in[k])
            repeat(pool, PAIRS, search)

            pool.wait_ge(place, FIRSTS_SET)
            pool.wait_ge(last_stored, 32)
            gather(patch_raw, last_tab, first_i[:, 1:2], patch_in)

            pool.wait_ge(q_zeroed, 16 * (BATCHES + 1))

            def scatter_q(i, first):
                for k in range(2):
                    pool.wait_ge(qs_copied, (i * 2 + k) * 2 + 2)
                    settle(pool)
                    for j in range(G):
                        scatter(q_edges, idx[k][:, j:j + 1], qs_b[k][:, j, :], qs_out[k])
            repeat(pool, PAIRS, scatter_q)
            for k in range(2):
                pool.wait_ge(q_stored[k], 16 * PAIRS)
            gather(q_first[:], q_tab, first_i[:, 0:1], q_first_in)
            pool.wait_ge(q_first_in, 16)
            for k in range(2):
                pool.wait_ge(qs_out[k], GWAIT * PAIRS)
            scatter(q_edges, chunk_start[:], q_first[:], q_first_out)

            for k in range(2):
                pool.wait_ge(kv_stored[k], 16 * PAIRS)
            pool.wait_ge(edge_ready, 1)

            def batch_b(i, first):
                for k in range(2):
                    n = i * 2 + k
                    pool.wait_ge(idx_set, n + 1)
                    if not first:
                        pool.wait_ge(weighed_s, n - 1)
                    settle(pool)
                    for b in range(B):
                        gather(kvb[k][:, b, :], kv_tab, idx[k][:, b:b + 1], kv_in[k])
            repeat(pool, BPAIRS, batch_b)

            for k in range(2):
                pool.wait_ge(states_out[k], 16 * BPAIRS)
            gather(patch_row, states0, patch_i[:, 0:1], patch_row_in)
            pool.wait_ge(patch_done, 1)
            scatter(states0, patch_i[:, 1:2], patch_row, patch_out)
            pool.wait_ge(patch_out, 16)

            def group_c(i, first):
                for k in range(2):
                    g = i * 2 + k
                    pool.wait_ge(sum_idx, g + 1)
                    if not first:
                        pool.wait_ge(num_s, g - 1)
                    settle(pool)
                    for j in range(G):
                        gather(sg[k][:, j, :], states0, idx[k][:, j:j + 1], sg_in[k])
                    pool.wait_ge(ng_in[k], i * 48 + 48)
                    nc.gpsimd.tensor_tensor(h0g[k], h0g[k], bo[:].unsqueeze(1).to_broadcast([P, G, HID]), ALU.add)\
                        .then_inc(h0bo_s, 1)
            repeat(pool, PAIRS, group_c)

            for k in range(2):
                pool.wait_ge(h2_stored[k], 16 * PAIRS)
            pool.wait_ge(sum_s, 1)

            def batch_d(i, first):
                for k in range(2):
                    n = i * 2 + k
                    pool.wait_ge(idx1_set, n + 1)
                    if not (first and k == 0):
                        pool.wait_ge(sum_s, (n - 1) * B + 2)
                    if not first:
                        pool.wait_ge(sums_out[k], i * 16)
                    settle(pool)
                    for b in range(B):
                        gather(rows[k][:, b, :], h2_tab, idx[k][:, b:b + 1], rows_in[k])
            repeat(pool, BPAIRS, batch_d)
            for k in range(2):
                pool.wait_ge(sums_out[k], 16 * BPAIRS)
            gather(patch_row1, states1, patch_i[:, 0:1], row1_in)
            pool.wait_ge(row1_s, 1)
            scatter(states1, patch_i[:, 1:2], patch_row1, row1_out)
            pool.wait_ge(row1_out, 16)

            def group_e(i, first):
                for k in range(2):
                    g = i * 2 + k
                    pool.wait_ge(end_idx, g + 1)
                    if not first:
                        pool.wait_ge(h_s, g - 1)
                    settle(pool)
                    for j in range(G):
                        gather(ng[k][:, j, :], states1, idx[k][:, j:j + 1], nsum_in[k])
            repeat(pool, PAIRS, group_e)

        @block.scalar
        def _(act):
            act.wait_ge(weights_in, 16 * WEIGHTS)
            act.wait_ge(masks, 3)

            def group_a(i, first):
                for k in range(2):
                    g = i * 2 + k
                    norm_act(act, lnA[0], g + 1)
                    norm_act(act, lnA[1], g + 1)
                    act.wait_ge(lnA[0].s["out"], g + 1)
                    act.dma_start(by_node(h0_tab)[:, bass.ds(g * G, G), :], h0_b[k]).then_inc(h0_stored[k], 16)
                    act.wait_ge(hn_T, g + 1)
                    nc.scalar.activation(hnT[k], two_banks(2 * k)[0], ACT.Identity, bias=cols[:, 1:2],
                                         scale=cols[:, 0:1]).then_inc(hnT_set, 1)
                    if not first:
                        act.wait_ge(kv_stored[k], i * 16)
                    for j in range(G):
                        m = g * G + j
                        bank = ps[:, 4 + (k * G + j) % 2, :]
                        act.wait_ge(qkv_ps, m + 1)
                        settle(act)
                        nc.scalar.copy(nodes[:, bass.ds(m, 1), :].rearrange("p a f -> p (a f)"), bank[:, 0:HID])\
                            .then_inc(q_set, 1)
                        nc.scalar.copy(kv_b[k][:, j, :], bank[:, HID:3 * HID]).then_inc(kv_set, 1)
                    act.wait_ge(q_set, g * G + G)
                    act.dma_start(by_node(q_tab)[:, bass.ds(g * G, G), :], nodes[:, bass.ds(g * G, G), :])\
                        .then_inc(q_stored[k], 16)
                    act.wait_ge(kv_set, g * G + G)
                    act.dma_start(by_node(kv_tab)[:, bass.ds(g * G, G), :], kv_b[k]).then_inc(kv_stored[k], 16)
            repeat(act, PAIRS, group_a)

            act.wait_ge(last_set, 1)
            act.dma_start(last_tab[0:1, :], minus1[0:1, :]).then_inc(last_stored, 16)
            act.dma_start(last_tab[1:NP + 1, :].rearrange("(p j) o -> p (j o)", j=NODE_COLS), last_i)\
                .then_inc(last_stored, 16)
            act.wait_ge(last_stored, 32)
            act.dma_start(before_i, last_tab[0:NP, :].rearrange("(p j) o -> p (j o)", j=NODE_COLS))\
                .then_inc(before_in, 16)

            act.wait_ge(place, STARTS_SET)

            def copy_q(i, first):
                for k in range(2):
                    g = (i * 2 + k) * G
                    if not first:
                        act.wait_ge(qs_out[k], i * GWAIT)
                        settle(act)
                    nc.scalar.copy(qs_b[k], nodes[:, bass.ds(g, G), :]).then_inc(qs_copied, 1)
                    nc.scalar.copy(idx[k][:, 0:G], start_i[:, bass.ds(g, G)]).then_inc(qs_copied, 1)
            repeat(act, PAIRS, copy_q)

            act.wait_ge(edge_ready, 1)
            for k in range(2):
                nc.scalar.copy(idx[k][:], src_all[:, k * B:(k + 1) * B]).then_inc(idx_set, 1)

            def gates(n, k):
                nc.scalar.copy(keepb[k], keep[:, bass.ds(n * B, B)]).then_inc(gates_set, 1)
                nc.scalar.copy(penb[k][:, 0:NH * CW].rearrange("p (h t) -> p h t", h=NH)[:, :, 1:CW],
                               pen[:, bass.ds(n * B, B)].unsqueeze(1).to_broadcast([P, NH, B])).then_inc(gates_set, 1)
            gates(0, 0)

            def batch_b(i, first):
                for k in range(2):
                    n = i * 2 + k
                    if not (first and k == 0):
                        act.wait_ge(state_s, n * B)
                        settle(act)
                    gates(n + 1, 1 - k)
                    act.wait_ge(prod_s, n + 1)
                    settle(act)
                    nc.scalar.copy(idx[k][:], src_all[:, bass.ds((n + 2) * B, B)]).then_inc(idx_set, 1)
                    act.wait_ge(dif_s, n + 1)
                    if not first:
                        act.wait_ge(states_out[k], i * 16)
                    heads = stb[k][:, :, 0:SW].rearrange("p b (h s) -> p h b s", s=HS)
                    nc.scalar.activation(heads[:, :, :, HD], dif[:, :, 1:CW], ACT.Exp, scale=SCALE)\
                        .then_inc(probs_s, 1)
                    nc.scalar.activation(rescale, dif[:, :, 0], ACT.Exp, scale=SCALE).then_inc(rescale_s, 1)
                    nc.scalar.copy(stb[k][:, :, SW:RW].rearrange("p b h -> p h b"), top[:, :, 1:CW])\
                        .then_inc(top_out, 1)
            repeat(act, BPAIRS, batch_b)

            act.wait_ge(chunk_s, 4)
            nc.scalar.activation(weight, masked, ACT.Exp, scale=SCALE).then_inc(weight_s, 1)
            act.wait_ge(weightT_ps, 1)
            nc.scalar.copy(weightT.rearrange("p h c -> p (h c)"), ps[:, 2:4, :].rearrange("p a b -> p (a b)"))\
                .then_inc(weightT_s, 1)
            act.wait_ge(chunk_s, 9)
            nc.scalar.activation(patch_w, patch_low, ACT.Exp, scale=SCALE).then_inc(patch_exp, 1)

            act.wait_ge(patch_out, 16)

            def exp_c(g, k):
                act.wait_ge(low1_s, g + 1)
                nc.scalar.activation(w_c[k], low_c[k], ACT.Exp, scale=SCALE).then_inc(w_cs, 1)

            def finish_c(g, k, stored):
                norm_act(act, lnC[1], g + 1)
                act.wait_ge(lnC[1].s["out"], g + 1)
                act.dma_start(by_node(h2_tab)[:, bass.ds(g * G, G), :], h2b[k]).then_inc(h2_stored[k], 16)

            def group_c(i, first):
                for k in range(2):
                    g = i * 2 + k
                    exp_c(g, k)
                    act.wait_ge(aggT_ps, g + 1)
                    nc.scalar.copy(xT[k], two_banks(4 * k)[0]).then_inc(aggT_s, 1)
                    if not (first and k == 0):
                        finish_c(g - 1, 1 - k, i)
                    norm_act(act, lnC[0], g + 1)
                    act.wait_ge(hnT2_ps, g + 1)
                    nc.scalar.activation(xT[k], two_banks(4 * k)[0], ACT.Identity, bias=cols[:, 3:4],
                                         scale=cols[:, 2:3]).then_inc(hnT2_s, 1)
                    for c in range(FC):
                        act.wait_ge(ff1_ps, g * FC + c + 1)
                        nc.scalar.activation(gT[k][:, c, :].rearrange("p (h f) -> p h f", h=2),
                                             halves(4 * k + 2 - 2 * (c % 2)), ACT.Gelu, bias=bf1[:, c:c + 1])\
                            .then_inc(gelu_s, 1)
            repeat(act, PAIRS, group_c)
            finish_c(2 * PAIRS - 1, 1, None)

            act.wait_ge(sum_s, 1)

            def batch_d(i, first):
                for k in range(2):
                    n = i * 2 + k
                    if not first:
                        act.wait_ge(sum_s, (n - 1) * B + 1)
                        settle(act)
                    nc.scalar.copy(keepd[k], keep[:, bass.ds(n * B, B)]).then_inc(keep1_set, 1)
                    nc.scalar.copy(idx[k][:], src_all[:, bass.ds(n * B, B)]).then_inc(idx1_set, 1)
            repeat(act, BPAIRS, batch_d)
            act.wait_ge(sameT_ps, 1)
            nc.scalar.copy(sameT, ps[:, 0, 0:P]).then_inc(sameT_s, 1)

            def group_e(i, first):
                for k in range(2):
                    g = i * 2 + k
                    act.wait_ge(hT_ps, g + 1)
                    nc.scalar.copy(hT[k], two_banks(4 * k)[0]).then_inc(hT_s, 1)
                    act.wait_ge(mlp1_ps, g + 1)
                    nc.scalar.activation(rT[k].rearrange("p (h f) -> p h f", h=2), halves(4 * k + 2), ACT.Relu,
                                         bias=gb1[:]).then_inc(relu_s, 1)
            repeat(act, PAIRS, group_e)

        @block.tensor
        def _(pe):
            pe.wait_ge(prep, PREP_DIAG)
            nc.tensor.matmul(ps[:, 6, 0:P], ones[:], diag, start=True, stop=True).then_inc(last_rows, 1)
            nc.tensor.matmul(ps[:, 7, 0:SAMPLES + 1], step_back, samples, start=True, stop=True)\
                .then_inc(sample_delta, 1)
            pe.wait_ge(weights_in, 16 * WEIGHTS)
            pe.wait_ge(prep, PREP_ALL)

            def group_a(i, first):
                for k in range(2):
                    g = i * 2 + k
                    pe.wait_ge(starts, g + 1)
                    for j in range(G):
                        done = nc.tensor.matmul(ps[:, 6 + k, j * (SAMPLES + 1):(j + 1) * (SAMPLES + 1)],
                                                starts_ge[k][:, j, :], deltas, start=True, stop=True)
                    done.then_inc(sample_row, 1)
                    pe.wait_ge(lnA[1].s["out"], g + 1)
                    for j in range(G):
                        done = nc.tensor.transpose(two_banks(2 * k)[1][j], hn_b[k][:, j, :], ident[:])
                    done.then_inc(hn_T, 1)
                    pe.wait_ge(hnT_set, g + 1)
                    for j in range(G):
                        m = g * G + j
                        bank = ps[:, 4 + (k * G + j) % 2, 0:3 * HID]
                        if not (first and k * G + j < 2):
                            pe.wait_ge(kv_set, m - 1)
                            pe.wait_ge(q_set, m - 1)
                        nc.tensor.matmul(bank, ones[0:1, :], bqkv[:], start=True, stop=False)
                        nc.tensor.matmul(bank, hnT[k][:, j * HID:(j + 1) * HID], wqkv[:], start=False, stop=True)\
                            .then_inc(qkv_ps, 1)
            repeat(pe, PAIRS, group_a)

            pe.wait_ge(chunk_s, 1)
            for t in range(2):
                done = nc.tensor.matmul(ps[:, t, :], ones[:], diag8[:, 4 * t:4 * t + 4, :].rearrange("p h c -> p (h c)"),
                                        start=True, stop=True)
            done.then_inc(tops_ps, 1)
            pe.wait_ge(chunk_s, 5)
            for h in range(NH):
                done = nc.tensor.transpose(ps[:, 2 + h // 4, (h % 4) * P:(h % 4 + 1) * P], weight[:, h, :], ident[:])
            done.then_inc(weightT_ps, 1)
            pe.wait_ge(weightT_s, 1)
            for h in range(NH):
                done = nc.tensor.matmul(ps[:, 4, h * HS:(h + 1) * HS], weightT[:, h, :],
                                        stb[LAST][:, B - 1, h * HS:(h + 1) * HS], start=True, stop=True)
            done.then_inc(carry_ps, 1)

            def group_c(i, first):
                for k in range(2):
                    g = i * 2 + k
                    flat, tiles = two_banks(4 * k)
                    flat2, tiles2 = two_banks(4 * k + 2)
                    pe.wait_ge(agg_s, g + 1)
                    for j in range(G):
                        done = nc.tensor.transpose(tiles[j], qg[k][:, j, :], ident[:])
                    done.then_inc(aggT_ps, 1)
                    pe.wait_ge(aggT_s, g + 1)
                    if not first:
                        pe.wait_ge(x2_s, g - 1)
                    for j in range(G):
                        done = nc.tensor.matmul(tiles2[j], xT[k][:, j * HID:(j + 1) * HID], wo[:], start=True, stop=True)
                    done.then_inc(att_ps, 1)
                    pe.wait_ge(lnC[0].s["out"], g + 1)
                    for j in range(G):
                        done = nc.tensor.transpose(tiles[j], hn2[k][:, j, :], ident[:])
                    done.then_inc(hnT2_ps, 1)
                    pe.wait_ge(hnT2_s, g + 1)
                    for c in range(FC):
                        if c >= 2:
                            pe.wait_ge(gelu_s, g * FC + c - 1)
                        for h in range(2):
                            done = nc.tensor.matmul(halves(4 * k + 2 - 2 * (c % 2))[:, h, :], w1[:, c * P:(c + 1) * P],
                                                    xT[k][:, h * HALF:(h + 1) * HALF], start=True, stop=True)
                        done.then_inc(ff1_ps, 1)
                    pe.wait_ge(gelu_s, g * FC + FC)
                    for j in range(G):
                        for c in range(FC):
                            done = nc.tensor.matmul(tiles2[j], gT[k][:, c, j * HID:(j + 1) * HID], w2[:, c, :],
                                                    start=(c == 0), stop=(c == FC - 1))
                    done.then_inc(ff2_ps, 1)
            repeat(pe, PAIRS, group_c)

            nc.tensor.transpose(ps[:, 0, 0:P], same_dst[:], ident[:]).then_inc(sameT_ps, 1)
            pe.wait_ge(sameT_s, 1)
            pe.wait_ge(sum_s, STEPS + 1)
            nc.tensor.matmul(ps[:, 1, 0:HID], sameT, rows[LAST][:, B - 1, :], start=True, stop=True)\
                .then_inc(carry1_ps, 1)
            pe.wait_ge(row1_s, 1)

            def group_e(i, first):
                for k in range(2):
                    g = i * 2 + k
                    flat, tiles = two_banks(4 * k)
                    pe.wait_ge(h_s, g + 1)
                    if not first:
                        pe.wait_ge(out_s, g - 1)
                    for j in range(G):
                        done = nc.tensor.transpose(tiles[j], hg[k][:, j, :], ident[:])
                    done.then_inc(hT_ps, 1)
                    pe.wait_ge(hT_s, g + 1)
                    for h in range(2):
                        done = nc.tensor.matmul(halves(4 * k + 2)[:, h, :], gw1[:], hT[k][:, h * HALF:(h + 1) * HALF],
                                                start=True, stop=True)
                    done.then_inc(mlp1_ps, 1)
                    pe.wait_ge(relu_s, g + 1)
                    for j in range(G):
                        done = nc.tensor.matmul(tiles[j], rT[k][:, j * HID:(j + 1) * HID], gw2[:], start=True, stop=True)
                    done.then_inc(mlp2_ps, 1)
            repeat(pe, PAIRS, group_e)

        @block.vector
        def _(dve):
            nc.vector.memset(zeros, 0.0).then_inc(memset_done, 1)
            nc.vector.memset(dst_all, N).then_inc(memset_done, 1)
            nc.vector.memset(src_all[:], 0).then_inc(memset_done, 1)
            nc.vector.memset(nodes[FULL // 32 * 32:P, REST:NODE_COLS, :], 0.0).then_inc(memset_done, 1)

            steps = [0]

            def step(ins):
                steps[0] += 1
                ins.then_inc(prep, 1)
                dve.wait_ge(prep, steps[0])

            step(nc.vector.memset(sum_i[:], 0))
            dve.wait_ge(consts, 11)
            dve.wait_ge(masks, 3)
            dve.wait_ge(edges_in, 64)
            step(nc.vector.tensor_copy(dst_f, dst_all))
            step(nc.vector.tensor_scalar(diag, ident[:], dst_f[:, STEPS - 1:STEPS], None, ALU.mult))
            step(nc.vector.tensor_copy(samples[:, 0:SAMPLES], dst_f[:, 0:STEPS:SAMPLE]))
            step(nc.vector.tensor_copy(samples[:, SAMPLES:SAMPLES + 1], chunk_i))
            step(nc.vector.tensor_tensor(step_back, ident[:], back_one, ALU.subtract))
            assert steps[0] == PREP_DIAG
            step(nc.vector.tensor_copy(node_f, node_i))
            step(nc.vector.tensor_copy(row_node, row_node_i))
            step(nc.vector.tensor_copy(first_less_j, col_i))
            step(nc.vector.tensor_scalar(first_less_j, first_less_j, -1.0, dst_f[:, 0:1], ALU.mult, ALU.add))
            step(nc.vector.memset(first_less_j[0:1, :], -float(NP)))
            step(nc.vector.memset(keep[:], 0.0))
            step(nc.vector.tensor_tensor(keep[:, 1:STEPS], dst_f[:, 1:STEPS], dst_f[:, 0:STEPS - 1], ALU.is_equal))
            step(nc.vector.tensor_scalar(pen[:], keep[:], -1.0, BIG, ALU.add, ALU.mult))
            dve.wait_ge(last_rows, 1)
            step(nc.vector.tensor_scalar(last_row, ps[:, 6, 0:P], dst_f[:, 0:1], None, ALU.is_equal))
            step(nc.vector.tensor_tensor(same_dst[:], last_row, earlier[:], ALU.mult))
            step(nc.vector.tensor_scalar(same_pen[:], same_dst[:], -1.0, BIG, ALU.add, ALU.mult))
            dve.wait_ge(sample_delta, 1)
            step(nc.vector.tensor_copy(deltas, ps[:, 7, 0:SAMPLES + 1]))
            assert steps[0] == PREP_ALL
            dve.wait_ge(x_in, 32)

            def last_edges(g, k, i):
                cols_g = bass.ds(g * G, G)
                dve.wait_ge(look_in[k], i * GWAIT + GWAIT)
                nc.vector.tensor_tensor(cmp3, look[k].bitcast(I32), spread(node_f[:, cols_g], SAMPLE), ALU.is_le)\
                    .then_inc(count_s, 1)
                dve.wait_ge(count_s, g * 2 + 1)
                nc.vector.tensor_reduce(cnt3, cmp3, AX.X, ALU.add).then_inc(count_s, 1)
                dve.wait_ge(count_s, g * 2 + 2)
                nc.vector.scalar_tensor_tensor(last_f[:, cols_g], block_f[:, cols_g], float(SAMPLE), cnt3,
                                               ALU.mult, ALU.add).then_inc(last_s, 1)

            def group_a(i, first):
                for k in range(2):
                    g = i * 2 + k
                    cols_g = bass.ds(g * G, G)
                    nc.vector.tensor_tensor(starts_ge[k], row_node.unsqueeze(1).to_broadcast([P, G, P]),
                                            spread(first_less_j[:, cols_g], P), ALU.is_ge).then_inc(starts, 1)
                    settle(dve)
                    norm_dve(dve, lnA[0], g + 1, nodes[:, cols_g, :])
                    if not first:
                        dve.wait_ge(h0_stored[k], i * 16)
                    relu_norm(lnA[0], h0_b[k]).then_inc(lnA[0].s["out"], 1)
                    dve.wait_ge(lnA[0].s["out"], g + 1)
                    norm_dve(dve, lnA[1], g + 1, h0_b[k])
                    if not first:
                        dve.wait_ge(hn_T, g - 1)
                    nc.vector.tensor_tensor(hn_b[k], lnA[1].cen, spread(lnA[1].rstd, HID), ALU.mult)\
                        .then_inc(lnA[1].s["out"], 1)
                    if not first:
                        last_edges(g - 2, k, i - 1)
                    dve.wait_ge(sample_row, g + 1)
                    got = ps[:, 6 + k, 0:G * (SAMPLES + 1)].rearrange("p (j s) -> p j s", j=G)
                    nc.vector.tensor_tensor(cmp2, got[:, :, 0:SAMPLES], spread(node_f[:, cols_g], SAMPLES), ALU.is_le)\
                        .then_inc(search_s, 1)
                    dve.wait_ge(search_s, g * 4 + 1)
                    nc.vector.tensor_reduce(cnt2, cmp2, AX.X, ALU.add).then_inc(search_s, 1)
                    dve.wait_ge(search_s, g * 4 + 2)
                    nc.vector.tensor_scalar(blk2, cnt2, -1.0, 0.0, ALU.add, ALU.max).then_inc(search_s, 1)
                    dve.wait_ge(search_s, g * 4 + 3)
                    nc.vector.scalar_tensor_tensor(block_f[:, cols_g], got[:, :, SAMPLES], float(SAMPLES), blk2,
                                                   ALU.mult, ALU.add).then_inc(search_s, 1)
                    dve.wait_ge(search_s, g * 4 + 4)
                    nc.vector.tensor_scalar_add(idx[k][:, 0:G], block_f[:, cols_g], 0.0).then_inc(block_idx, 1)
            repeat(dve, PAIRS, group_a)
            for k in range(2):
                last_edges(2 * PAIRS - 2 + k, k, PAIRS - 1)

            placed = [0]

            def stage(ins):
                placed[0] += 1
                ins.then_inc(place, 1)
                dve.wait_ge(place, placed[0])

            dve.wait_ge(last_s, 2 * PAIRS)
            stage(nc.vector.tensor_scalar_add(last_f, last_f, -1.0))
            nc.vector.tensor_copy(last_i, last_f).then_inc(last_set, 1)
            stage(nc.vector.tensor_copy(first_i[:, 0:1], dst_f[:, 0:1]))
            stage(nc.vector.tensor_scalar_add(first_i[:, 1:2], dst_f[:, 0:1], 1.0))
            assert placed[0] == FIRSTS_SET
            dve.wait_ge(before_in, 16)
            stage(nc.vector.tensor_copy(before_f, before_i))
            stage(nc.vector.tensor_tensor(has_edges[:], last_f, before_f, ALU.is_gt))
            stage(nc.vector.tensor_scalar(start_f, has_edges[:], -NOWHERE, NOWHERE + 1.0, ALU.mult, ALU.add))
            stage(nc.vector.tensor_tensor(start_i[:], start_f, before_f, ALU.add))
            assert placed[0] == STARTS_SET
            stage(nc.vector.tensor_scalar_max(sum_i[:, 0:NODE_COLS], last_f, 0.0))
            dve.wait_ge(patch_in, 16)
            stage(nc.vector.tensor_copy(patch_f[:, 0:1], patch_raw))
            stage(nc.vector.tensor_copy(patch_f[:, 1:2], chunk_start[:]))
            stage(nc.vector.tensor_scalar_add(patch_f[:, 1:2], patch_f[:, 1:2], float(STEPS)))
            stage(nc.vector.tensor_tensor(patch_f[:, 2:3], patch_f[:, 0:1], patch_f[:, 1:2], ALU.is_ge))
            stage(nc.vector.tensor_copy(patch_i[:, 0:1], patch_f[:, 0:1]))
            stage(nc.vector.scalar_tensor_tensor(patch_i[:, 1:2], patch_f[:, 2:3], NOWHERE, patch_f[:, 0:1],
                                                 ALU.mult, ALU.add))
            assert placed[0] == PLACED

            dve.wait_ge(q_first_out, 16)
            dve.wait_ge(q_zeroed, 16 * (BATCHES + 1))
            for k in range(2):
                dve.wait_ge(h0_stored[k], 16 * PAIRS)
                dve.wait_ge(q_stored[k], 16 * PAIRS)
                dve.wait_ge(kv_stored[k], 16 * PAIRS)
                dve.wait_ge(qs_out[k], GWAIT * PAIRS)
            nc.vector.memset(no_q, 0.0)
            nc.vector.memset(stb[1][:, B - 1, :], 0.0)
            nc.vector.memset(top, -BIG)
            for k in range(2):
                done = nc.vector.memset(penb[k], -BIG)
            done.then_inc(edge_ready, 1)

            def fill(n, k, b, value):
                if b is None:
                    return
                before = (no_q if value is None else qb[1 - k][:, B - 1, :]) if b == 0 else qb[k][:, b - 1, :]
                if not (b == 0 and value is None):
                    dve.wait_ge(q_filled, n * B + b)
                nc.vector.scalar_tensor_tensor(qb[k][:, b, :], before, keepb[k][:, b:b + 1], qb[k][:, b, :],
                                               ALU.mult, ALU.add).then_inc(q_filled, 1)

            dve.wait_ge(edge_ready, 1)
            dve.wait_ge(gates_set, 2)
            dve.wait_ge(q_in[0], 16)
            for b in range(B):
                fill(0, 0, b, None)

            AHEAD = 4

            def batch_b(i, first):
                for k in range(2):
                    n = i * 2 + k
                    other = 1 - k
                    st = stb[k][:, :, 0:SW]
                    dve.wait_ge(q_filled, n * B + B)
                    dve.wait_ge(kv_in[k], i * BW + BW)
                    keys = kvb[k][:, :, 0:HID]
                    nc.vector.tensor_tensor(keys, keys, qb[k], ALU.mult).then_inc(prod_s, 1)
                    if not (first and k == 0):
                        dve.wait_ge(scan_s, n * 4)
                    nc.vector.tensor_copy(score[:, :, 0], top[:, :, B]).then_inc(scan_s, 1)
                    dve.wait_ge(prod_s, n + 1)
                    nc.vector.tensor_reduce(score[:, :, 1:CW].rearrange("p h t -> p t h"),
                                            keys.rearrange("p b (h d) -> p b h d", d=HD), AX.X, ALU.add)\
                        .then_inc(scan_s, 1)
                    dve.wait_ge(scan_s, n * 4 + 1)
                    dve.wait_ge(scan_s, n * 4 + 2)
                    flat = score.rearrange("p h t -> p (h t)")
                    nc.vector.tensor_tensor_scan(run_max, penb[k][:, 0:NH * CW], flat, 0.0, ALU.add, ALU.max)\
                        .then_inc(scan_s, 1)
                    dve.wait_ge(scan_s, n * 4 + 3)
                    if not (first and k == 0):
                        dve.wait_ge(top_out, n)
                    nc.vector.tensor_tensor_scan(top.rearrange("p h t -> p (h t)")[:, ::-1],
                                                 penb[k][:, 1:NH * CW + 1][:, ::-1], run_max[:, ::-1], 0.0,
                                                 ALU.add, ALU.max).then_inc(scan_s, 1)
                    dve.wait_ge(scan_s, n * 4 + 4)
                    if not (first and k == 0):
                        dve.wait_ge(rescale_s, n)
                    nc.vector.tensor_tensor(dif, score, top, ALU.subtract).then_inc(dif_s, 1)
                    dve.wait_ge(gates_set, n * 2 + 4)
                    if k == 0:
                        dve.wait_ge(q_in[1], i * 16 + 16)
                    else:
                        dve.wait_ge(q_in[0], i * 16 + 32)
                    for b in range(AHEAD):
                        fill(n + 1, other, b, n)
                    dve.wait_ge(probs_s, n + 1)
                    heads = st.rearrange("p b (h s) -> p b h s", s=HS)
                    nc.vector.tensor_tensor(heads[:, :, :, 0:HD],
                                            kvb[k][:, :, HID:2 * HID].rearrange("p b (h d) -> p b h d", d=HD),
                                            heads[:, :, :, HD:HS].to_broadcast([P, B, NH, HD]), ALU.mult)\
                        .then_inc(weighed_s, 1)
                    dve.wait_ge(rescale_s, n + 1)
                    nc.vector.tensor_tensor(carried.rearrange("p (h s) -> p h s", s=HS),
                                            stb[other][:, B - 1, 0:SW].rearrange("p (h s) -> p h s", s=HS),
                                            spread(rescale, HS), ALU.mult).then_inc(carried_s, 1)
                    dve.wait_ge(weighed_s, n + 1)
                    dve.wait_ge(carried_s, n + 1)
                    for b in range(B):
                        if b:
                            dve.wait_ge(state_s, n * B + b)
                        nc.vector.scalar_tensor_tensor(st[:, b, :], st[:, b - 1, :] if b else carried,
                                                       keepb[k][:, b:b + 1], st[:, b, :], ALU.mult, ALU.add)\
                            .then_inc(state_s, 1)
                        if b + AHEAD < B:
                            fill(n + 1, other, b + AHEAD, n)
            repeat(dve, BPAIRS, batch_b)

            chunked = [0]

            def link(ins):
                chunked[0] += 1
                ins.then_inc(chunk_s, 1)
                dve.wait_ge(chunk_s, chunked[0])

            dve.wait_ge(top_out, BATCHES)
            ends = stb[LAST][:, B - 1, :]
            link(nc.vector.tensor_tensor(diag8, ident[:].unsqueeze(1).to_broadcast([P, NH, P]), spread(ends[:, SW:RW], P),
                                         ALU.mult))
            dve.wait_ge(tops_ps, 1)
            link(nc.vector.tensor_tensor(masked, ps[:, 0:2, :].rearrange("p a (h c) -> p (a h) c", c=P),
                                         same_pen[:].unsqueeze(1).to_broadcast([P, NH, P]), ALU.add))
            link(nc.vector.tensor_reduce(carry_max, masked, AX.X, ALU.max))
            link(nc.vector.tensor_tensor(masked, masked, spread(carry_max, P), ALU.subtract))
            dve.wait_ge(weight_s, 1)
            link(nc.vector.tensor_tensor(weight, weight, same_dst[:].unsqueeze(1).to_broadcast([P, NH, P]), ALU.mult))
            dve.wait_ge(patch_row_in, 16)
            link(nc.vector.tensor_tensor(patch_top, patch_row[:, SW:RW], carry_max, ALU.max))
            link(nc.vector.tensor_tensor(patch_low[:, 0, :], patch_row[:, SW:RW], patch_top, ALU.subtract))
            link(nc.vector.tensor_tensor(patch_low[:, 1, :], carry_max, patch_top, ALU.subtract))
            link(nc.vector.tensor_copy(patch_row[:, SW:RW], patch_top))
            dve.wait_ge(patch_exp, 1)
            by_head = patch_row[:, 0:SW].rearrange("p (h s) -> p h s", s=HS)
            link(nc.vector.tensor_tensor(by_head, by_head, spread(patch_w[:, 0, :], HS), ALU.mult))
            dve.wait_ge(carry_ps, 1)
            link(nc.vector.tensor_tensor(patch_add, ps[:, 4, 0:SW].rearrange("p (h s) -> p h s", s=HS),
                                         spread(patch_w[:, 1, :], HS), ALU.mult))
            nc.vector.tensor_tensor(by_head, by_head, patch_add, ALU.add).then_inc(patch_done, 1)

            dve.wait_ge(patch_out, 16)
            dve.wait_ge(x_in, 64)
            for k in range(2):
                nc.vector.tensor_copy(idx[k][:, 0:G], sum_i[:, k * G:(k + 1) * G]).then_inc(sum_idx, 1)

            def attend(g, k, i):
                n = g + 1
                dve.wait_ge(ng_in[k], i * 48 + 48)
                keys, vals = kvg[k][:, :, 0:HID], kvg[k][:, :, HID:2 * HID]
                vals_h = vals.rearrange("p j (h d) -> p j h d", d=HD)
                nc.vector.tensor_tensor(qg[k], qg[k], keys, ALU.mult).then_inc(attend_s, 1)
                dve.wait_ge(attend_s, g * 9 + 1)
                nc.vector.tensor_reduce(self_e[k], qg[k].rearrange("p j (h d) -> p j h d", d=HD), AX.X, ALU.add)\
                    .then_inc(attend_s, 1)
                dve.wait_ge(attend_s, g * 9 + 2)
                dve.wait_ge(sg_in[k], i * GWAIT + GWAIT)
                tops = sg[k][:, :, SW:RW]
                low = [low_c[k][:, t, :].rearrange("p (j h) -> p j h", h=NH) for t in range(2)]
                w = [w_c[k][:, t, :].rearrange("p (j h) -> p j h", h=NH) for t in range(2)]
                nc.vector.tensor_tensor(top_c[k], tops, self_e[k], ALU.max).then_inc(attend_s, 1)
                dve.wait_ge(attend_s, g * 9 + 3)
                nc.vector.tensor_tensor(low[0], tops, top_c[k], ALU.subtract).then_inc(attend_s, 1)
                nc.vector.tensor_tensor(low[1], self_e[k], top_c[k], ALU.subtract).then_inc(low1_s, 1)
                dve.wait_ge(w_cs, n)
                states = sg[k][:, :, 0:SW].rearrange("p j (h s) -> p j h s", s=HS)
                nc.vector.tensor_tensor(states, states, w[0].unsqueeze(3).to_broadcast([P, G, NH, HS]), ALU.mult)\
                    .then_inc(attend_s, 1)
                nc.vector.tensor_tensor(vals_h, vals_h, w[1].unsqueeze(3).to_broadcast([P, G, NH, HD]), ALU.mult)\
                    .then_inc(attend_s, 1)
                dve.wait_ge(attend_s, g * 9 + 5)
                nc.vector.tensor_tensor(rden[k], states[:, :, :, HD], w[1], ALU.add).then_inc(attend_s, 1)
                dve.wait_ge(attend_s, g * 9 + 6)
                nc.vector.tensor_tensor(vals_h, vals_h, states[:, :, :, 0:HD], ALU.add).then_inc(num_s, 1)
                dve.wait_ge(attend_s, g * 9 + 7)
                nc.vector.reciprocal(rden[k], rden[k]).then_inc(attend_s, 1)
                dve.wait_ge(attend_s, g * 9 + 8)
                nc.vector.tensor_tensor(rden[k], rden[k], spread(has_edges[:, bass.ds(g * G, G)], NH), ALU.mult)\
                    .then_inc(attend_s, 1)
                dve.wait_ge(attend_s, g * 9 + 9)
                dve.wait_ge(num_s, n)
                nc.vector.tensor_tensor(qg[k].rearrange("p j (h d) -> p j h d", d=HD), vals_h,
                                        rden[k].unsqueeze(3).to_broadcast([P, G, NH, HD]), ALU.mult).then_inc(agg_s, 1)
                nc.vector.tensor_copy(idx[k][:, 0:G], sum_i[:, bass.ds((g + 2) * G, G)]).then_inc(sum_idx, 1)

            def finish(g, k, i, fresh):
                n = g + 1
                here = nodes[:, bass.ds(g * G, G), :]
                nc.vector.tensor_tensor(xb[k], h0g[k], bf2[:].unsqueeze(1).to_broadcast([P, G, HID]), ALU.add)\
                    .then_inc(xsum_s, 1)
                dve.wait_ge(xsum_s, g * 2 + 1)
                nc.vector.tensor_tensor(xb[k], xb[k], here, ALU.add).then_inc(xsum_s, 1)
                dve.wait_ge(xsum_s, g * 2 + 2)
                dve.wait_ge(ff2_ps, n)
                tiles = two_banks(4 * k + 2)[0].rearrange("p (j f) -> p j f", j=G)
                nc.vector.tensor_tensor(here, tiles, xb[k], ALU.add).then_inc(x2_s, 1)
                dve.wait_ge(x2_s, n)
                settle(dve)
                norm_dve(dve, lnC[1], n, here)
                if not fresh:
                    dve.wait_ge(h2_stored[k], i * 16)
                relu_norm(lnC[1], h2b[k]).then_inc(lnC[1].s["out"], 1)

            def group_c(i, first):
                for k in range(2):
                    g = i * 2 + k
                    attend(g, k, i)
                    if k == 1:
                        finish(g - 1, 0, i, first)
                    elif not first:
                        finish(g - 1, 1, i - 1, isinstance(i, int) and i == 1)
                    dve.wait_ge(att_ps, g + 1)
                    dve.wait_ge(h0bo_s, g + 1)
                    tiles = two_banks(4 * k + 2)[0].rearrange("p (j f) -> p j f", j=G)
                    nc.vector.tensor_tensor(h0g[k], tiles, h0g[k], ALU.add).then_inc(x1_s, 1)
                    dve.wait_ge(x1_s, g + 1)
                    norm_dve(dve, lnC[0], g + 1, h0g[k])
                    nc.vector.tensor_tensor(hn2[k], lnC[0].cen, spread(lnC[0].rstd, HID), ALU.mult)\
                        .then_inc(lnC[0].s["out"], 1)
            repeat(dve, PAIRS, group_c, peel=2)
            finish(2 * PAIRS - 1, 1, PAIRS - 1, False)

            for k in range(2):
                dve.wait_ge(h2_stored[k], 16 * PAIRS)
            nc.vector.memset(rows[1][:, B - 1, :], 0.0).then_inc(sum_s, 1)

            def batch_d(i, first):
                for k in range(2):
                    n = i * 2 + k
                    dve.wait_ge(keep1_set, n + 1)
                    dve.wait_ge(rows_in[k], i * BW + BW)
                    for b in range(B):
                        dve.wait_ge(sum_s, n * B + b + 1)
                        before = rows[k][:, b - 1, :] if b else rows[1 - k][:, B - 1, :]
                        nc.vector.scalar_tensor_tensor(rows[k][:, b, :], before, keepd[k][:, b:b + 1], rows[k][:, b, :],
                                                       ALU.mult, ALU.add).then_inc(sum_s, 1)
            repeat(dve, BPAIRS, batch_d)
            dve.wait_ge(row1_in, 16)
            dve.wait_ge(carry1_ps, 1)
            nc.vector.tensor_tensor(patch_row1, patch_row1, ps[:, 1, 0:HID], ALU.add).then_inc(row1_s, 1)

            dve.wait_ge(row1_out, 16)
            nc.vector.tensor_scalar_add(eps1[:], eps1[:], 1.0).then_inc(eps_set, 1)
            dve.wait_ge(eps_set, 1)
            for k in range(2):
                nc.vector.tensor_copy(idx[k][:, 0:G], sum_i[:, k * G:(k + 1) * G]).then_inc(end_idx, 1)

            def output(g, k):
                here = nodes[:, bass.ds(g * G, G), :]
                nc.vector.tensor_tensor(here, here, gb2[:].unsqueeze(1).to_broadcast([P, G, HID]), ALU.add)\
                    .then_inc(xb2_s, 1)
                dve.wait_ge(xb2_s, g + 1)
                dve.wait_ge(mlp2_ps, g + 1)
                tiles = two_banks(4 * k)[0].rearrange("p (j f) -> p j f", j=G)
                nc.vector.tensor_tensor(here, tiles, here, ALU.add).then_inc(out_s, 1)

            def group_e(i, first):
                for k in range(2):
                    g = i * 2 + k
                    dve.wait_ge(nsum_in[k], i * GWAIT + GWAIT)
                    nc.vector.tensor_tensor(ng[k], ng[k], spread(has_edges[:, bass.ds(g * G, G)], HID), ALU.mult)\
                        .then_inc(masked_s, 1)
                    nc.vector.tensor_copy(idx[k][:, 0:G], sum_i[:, bass.ds((g + 2) * G, G)]).then_inc(end_idx, 1)
                    dve.wait_ge(h2_in[k], i * 16 + 16)
                    dve.wait_ge(masked_s, g + 1)
                    nc.vector.scalar_tensor_tensor(hg[k], hg[k], eps1[:], ng[k], ALU.mult, ALU.add).then_inc(h_s, 1)
                    if not (first and k == 0):
                        output(g - 1, 1 - k)
            repeat(dve, PAIRS, group_e)
            output(2 * PAIRS - 1, 1)


_INS = ["x", "src", "dst"] + ["L0_gnn_" + n for n in (
    "Wq", "bq", "Wk", "bk", "Wv", "bv", "Wo", "bo", "g1", "b1", "g2", "b2", "W1", "bf1", "W2", "bf2")] + [
    "L1_gnn_" + n for n in ("eps", "W1", "b1", "W2", "b2")]


def kernel(**inputs):
    import numpy as np
    import concourse.bacc as bacc
    from concourse import mybir as mb
    from concourse.bass_utils import run_bass_kernel_spmd

    nc = bacc.Bacc("TRN2", target_bir_lowering=False, num_devices=1)
    arrays, aps = {}, {}
    for name in _INS:
        array = np.ascontiguousarray(inputs[name])
        arrays["in_" + name] = array
        aps[name] = nc.dram_tensor("in_" + name, array.shape, mb.dt.from_np(array.dtype), kind="ExternalInput").ap()
    out = nc.dram_tensor("out", (N, HID), mb.dt.float32, kind="ExternalOutput").ap()
    build(nc, aps, out)
    result = run_bass_kernel_spmd(nc, [arrays], core_ids=[0])
    return result.results[0]["out"]
```

```python
import concourse.bass as bass
from concourse import mybir
from contextlib import ExitStack

F32 = mybir.dt.float32
I32 = mybir.dt.int32
ALU = mybir.AluOpType
ACT = mybir.ActivationFunctionType
AX = mybir.AxisListType

P = 128
N = 12500
E = 200000
HID = 128
NH = 8
HD = HID // NH
FFN = 512
FC = FFN // P
LN_EPS = 1e-5

NODE_COLS = -(-N // P)
NP = P * NODE_COLS
FULL = N // NODE_COLS
REST = N - FULL * NODE_COLS
G = 7
PAIRS = NODE_COLS // (2 * G)
GW = G * HID
HALF = GW // 2

B = 16
BATCHES = -(-E // (P * B))
STEPS = B * BATCHES
EP = P * STEPS
EFULL = E // STEPS
EREST = E - EFULL * STEPS
BPAIRS = BATCHES // 2
SAMPLE = 32
SAMPLES = STEPS // SAMPLE
BLOCKS = EP // SAMPLE

HS = HD + 1
SW = NH * HS
RW = SW + NH
BIG = 1e30
NOWHERE = float(1 << 21)
SCALE = 1.0 / HD ** 0.5

ARENA = 28000
WEIGHTS = 24
QKV_BANKS = 4
PREP_DIAG, PREP_ALL = 6, 18
FIRSTS_SET, STARTS_SET, PLACED = 3, 7, 16

assert NODE_COLS % (2 * G) == 0 and BATCHES % 2 == 0 and STEPS % SAMPLE == 0


class Carve:

    def __init__(self, tensor):
        self.tensor, self.at = tensor, 0

    def take(self, *shape):
        n = 1
        for s in shape:
            n *= s
        part = self.tensor[:, self.at:self.at + n]
        self.at += n
        assert self.at <= ARENA, self.at
        if len(shape) == 1:
            return part
        names = "abc"[:len(shape)]
        return part.rearrange(f"p ({' '.join(names)}) -> p {' '.join(names)}", **dict(zip(names[1:], shape[1:])))

    def two(self, *shape):
        return [self.take(*shape) for _ in range(2)]


def spread(ap, n):
    return ap.unsqueeze(2).to_broadcast([ap.shape[0], ap.shape[1], n])


def repeat(eng, count, body, peel=1, tail=0):
    for i in range(peel):
        body(i, i == 0)
    with eng.Fori(peel, count - tail) as i:
        body(i, False)
    for i in range(count - tail, count):
        body(i, False)


def build(nc, a, out):
    ctx = ExitStack()
    with ctx:
        def sb(name, shape, dt=F32):
            return ctx.enter_context(nc.sbuf_tensor(name, shape, dt))

        def sem(name):
            return ctx.enter_context(nc.semaphore(name))

        def sem2(name):
            return [sem(f"{name}{k}") for k in range(2)]

        def dram(name, shape, dt=F32):
            return nc.dram_tensor(name, shape, dt).ap()

        x_tail = dram("x_tail", [NODE_COLS, HID])
        kv_tab = dram("kv_tab", [NP, 2 * HID])
        h2_tab = dram("h2_tab", [NP, HID])
        q_edges = dram("q_edges", [EP, HID])
        states0 = dram("states0", [EP, RW])
        states1 = dram("states1", [EP, HID])
        dst_tab = dram("dst_tab", [EP // SAMPLE, SAMPLE], I32)
        last_tab = dram("last_tab", [NP + 1, 1], I32)

        def by_node(tab):
            return tab.rearrange("(p j) f -> p j f", j=NODE_COLS)

        def by_step(tab):
            return tab.rearrange("(p t) f -> p t f", t=STEPS)

        nodes = sb("nodes", [P, NODE_COLS, HID])
        src_all = sb("src_all", [P, STEPS + 2 * B], I32)
        keep = sb("keep", [P, STEPS + B])
        pen = sb("pen", [P, STEPS + B])
        ident = sb("ident", [P, P])
        ones = sb("ones", [P, P])
        earlier = sb("earlier", [P, P])
        same_dst = sb("same_dst", [P, P])
        same_pen = sb("same_pen", [P, P])
        has_edges = sb("has_edges", [P, NODE_COLS])
        start_i = sb("start_i", [P, NODE_COLS], I32)
        sum_i = sb("sum_i", [P, NODE_COLS + 2 * G], I32)
        patch_i = sb("patch_i", [P, 2], I32)
        chunk_start = sb("chunk_start", [P, 1], I32)
        first_i = sb("first_i", [P, 2], I32)
        q_first = sb("q_first", [P, HID])
        q_row_i = sb("q_row_i", [P, 1], I32)
        idx = [sb(f"idx{k}", [P, B], I32) for k in range(2)]
        node_idx = [sb(f"node_idx{k}", [P, G], I32) for k in range(2)]
        eps_t = sb("eps_t", [P, 1])
        rstd0 = sb("rstd0", [P, NODE_COLS])
        nmean0 = sb("nmean0", [P, NODE_COLS])
        eps1 = sb("eps1", [P, 1])
        wqkv = sb("wqkv", [P, 3 * HID])
        bqkv = sb("bqkv", [P, 3 * HID])
        wo = sb("wo", [P, HID])
        bo = sb("bo", [P, HID])
        cols = sb("cols", [P, 4])
        w1 = sb("w1", [P, FFN])
        bf1 = sb("bf1", [P, FC])
        w2 = sb("w2", [P, FC, HID])
        bf2 = sb("bf2", [P, HID])
        gw1 = sb("gw1", [P, HID])
        gb1 = sb("gb1", [P, 1])
        gw2 = sb("gw2", [P, HID])
        gb2 = sb("gb2", [P, HID])
        arena = sb("arena", [P, ARENA])
        ps = ctx.enter_context(nc.psum_tensor("ps", [P, 8, 512], F32))

        def two_banks(b):
            flat = ps[:, b:b + 2, :].rearrange("p a b -> p (a b)")
            return flat[:, 0:GW], [flat[:, j * HID:(j + 1) * HID] for j in range(G)]

        def qkv_bank(j):
            return ps[:, 2 + j % QKV_BANKS, 0:3 * HID]

        def halves(b):
            return ps[:, b:b + 2, 0:HALF]

        def column(ap, m):
            return ap[:, bass.ds(m, 1), :].rearrange("p a f -> p (a f)")

        class Norm:
            def __init__(self, tag, carve):
                self.own = sem(f"{tag}_own")
                self.var = sem(f"{tag}_var")
                self.std = sem(f"{tag}_std")
                self.ready = sem(f"{tag}_ready")
                self.stats, self.mean_var, self.dev = carve.take(G, 6), carve.take(G, 2), carve.take(G)

        def norm_stats(dve, ln, n, cols):
            for j in range(G):
                done = nc.vector.bn_stats(ln.stats[:, j, :], cols[j])
            done.then_inc(ln.own, 1)
            dve.wait_ge(ln.own, n * 2 - 1)
            settle(dve)
            for j in range(G):
                done = nc.vector.bn_aggr(ln.mean_var[:, j, :], ln.stats[:, j, :])
            done.then_inc(ln.var, 1)

        def norm_root(act, ln, n):
            act.wait_ge(ln.var, n)
            nc.scalar.activation(ln.dev, ln.mean_var[:, :, 1], ACT.Sqrt, bias=eps_t[:]).then_inc(ln.std, 1)

        def norm_scale(dve, ln, n, rstd, nmr):
            dve.wait_ge(ln.std, n)
            settle(dve)
            nc.vector.reciprocal(rstd, ln.dev).then_inc(ln.own, 1)
            dve.wait_ge(ln.own, n * 2)
            nc.vector.scalar_tensor_tensor(nmr, ln.mean_var[:, :, 0], -1.0, rstd, ALU.mult, ALU.mult)\
                .then_inc(ln.ready, 1)

        def norm_act(to, cols, func, rstd, nmr):
            for j in range(G):
                done = nc.scalar.activation(to[:, j, :], cols[j], func, bias=nmr(j), scale=rstd(j))
            return done

        cA = Carve(arena)
        qs_b = cA.two(G, HID)
        zeros = cA.take(B, HID)
        dst_all = cA.take(STEPS).bitcast(I32)
        dst_f = cA.take(STEPS)
        last_row = cA.take(P)
        diag = cA.take(P)
        step_back = cA.take(P)
        back_one = cA.take(P)
        samples = cA.take(SAMPLES + 1)
        deltas = cA.take(SAMPLES + 1)
        row_node_i = cA.take(P).bitcast(I32)
        row_node = cA.take(P)
        node_i = cA.take(NODE_COLS).bitcast(I32)
        node_f = cA.take(NODE_COLS)
        col_i = cA.take(NODE_COLS).bitcast(I32)
        first_less_j = cA.take(NODE_COLS)
        block_f = cA.take(NODE_COLS)
        last_f = cA.take(NODE_COLS)
        last_i = cA.take(NODE_COLS).bitcast(I32)
        before_i = cA.take(NODE_COLS).bitcast(I32)
        before_f = cA.take(NODE_COLS)
        start_f = cA.take(NODE_COLS)
        minus1 = cA.take(1).bitcast(I32)
        chunk_i = cA.take(1).bitcast(I32)
        patch_raw = cA.take(1).bitcast(I32)
        patch_f = cA.take(4)
        starts_ge = cA.two(G, P)
        cmp2 = cA.take(G, SAMPLES)
        cnt2 = cA.take(G)
        blk2 = cA.take(G)
        look = cA.two(G, SAMPLE)
        cmp3 = cA.take(G, SAMPLE)
        cnt3 = cA.take(G)
        start_raw = cA.take(1).bitcast(I32)
        lnA = [Norm(f"lnA{t}", cA) for t in range(2)]
        nmr0, rstd1, nmr1 = cA.take(G), cA.take(G), cA.take(G)
        h0_b = cA.take(G, HID)
        hn_b = cA.take(G, HID)
        hnT = cA.take(GW)
        kv_b = cA.two(G, 2 * HID)

        memset_done = sem("memset_done")
        consts = sem("consts")
        masks = sem("masks")
        edges_in = sem("edges_in")
        x_first, x_in = sem("x_first"), sem("x_in")
        x_tail_in = sem("x_tail_in")
        weights_in = sem("weights_in")
        q_zeroed = sem2("q_zeroed")
        prep = sem("prep")
        sample_delta = sem("sample_delta")
        last_rows = sem("last_rows")
        dst_tab_in = sem("dst_tab_in")
        starts = sem("starts")
        sample_row = sem("sample_row")
        search_s = sem("search_s")
        block_idx = sem("block_idx")
        look_in = sem2("look_in")
        count_s = sem("count_s")
        last_s = sem("last_s")
        turns = sem("turns")
        h0_set, hn_set = sem("h0_set"), sem("hn_set")
        hn_T = sem("hn_T")
        hnT_set = sem("hnT_set")
        qkv_ps = sem("qkv_ps")
        kv_set = sem("kv_set")
        kv_stored = sem2("kv_stored")
        last_set = sem("last_set")
        last_stored = sem("last_stored")
        before_in = sem("before_in")
        place = sem("place")
        patch_in = sem("patch_in")
        qs_copied = sem("qs_copied")
        qs_out = sem2("qs_out")
        q_first_in = sem("q_first_in")

        CW = B + 1
        cB = Carve(arena)
        diag8 = cB.take(NH, P)
        masked = cB.take(NH, P)
        weight = cB.take(NH, P)
        weightT = cB.take(NH, P)
        kvb = cB.two(B, 2 * HID)
        qb = cB.two(B, HID)
        stb = cB.two(B, RW)
        score = cB.take(NH, CW)
        run_max = cB.take(NH * CW)
        top = cB.take(NH, CW)
        dif = cB.take(NH, CW)
        penb = cB.two(NH * CW + 1)
        keepb = cB.two(B)
        rescale = cB.take(NH)
        carried = cB.take(SW)
        carry_max = cB.take(NH)
        carry = cB.take(NH, HS)
        patch_row = cB.take(RW)
        patch_top = cB.take(NH)
        patch_low = cB.take(2, NH)
        patch_w = cB.take(2, NH)
        patch_add = cB.take(NH, HS)

        edge_ready = sem("edge_ready")
        idx_set = sem("idx_set")
        gates_set = sem("gates_set")
        q_in, kv_in, states_out = sem2("q_in"), sem2("kv_in"), sem2("states_out")
        q_filled = sem("q_filled")
        prod_s, dif_s = sem("prod_s"), sem("dif_s")
        scan_s = sem("scan_s")
        probs_s, rescale_s, top_out = sem("probs_s"), sem("rescale_s"), sem("top_out")
        weighed_s, carried_s = sem("weighed_s"), sem("carried_s")
        state_s = sem("state_s")
        chunk_s = sem("chunk_s")
        tops_ps, weight_s, weightT_ps, weightT_s, carry_ps = (sem(n) for n in (
            "tops_ps", "weight_s", "weightT_ps", "weightT_s", "carry_ps"))
        patch_row_in, patch_exp, patch_done, patch_out = (sem(n) for n in (
            "patch_row_in", "patch_exp", "patch_done", "patch_out"))

        cC = Carve(arena)
        sg = cC.two(G, RW)
        beside = Carve(arena)
        beside.at = cB.at
        xg = beside.two(G, HID)
        kvg = beside.two(G, 2 * HID)
        qg = cC.two(G, HID)
        h0g = cC.two(G, HID)
        self_e = cC.two(G, NH)
        top_c = cC.two(G, NH)
        low_c = cC.two(2, G * NH)
        w_c = cC.two(2, G * NH)
        rden = cC.two(G, NH)
        xT = cC.two(GW)
        gT = cC.two(FC, GW)
        xb = cC.two(G, HID)
        hn2 = cC.take(G, HID)
        h2b = cC.two(G, HID)
        lnC = [Norm(f"lnC{t}", cC) for t in range(2)]
        rstd2, nmr2 = cC.two(G), cC.two(G)
        rstd3, nmr3 = cC.two(G), cC.two(G)
        assert cC.at <= cB.at

        sum_idx = sem("sum_idx")
        sg_in, ng_in = sem2("sg_in"), sem2("ng_in")
        attend_s = sem("attend_s")
        low1_s, w_cs, num_s, agg_s = (sem(n) for n in ("low1_s", "w_cs", "num_s", "agg_s"))
        (h0_s, h0bo_s, aggT_ps, aggT_s, att_ps, x1_s, hn2_s, hnT2_ps, hnT2_s, ff1_ps, gelu_s, ff2_ps, xsum_s, xb_s, x2_s,
         h2_s) = (sem(n) for n in ("h0_s", "h0bo_s", "aggT_ps", "aggT_s", "att_ps", "x1_s", "hn2_s", "hnT2_ps", "hnT2_s",
                                   "ff1_ps", "gelu_s", "ff2_ps", "xsum_s", "xb_s", "x2_s", "h2_s"))
        centred_s = sem("centred_s")
        h2_stored = sem2("h2_stored")

        cD = Carve(arena)
        rows = cD.two(B, HID)
        keepd = cD.two(B)
        sameT = cD.take(P)
        patch_row1 = cD.take(HID)
        idx1_set, keep1_set = sem("idx1_set"), sem("keep1_set")
        rows_in, sums_out = sem2("rows_in"), sem2("sums_out")
        sum_s = sem("sum_s")
        sameT_ps, sameT_s, carry1_ps, row1_in, row1_s, row1_out = (sem(n) for n in (
            "sameT_ps", "sameT_s", "carry1_ps", "row1_in", "row1_s", "row1_out"))

        cE = Carve(arena)
        cE.at = cD.at
        ng = cE.two(G, HID)
        hg = cE.two(G, HID)
        hT = cE.two(GW)
        rT = cE.two(GW)
        end_idx, eps_set = sem("end_idx"), sem("eps_set")
        nsum_in, h2_in = sem2("nsum_in"), sem2("h2_in")
        masked_s, h_s, hT_ps, hT_s, mlp1_ps, relu_s, mlp2_ps, xb2_s, out_s = (sem(n) for n in (
            "masked_s", "h_s", "hT_ps", "hT_s", "mlp1_ps", "relu_s", "mlp2_ps", "xb2_s", "out_s"))
        out_stored = sem("out_stored")

        x_full = a["x"][0:FULL * NODE_COLS, :].rearrange("(p j) f -> p j f", j=NODE_COLS)
        x_rest = a["x"][FULL * NODE_COLS:N, :].rearrange("(p j) f -> p j f", p=1)
        LAST = (BATCHES - 1) % 2
        BW = 16 * B
        GWAIT = 16 * G

        def settle(eng):
            eng.sem_inc(turns, 1)

        def last_batch(n):
            return isinstance(n, int) and n == BATCHES - 1

        def last_group(g):
            return isinstance(g, int) and g == 2 * PAIRS - 1

        block = ctx.enter_context(nc.Block())

        @block.sync
        def _(sp):
            sp.wait_ge(memset_done, 2)
            for to, frm in ((dst_all, a["dst"]), (src_all, a["src"])):
                sp.dma_start(to[0:EFULL, 0:STEPS], frm[0:EFULL * STEPS].rearrange("(p t) -> p t", t=STEPS))\
                    .then_inc(edges_in, 16)
                sp.dma_start(to[EFULL:EFULL + 1, 0:EREST], frm[EFULL * STEPS:E].rearrange("(p t) -> p t", p=1))\
                    .then_inc(edges_in, 16)
            sp.wait_ge(memset_done, 3)
            sp.dma_start(nodes[0:FULL, 0:2 * G, :], x_full[:, 0:2 * G, :]).then_inc(x_first, 16)
            sp.dma_start(nodes[FULL:FULL + 1, 0:2 * G, :], x_rest[:, 0:2 * G, :]).then_inc(x_first, 16)
            sp.dma_start(nodes[0:FULL, 2 * G:NODE_COLS, :], x_full[:, 2 * G:NODE_COLS, :]).then_inc(x_in, 16)
            sp.dma_start(nodes[FULL:FULL + 1, 2 * G:REST, :], x_rest[:, 2 * G:REST, :]).then_inc(x_in, 16)
            sp.wait_ge(memset_done, 4)
            sp.dma_start(x_tail[0:REST, :], a["x"][FULL * NODE_COLS:N, :]).then_inc(x_tail_in, 16)
            sp.dma_start(x_tail[REST:NODE_COLS, :], zeros[0:NODE_COLS - REST, 0, :]).then_inc(x_tail_in, 16)

            def zero_fill(i, first):
                for k in range(2):
                    if not first:
                        sp.wait_ge(q_zeroed[k], i * 16)
                        settle(sp)
                    sp.dma_start(by_step(q_edges)[:, bass.ds((i * 2 + k) * B, B), :], zeros)\
                        .then_inc(q_zeroed[k], 16)
            repeat(sp, BPAIRS, zero_fill)

            q_rows = by_step(q_edges)
            for k in range(2):
                sp.wait_ge(qs_out[k], GWAIT * PAIRS)
            sp.wait_ge(edge_ready, 1)
            sp.dma_start(qb[0], q_rows[:, 0:B, :]).then_inc(q_in[0], 16)

            def store_b(n, k):
                sp.wait_ge(state_s, n * B + B)
                settle(sp)
                sp.wait_ge(top_out, n + 1)
                settle(sp)
                sp.dma_start(by_step(states0)[:, bass.ds(n * B, B), :], stb[k]).then_inc(states_out[k], 16)

            def batch_b(i, first):
                for k in range(2):
                    n = i * 2 + k
                    if not last_batch(n):
                        sp.wait_ge(q_filled, n * B + 1)
                        settle(sp)
                        sp.dma_start(qb[1 - k], q_rows[:, bass.ds(n * B + B, B), :]).then_inc(q_in[1 - k], 16)
                    if not (first and k == 0):
                        store_b(n - 1, 1 - k)
            repeat(sp, BPAIRS, batch_b, tail=1)

            sp.wait_ge(x_tail_in, 32)

            def group_c(i, first):
                for k in range(2):
                    g = i * 2 + k
                    if not first:
                        sp.wait_ge(xb_s, g - 1)
                        settle(sp)
                    sp.dma_start(xg[k][0:FULL, :, :], x_full[:, bass.ds(g * G, G), :]).then_inc(ng_in[k], 16)
                    sp.dma_start(xg[k][FULL:FULL + 1, :, :],
                                 x_tail[bass.ds(g * G, G), :].rearrange("(p j) f -> p j f", p=1)).then_inc(ng_in[k], 16)
                    sp.dma_start(kvg[k], by_node(kv_tab)[:, bass.ds(g * G, G), :]).then_inc(ng_in[k], 16)
            group_c(0, True)
            store_b(BATCHES - 1, LAST)
            with sp.Fori(1, PAIRS) as i:
                group_c(i, False)

            def batch_d(i, first):
                for k in range(2):
                    n = i * 2 + k
                    sp.wait_ge(sum_s, n * B + B + 1)
                    settle(sp)
                    sp.dma_start(by_step(states1)[:, bass.ds(n * B, B), :], rows[k]).then_inc(sums_out[k], 16)
            repeat(sp, BPAIRS, batch_d)

            out_full = out[0:FULL * NODE_COLS, :].rearrange("(p j) f -> p j f", j=NODE_COLS)

            def store_out(i):
                sp.wait_ge(out_s, i * 2 + 2)
                settle(sp)
                cols_i = bass.ds(i * 2 * G, 2 * G)
                sp.dma_start(out_full[:, cols_i, :], nodes[0:FULL, cols_i, :]).then_inc(out_stored, 16)

            def group_e(i, first):
                for k in range(2):
                    g = i * 2 + k
                    if not first:
                        sp.wait_ge(hT_ps, g - 1)
                        settle(sp)
                    sp.dma_start(hg[k], by_node(h2_tab)[:, bass.ds(g * G, G), :]).then_inc(h2_in[k], 16)
                if not first:
                    store_out(i - 1)
            repeat(sp, PAIRS, group_e)
            sp.wait_ge(out_s, 2 * PAIRS)
            sp.dma_start(out[FULL * NODE_COLS:N, :].rearrange("(p j) f -> p j f", p=1),
                         nodes[FULL:FULL + 1, 0:REST, :]).then_inc(out_stored, 16)
            store_out(PAIRS - 1)
            sp.wait_ge(out_stored, 16 * (PAIRS + 1))

        @block.gpsimd
        def _(pool):
            def gather(to, tab, at, done):
                pool.indirect_dma_start(to, None, tab, bass.IndirectOffsetOnAxis(ap=at, axis=0)).then_inc(done, 16)

            def scatter(tab, at, frm, done):
                pool.indirect_dma_start(tab, bass.IndirectOffsetOnAxis(ap=at, axis=0), frm, None,
                                        bounds_check=EP - 1, oob_is_err=False).then_inc(done, 16)

            nc.gpsimd.memset(ident[:], 0.0).then_inc(consts, 1)
            nc.gpsimd.memset(back_one, 0.0).then_inc(consts, 1)
            nc.gpsimd.memset(earlier[:], 1.0).then_inc(consts, 1)
            nc.gpsimd.memset(ones[:], 1.0).then_inc(consts, 1)
            nc.gpsimd.memset(eps_t[:], LN_EPS).then_inc(consts, 1)
            nc.gpsimd.memset(minus1, -1).then_inc(consts, 1)
            nc.gpsimd.iota(node_i, [[1, NODE_COLS]], base=0, channel_multiplier=NODE_COLS).then_inc(consts, 1)
            nc.gpsimd.iota(col_i, [[1, NODE_COLS]], base=0, channel_multiplier=0).then_inc(consts, 1)
            nc.gpsimd.iota(row_node_i, [[NODE_COLS, P]], base=0, channel_multiplier=0).then_inc(consts, 1)
            nc.gpsimd.iota(chunk_i, [[1, 1]], base=0, channel_multiplier=1).then_inc(consts, 1)
            nc.gpsimd.iota(chunk_start[:], [[1, 1]], base=0, channel_multiplier=STEPS).then_inc(consts, 1)
            pool.wait_ge(consts, 11)
            nc.gpsimd.affine_select(out=ident[:], in_=ident[:], compare_op=ALU.not_equal, fill=1.0, base=0,
                                    pattern=[[-1, P]], channel_multiplier=1).then_inc(masks, 1)
            nc.gpsimd.affine_select(out=back_one, in_=back_one, compare_op=ALU.not_equal, fill=1.0, base=1,
                                    pattern=[[-1, P]], channel_multiplier=1).then_inc(masks, 1)
            nc.gpsimd.affine_select(out=earlier[:], in_=earlier[:], compare_op=ALU.is_gt, fill=0.0, base=0,
                                    pattern=[[-1, P]], channel_multiplier=1).then_inc(masks, 1)

            def weight_in(to, frm):
                pool.dma_start(to, frm).then_inc(weights_in, 16)

            def as_column(name):
                return a[name].rearrange("(p o) -> p o", o=1)

            for t, name in enumerate(("g1", "b1", "g2", "b2")):
                weight_in(cols[:, t:t + 1], as_column("L0_gnn_" + name))
            for t, name in enumerate("qkv"):
                weight_in(wqkv[:, t * HID:(t + 1) * HID], a["L0_gnn_W" + name])
                weight_in(bqkv[:, t * HID:(t + 1) * HID], a["L0_gnn_b" + name].partition_broadcast(P))
            weight_in(wo[:], a["L0_gnn_Wo"])
            weight_in(w1[:], a["L0_gnn_W1"])
            weight_in(w2[:], a["L0_gnn_W2"].rearrange("(c p) f -> p c f", p=P))
            for c in range(FC):
                weight_in(bf1[:, c:c + 1], a["L0_gnn_bf1"][c * P:(c + 1) * P].rearrange("(p o) -> p o", o=1))
            for to, name in ((bo, "L0_gnn_bo"), (bf2, "L0_gnn_bf2"), (gb2, "L1_gnn_b2"), (eps1, "L1_gnn_eps")):
                weight_in(to[:], a[name].partition_broadcast(P))
            weight_in(gw1[:], a["L1_gnn_W1"])
            weight_in(gw2[:], a["L1_gnn_W2"])
            weight_in(gb1[:], as_column("L1_gnn_b1"))

            pool.wait_ge(dst_tab_in, 16)

            def search(i, first):
                for k in range(2):
                    pool.wait_ge(block_idx, i * 2 + k + 1)
                    settle(pool)
                    for j in range(G):
                        gather(look[k][:, j, :].bitcast(I32), dst_tab, idx[k][:, j:j + 1], look_in[k])
            repeat(pool, PAIRS, search)

            pool.wait_ge(place, FIRSTS_SET)
            pool.wait_ge(last_stored, 32)
            gather(patch_raw, last_tab, first_i[:, 1:2], patch_in)
            gather(start_raw, last_tab, first_i[:, 0:1], patch_in)

            for k in range(2):
                pool.wait_ge(kv_stored[k], 16 * PAIRS)
            pool.wait_ge(edge_ready, 1)

            def batch_b(i, first):
                for k in range(2):
                    n = i * 2 + k
                    pool.wait_ge(idx_set, n + 1)
                    if not first:
                        pool.wait_ge(weighed_s, n - 1)
                    settle(pool)
                    for b in range(B):
                        gather(kvb[k][:, b, :], kv_tab, idx[k][:, b:b + 1], kv_in[k])
            batch_b(0, True)

            for k in range(2):
                pool.wait_ge(q_zeroed[k], 16 * BPAIRS)

            def scatter_q(i, first):
                for k in range(2):
                    pool.wait_ge(qs_copied, (i * 2 + k) * 2 + 2)
                    settle(pool)
                    for j in range(G):
                        scatter(q_edges, node_idx[k][:, j:j + 1], qs_b[k][:, j, :], qs_out[k])
            repeat(pool, PAIRS, scatter_q)

            for k in range(2):
                pool.wait_ge(qs_out[k], GWAIT * PAIRS)
            pool.wait_ge(place, PLACED)
            gather(q_first[:], q_edges, q_row_i[:], q_first_in)

            with pool.Fori(1, BPAIRS) as i:
                batch_b(i, False)

            for k in range(2):
                pool.wait_ge(states_out[k], 16 * BPAIRS)
            gather(patch_row, states0, patch_i[:, 0:1], patch_row_in)
            pool.wait_ge(patch_done, 1)
            scatter(states0, patch_i[:, 1:2], patch_row, patch_out)
            pool.wait_ge(patch_out, 16)

            def add_bo(g, k):
                pool.wait_ge(h0_s, g + 1)
                nc.gpsimd.tensor_tensor(h0g[k], h0g[k], bo[:].unsqueeze(1).to_broadcast([P, G, HID]), ALU.add)\
                    .then_inc(h0bo_s, 1)

            def add_x(g, k):
                pool.wait_ge(x1_s, g + 1)
                nc.gpsimd.tensor_tensor(xb[k], h0g[k], bf2[:].unsqueeze(1).to_broadcast([P, G, HID]), ALU.add)\
                    .then_inc(xsum_s, 1)
                pool.wait_ge(xsum_s, g + 1)
                nc.gpsimd.tensor_tensor(xb[k], xb[k], xg[k], ALU.add).then_inc(xb_s, 1)

            def group_c(i, first):
                for k in range(2):
                    g = i * 2 + k
                    pool.wait_ge(sum_idx, g + 1)
                    if not first:
                        pool.wait_ge(num_s, g - 1)
                    settle(pool)
                    for j in range(G):
                        gather(sg[k][:, j, :], states0, node_idx[k][:, j:j + 1], sg_in[k])
                    if not first:
                        add_x(g - 2, k)
                    if not (first and k == 0):
                        add_bo(g - 1, 1 - k)
            repeat(pool, PAIRS, group_c)
            add_x(2 * PAIRS - 2, 0)
            add_bo(2 * PAIRS - 1, 1)
            add_x(2 * PAIRS - 1, 1)

            for k in range(2):
                pool.wait_ge(h2_stored[k], 16 * PAIRS)

            def batch_d(i, first):
                for k in range(2):
                    n = i * 2 + k
                    pool.wait_ge(idx1_set, n + 1)
                    if not first:
                        pool.wait_ge(sums_out[k], i * 16)
                    settle(pool)
                    for b in range(B):
                        if b == B - 1 and not (first and k == 0):
                            pool.wait_ge(sum_s, (n - 1) * B + 2)
                            settle(pool)
                        gather(rows[k][:, b, :], h2_tab, idx[k][:, b:b + 1], rows_in[k])
            repeat(pool, BPAIRS, batch_d)
            for k in range(2):
                pool.wait_ge(sums_out[k], 16 * BPAIRS)
            gather(patch_row1, states1, patch_i[:, 0:1], row1_in)
            pool.wait_ge(row1_s, 1)
            scatter(states1, patch_i[:, 1:2], patch_row1, row1_out)
            pool.wait_ge(row1_out, 16)

            def group_e(i, first):
                for k in range(2):
                    g = i * 2 + k
                    pool.wait_ge(end_idx, g + 1)
                    if not first:
                        pool.wait_ge(h_s, g - 1)
                    settle(pool)
                    for j in range(G):
                        gather(ng[k][:, j, :], states1, node_idx[k][:, j:j + 1], nsum_in[k])
            repeat(pool, PAIRS, group_e)

        @block.scalar
        def _(act):
            act.wait_ge(edges_in, 64)
            act.dma_start(dst_tab.rearrange("(p b) s -> p (b s)", p=P), dst_all).then_inc(dst_tab_in, 16)

            def store_kv(g, k):
                act.wait_ge(kv_set, g * G + G)
                act.dma_start(by_node(kv_tab)[:, bass.ds(g * G, G), :], kv_b[k]).then_inc(kv_stored[k], 16)

            def group_a(i, first):
                for k in range(2):
                    g = i * 2 + k
                    norm_root(act, lnA[0], g + 1)
                    act.wait_ge(lnA[0].ready, g + 1)
                    settle(act)
                    norm_act(h0_b, [column(nodes, g * G + j) for j in range(G)], ACT.Relu,
                             lambda j: rstd0[:, bass.ds(g * G + j, 1)], lambda j: nmr0[:, j:j + 1])\
                        .then_inc(h0_set, 1)
                    if not (first and k == 0):
                        store_kv(g - 1, 1 - k)
                    norm_root(act, lnA[1], g + 1)
                    act.wait_ge(lnA[1].ready, g + 1)
                    norm_act(hn_b, [h0_b[:, j, :] for j in range(G)], ACT.Identity,
                             lambda j: rstd1[:, j:j + 1], lambda j: nmr1[:, j:j + 1]).then_inc(hn_set, 1)
                    if first and k == 0:
                        act.wait_ge(weights_in, 16 * WEIGHTS)
                    act.wait_ge(hn_T, g + 1)
                    nc.scalar.activation(hnT, two_banks(0)[0], ACT.Identity, bias=cols[:, 1:2], scale=cols[:, 0:1])\
                        .then_inc(hnT_set, 1)
            repeat(act, PAIRS, group_a)
            store_kv(2 * PAIRS - 1, 1)

            act.wait_ge(last_set, 1)
            act.dma_start(last_tab[0:1, :], minus1[0:1, :]).then_inc(last_stored, 16)
            act.dma_start(last_tab[1:NP + 1, :].rearrange("(p j) o -> p (j o)", j=NODE_COLS), last_i)\
                .then_inc(last_stored, 16)
            act.wait_ge(last_stored, 32)
            act.dma_start(before_i, last_tab[0:NP, :].rearrange("(p j) o -> p (j o)", j=NODE_COLS))\
                .then_inc(before_in, 16)

            for k in range(2):
                nc.scalar.copy(idx[k][:], src_all[:, k * B:(k + 1) * B]).then_inc(idx_set, 1)

            act.wait_ge(place, STARTS_SET)

            def copy_q(i, first):
                for k in range(2):
                    g = (i * 2 + k) * G
                    if not first:
                        act.wait_ge(qs_out[k], i * GWAIT)
                        settle(act)
                    nc.scalar.copy(qs_b[k], nodes[:, bass.ds(g, G), :]).then_inc(qs_copied, 1)
                    nc.scalar.copy(node_idx[k][:], start_i[:, bass.ds(g, G)]).then_inc(qs_copied, 1)
            repeat(act, PAIRS, copy_q)

            act.wait_ge(edge_ready, 1)

            def gates(n, k):
                nc.scalar.copy(keepb[k], keep[:, bass.ds(n * B, B)]).then_inc(gates_set, 1)
                nc.scalar.copy(penb[k][:, 0:NH * CW].rearrange("p (h t) -> p h t", h=NH)[:, :, 1:CW],
                               pen[:, bass.ds(n * B, B)].unsqueeze(1).to_broadcast([P, NH, B])).then_inc(gates_set, 1)
            gates(0, 0)

            def batch_b(i, first):
                for k in range(2):
                    n = i * 2 + k
                    if not (first and k == 0):
                        act.wait_ge(state_s, n * B)
                        settle(act)
                    gates(n + 1, 1 - k)
                    act.wait_ge(prod_s, n + 1)
                    settle(act)
                    nc.scalar.copy(idx[k][:], src_all[:, bass.ds((n + 2) * B, B)]).then_inc(idx_set, 1)
                    act.wait_ge(dif_s, n + 1)
                    if not first:
                        act.wait_ge(states_out[k], i * 16)
                    heads = stb[k][:, :, 0:SW].rearrange("p b (h s) -> p h b s", s=HS)
                    nc.scalar.activation(rescale, dif[:, :, 0], ACT.Exp, scale=SCALE).then_inc(rescale_s, 1)
                    nc.scalar.activation(heads[:, :, :, HD], dif[:, :, 1:CW], ACT.Exp, scale=SCALE)\
                        .then_inc(probs_s, 1)
                    nc.scalar.copy(stb[k][:, :, SW:RW].rearrange("p b h -> p h b"), top[:, :, 1:CW])\
                        .then_inc(top_out, 1)
            repeat(act, BPAIRS, batch_b)

            act.wait_ge(chunk_s, 4)
            nc.scalar.activation(weight, masked, ACT.Exp, scale=SCALE).then_inc(weight_s, 1)
            act.wait_ge(weightT_ps, 1)
            nc.scalar.copy(weightT.rearrange("p h c -> p (h c)"), ps[:, 2:4, :].rearrange("p a b -> p (a b)"))\
                .then_inc(weightT_s, 1)
            act.wait_ge(chunk_s, 9)
            nc.scalar.activation(patch_w, patch_low, ACT.Exp, scale=SCALE).then_inc(patch_exp, 1)

            act.wait_ge(patch_out, 16)

            for k in range(2):
                nc.scalar.copy(idx[k][:], src_all[:, k * B:(k + 1) * B]).then_inc(idx1_set, 1)

            def norm2(g, k):
                norm_root(act, lnC[0], g + 1)
                act.wait_ge(lnC[0].ready, g + 1)
                norm_act(hn2, [h0g[k][:, j, :] for j in range(G)], ACT.Identity,
                         lambda j: rstd2[k][:, j:j + 1], lambda j: nmr2[k][:, j:j + 1]).then_inc(hn2_s, 1)
                act.wait_ge(hnT2_ps, g + 1)
                nc.scalar.activation(xT[k], two_banks(4 * k)[0], ACT.Identity, bias=cols[:, 3:4], scale=cols[:, 2:3])\
                    .then_inc(hnT2_s, 1)

            def norm3_and_gelus(g, k, stored, between):
                if stored is not None:
                    act.wait_ge(h2_stored[k], stored)
                j = 0
                for c in range(FC):
                    if between:
                        act.wait_ge(ff1_ps, (g + 1) * FC + c + 1)
                        gelu(g + 1, 1 - k, c)
                    if c == 1:
                        act.wait_ge(lnC[1].ready, g + 1)
                        settle(act)
                    while j < c * G // (FC - 1):
                        done = nc.scalar.activation(h2b[k][:, j, :], column(nodes, g * G + j), ACT.Relu,
                                                    bias=nmr3[k][:, j:j + 1], scale=rstd3[k][:, j:j + 1])
                        j += 1
                done.then_inc(h2_s, 1)
                act.wait_ge(h2_s, g + 1)
                act.dma_start(by_node(h2_tab)[:, bass.ds(g * G, G), :], h2b[k]).then_inc(h2_stored[k], 16)

            def loop_exp(g, k):
                act.wait_ge(low1_s, g + 1)
                nc.scalar.activation(w_c[k], low_c[k], ACT.Exp, scale=SCALE).then_inc(w_cs, 1)

            def gelu(g, k, c):
                nc.scalar.activation(gT[k][:, c, :].rearrange("p (h f) -> p h f", h=2),
                                     halves(4 * k + 2 - 2 * (c % 2)), ACT.Gelu, bias=bf1[:, c:c + 1]).then_inc(gelu_s, 1)

            def group_c(i, first):
                for k in range(2):
                    g = i * 2 + k
                    if not (first and k == 0):
                        norm2(g - 1, 1 - k)
                    act.wait_ge(aggT_ps, g + 1)
                    nc.scalar.copy(xT[k], two_banks(4 * k)[0]).then_inc(aggT_s, 1)
                    if not first:
                        norm_root(act, lnC[1], g - 1)
                    if not last_group(g):
                        loop_exp(g + 1, 1 - k)
                    if not first:
                        norm3_and_gelus(g - 2, k, None if isinstance(i, int) and i == 1 else i * 16 - 16, True)
                    elif k == 1:
                        for c in range(FC):
                            act.wait_ge(ff1_ps, c + 1)
                            gelu(0, 0, c)
            loop_exp(0, 0)
            repeat(act, PAIRS, group_c, peel=2, tail=1)
            norm2(2 * PAIRS - 1, 1)
            norm_root(act, lnC[1], 2 * PAIRS - 1)
            norm3_and_gelus(2 * PAIRS - 2, 0, PAIRS * 16 - 16, True)
            norm_root(act, lnC[1], 2 * PAIRS)
            norm3_and_gelus(2 * PAIRS - 1, 1, PAIRS * 16 - 16, False)

            act.wait_ge(sum_s, 1)

            def batch_d(i, first):
                for k in range(2):
                    n = i * 2 + k
                    if not first:
                        act.wait_ge(sum_s, (n - 1) * B + 1)
                        settle(act)
                    nc.scalar.copy(keepd[k], keep[:, bass.ds(n * B, B)]).then_inc(keep1_set, 1)
                    if not first:
                        nc.scalar.copy(idx[k][:], src_all[:, bass.ds(n * B, B)]).then_inc(idx1_set, 1)
            repeat(act, BPAIRS, batch_d)
            act.wait_ge(sameT_ps, 1)
            nc.scalar.copy(sameT, ps[:, 0, 0:P]).then_inc(sameT_s, 1)

            def group_e(i, first):
                for k in range(2):
                    g = i * 2 + k
                    act.wait_ge(hT_ps, g + 1)
                    nc.scalar.copy(hT[k], two_banks(4 * k)[0]).then_inc(hT_s, 1)
                    act.wait_ge(mlp1_ps, g + 1)
                    nc.scalar.activation(rT[k].rearrange("p (h f) -> p h f", h=2), halves(4 * k + 2), ACT.Relu,
                                         bias=gb1[:]).then_inc(relu_s, 1)
            repeat(act, PAIRS, group_e)

        @block.tensor
        def _(pe):
            pe.wait_ge(prep, PREP_DIAG)
            nc.tensor.matmul(ps[:, 6, 0:P], ones[:], diag, start=True, stop=True).then_inc(last_rows, 1)
            nc.tensor.matmul(ps[:, 7, 0:SAMPLES + 1], step_back, samples, start=True, stop=True)\
                .then_inc(sample_delta, 1)
            pe.wait_ge(prep, PREP_ALL)

            def group_a(i, first):
                for k in range(2):
                    g = i * 2 + k
                    pe.wait_ge(starts, g + 1)
                    for j in range(G):
                        done = nc.tensor.matmul(ps[:, 6 + k, j * (SAMPLES + 1):(j + 1) * (SAMPLES + 1)],
                                                starts_ge[k][:, j, :], deltas, start=True, stop=True)
                    done.then_inc(sample_row, 1)
                    pe.wait_ge(hn_set, g + 1)
                    for j in range(G):
                        done = nc.tensor.transpose(two_banks(0)[1][j], hn_b[:, j, :], ident[:])
                    done.then_inc(hn_T, 1)
                    if first and k == 0:
                        pe.wait_ge(weights_in, 16 * WEIGHTS)
                    pe.wait_ge(hnT_set, g + 1)
                    for j in range(G):
                        if j >= QKV_BANKS:
                            pe.wait_ge(kv_set, g * G + j - QKV_BANKS + 1)
                        elif not (first and k == 0):
                            pe.wait_ge(kv_set, (g - 1) * G + (G - 1 - j) // QKV_BANKS * QKV_BANKS + j + 1)
                        nc.tensor.matmul(qkv_bank(j), hnT[:, j * HID:(j + 1) * HID], wqkv[:], start=True, stop=True)\
                            .then_inc(qkv_ps, 1)
            repeat(pe, PAIRS, group_a)

            pe.wait_ge(chunk_s, 1)
            for t in range(2):
                done = nc.tensor.matmul(ps[:, t, :], ones[:], diag8[:, 4 * t:4 * t + 4, :].rearrange("p h c -> p (h c)"),
                                        start=True, stop=True)
            done.then_inc(tops_ps, 1)
            pe.wait_ge(chunk_s, 5)
            for h in range(NH):
                done = nc.tensor.transpose(ps[:, 2 + h // 4, (h % 4) * P:(h % 4 + 1) * P], weight[:, h, :], ident[:])
            done.then_inc(weightT_ps, 1)
            pe.wait_ge(weightT_s, 1)
            pe.wait_ge(state_s, STEPS)
            for h in range(NH):
                done = nc.tensor.matmul(ps[:, 4, h * HS:(h + 1) * HS], weightT[:, h, :],
                                        stb[LAST][:, B - 1, h * HS:(h + 1) * HS], start=True, stop=True)
            done.then_inc(carry_ps, 1)

            def norm_T(g, k):
                pe.wait_ge(hn2_s, g + 1)
                for j in range(G):
                    done = nc.tensor.transpose(two_banks(4 * k)[1][j], hn2[:, j, :], ident[:])
                done.then_inc(hnT2_ps, 1)

            def ffn(g, k):
                pe.wait_ge(hnT2_s, g + 1)
                for c in range(FC):
                    if c >= 2:
                        pe.wait_ge(gelu_s, g * FC + c - 1)
                    for h in range(2):
                        done = nc.tensor.matmul(halves(4 * k + 2 - 2 * (c % 2))[:, h, :], w1[:, c * P:(c + 1) * P],
                                                xT[k][:, h * HALF:(h + 1) * HALF], start=True, stop=True)
                    done.then_inc(ff1_ps, 1)
                pe.wait_ge(gelu_s, g * FC + FC)
                for j in range(G):
                    for c in range(FC):
                        done = nc.tensor.matmul(two_banks(4 * k + 2)[1][j], gT[k][:, c, j * HID:(j + 1) * HID], w2[:, c, :],
                                                start=(c == 0), stop=(c == FC - 1))
                done.then_inc(ff2_ps, 1)

            def group_c(i, first):
                for k in range(2):
                    g = i * 2 + k
                    if not (first and k == 0):
                        norm_T(g - 1, 1 - k)
                    pe.wait_ge(agg_s, g + 1)
                    for j in range(G):
                        done = nc.tensor.transpose(two_banks(4 * k)[1][j], qg[k][:, j, :], ident[:])
                    done.then_inc(aggT_ps, 1)
                    pe.wait_ge(aggT_s, g + 1)
                    if not first:
                        pe.wait_ge(x2_s, g - 1)
                    for j in range(G):
                        done = nc.tensor.matmul(two_banks(4 * k + 2)[1][j], xT[k][:, j * HID:(j + 1) * HID], wo[:],
                                                start=True, stop=True)
                    done.then_inc(att_ps, 1)
                    if not (first and k == 0):
                        ffn(g - 1, 1 - k)
            repeat(pe, PAIRS, group_c)
            norm_T(2 * PAIRS - 1, 1)
            ffn(2 * PAIRS - 1, 1)

            nc.tensor.transpose(ps[:, 0, 0:P], same_dst[:], ident[:]).then_inc(sameT_ps, 1)
            pe.wait_ge(sameT_s, 1)
            pe.wait_ge(sum_s, STEPS + 1)
            nc.tensor.matmul(ps[:, 1, 0:HID], sameT, rows[LAST][:, B - 1, :], start=True, stop=True)\
                .then_inc(carry1_ps, 1)
            pe.wait_ge(row1_s, 1)

            def group_e(i, first):
                for k in range(2):
                    g = i * 2 + k
                    flat, tiles = two_banks(4 * k)
                    pe.wait_ge(h_s, g + 1)
                    if not first:
                        pe.wait_ge(out_s, g - 1)
                    for j in range(G):
                        done = nc.tensor.transpose(tiles[j], hg[k][:, j, :], ident[:])
                    done.then_inc(hT_ps, 1)
                    pe.wait_ge(hT_s, g + 1)
                    for h in range(2):
                        done = nc.tensor.matmul(halves(4 * k + 2)[:, h, :], gw1[:], hT[k][:, h * HALF:(h + 1) * HALF],
                                                start=True, stop=True)
                    done.then_inc(mlp1_ps, 1)
                    pe.wait_ge(relu_s, g + 1)
                    for j in range(G):
                        done = nc.tensor.matmul(tiles[j], rT[k][:, j * HID:(j + 1) * HID], gw2[:], start=True, stop=True)
                    done.then_inc(mlp2_ps, 1)
            repeat(pe, PAIRS, group_e)

        @block.vector
        def _(dve):
            nc.vector.memset(dst_all, N).then_inc(memset_done, 1)
            nc.vector.memset(src_all[:], 0).then_inc(memset_done, 1)
            nc.vector.memset(nodes[FULL // 32 * 32:P, REST:NODE_COLS, :], 0.0).then_inc(memset_done, 1)
            nc.vector.memset(zeros, 0.0).then_inc(memset_done, 1)

            steps = [0]

            def step(ins):
                steps[0] += 1
                ins.then_inc(prep, 1)
                dve.wait_ge(prep, steps[0])

            step(nc.vector.memset(sum_i[:], 0))
            dve.wait_ge(consts, 11)
            dve.wait_ge(masks, 3)
            dve.wait_ge(edges_in, 64)
            step(nc.vector.tensor_copy(dst_f, dst_all))
            step(nc.vector.tensor_scalar(diag, ident[:], dst_f[:, STEPS - 1:STEPS], None, ALU.mult))
            step(nc.vector.tensor_copy(samples[:, 0:SAMPLES], dst_f[:, 0:STEPS:SAMPLE]))
            step(nc.vector.tensor_copy(samples[:, SAMPLES:SAMPLES + 1], chunk_i))
            step(nc.vector.tensor_tensor(step_back, ident[:], back_one, ALU.subtract))
            assert steps[0] == PREP_DIAG
            step(nc.vector.tensor_copy(node_f, node_i))
            step(nc.vector.tensor_copy(row_node, row_node_i))
            step(nc.vector.tensor_copy(first_less_j, col_i))
            step(nc.vector.tensor_scalar(first_less_j, first_less_j, -1.0, dst_f[:, 0:1], ALU.mult, ALU.add))
            step(nc.vector.memset(first_less_j[0:1, :], -float(NP)))
            step(nc.vector.memset(keep[:], 0.0))
            step(nc.vector.tensor_tensor(keep[:, 1:STEPS], dst_f[:, 1:STEPS], dst_f[:, 0:STEPS - 1], ALU.is_equal))
            step(nc.vector.tensor_scalar(pen[:], keep[:], -1.0, BIG, ALU.add, ALU.mult))
            dve.wait_ge(last_rows, 1)
            step(nc.vector.tensor_scalar(last_row, ps[:, 6, 0:P], dst_f[:, 0:1], None, ALU.is_equal))
            step(nc.vector.tensor_tensor(same_dst[:], last_row, earlier[:], ALU.mult))
            step(nc.vector.tensor_scalar(same_pen[:], same_dst[:], -1.0, BIG, ALU.add, ALU.mult))
            dve.wait_ge(sample_delta, 1)
            step(nc.vector.tensor_copy(deltas, ps[:, 7, 0:SAMPLES + 1]))
            assert steps[0] == PREP_ALL
            dve.wait_ge(x_first, 32)

            def last_edges(g, k, i):
                cols_g = bass.ds(g * G, G)
                dve.wait_ge(look_in[k], i * GWAIT + GWAIT)
                nc.vector.tensor_tensor(cmp3, look[k].bitcast(I32), spread(node_f[:, cols_g], SAMPLE), ALU.is_le)\
                    .then_inc(count_s, 1)
                dve.wait_ge(count_s, g * 2 + 1)
                nc.vector.tensor_reduce(cnt3, cmp3, AX.X, ALU.add).then_inc(count_s, 1)
                dve.wait_ge(count_s, g * 2 + 2)
                nc.vector.scalar_tensor_tensor(last_f[:, cols_g], block_f[:, cols_g], float(SAMPLE), cnt3,
                                               ALU.mult, ALU.add).then_inc(last_s, 1)

            def take_qkv(g, k, stored):
                if stored is not None:
                    dve.wait_ge(kv_stored[k], stored)
                for j in range(G):
                    m = g * G + j
                    dve.wait_ge(qkv_ps, m + 1)
                    nc.vector.tensor_tensor(kv_b[k][:, j, :], qkv_bank(j)[:, HID:3 * HID], bqkv[:, HID:3 * HID], ALU.add)
                    nc.vector.tensor_tensor(column(nodes, m), qkv_bank(j)[:, 0:HID], bqkv[:, 0:HID], ALU.add)\
                        .then_inc(kv_set, 1)

            def group_a(i, first):
                for k in range(2):
                    g = i * 2 + k
                    cols_g = bass.ds(g * G, G)
                    nc.vector.tensor_tensor(starts_ge[k], row_node.unsqueeze(1).to_broadcast([P, G, P]),
                                            spread(first_less_j[:, cols_g], P), ALU.is_ge).then_inc(starts, 1)
                    if first and k == 1:
                        dve.wait_ge(x_in, 32)
                    settle(dve)
                    norm_stats(dve, lnA[0], g + 1, [column(nodes, g * G + j) for j in range(G)])
                    dve.wait_ge(lnA[0].var, g + 1)
                    nc.vector.tensor_scalar_mul(nmean0[:, cols_g], lnA[0].mean_var[:, :, 0], -1.0)
                    norm_scale(dve, lnA[0], g + 1, rstd0[:, cols_g], nmr0)
                    if k == 1:
                        take_qkv(g - 1, 0, None if first else i * 16)
                    elif not first:
                        take_qkv(g - 1, 1, None if isinstance(i, int) and i == 1 else i * 16 - 16)
                    dve.wait_ge(h0_set, g + 1)
                    norm_stats(dve, lnA[1], g + 1, [h0_b[:, j, :] for j in range(G)])
                    norm_scale(dve, lnA[1], g + 1, rstd1, nmr1)
                    if not first:
                        last_edges(g - 2, k, i - 1)
                    dve.wait_ge(sample_row, g + 1)
                    got = ps[:, 6 + k, 0:G * (SAMPLES + 1)].rearrange("p (j s) -> p j s", j=G)
                    nc.vector.tensor_tensor(cmp2, got[:, :, 0:SAMPLES], spread(node_f[:, cols_g], SAMPLES), ALU.is_le)\
                        .then_inc(search_s, 1)
                    dve.wait_ge(search_s, g * 4 + 1)
                    nc.vector.tensor_reduce(cnt2, cmp2, AX.X, ALU.add).then_inc(search_s, 1)
                    dve.wait_ge(search_s, g * 4 + 2)
                    nc.vector.tensor_scalar(blk2, cnt2, -1.0, 0.0, ALU.add, ALU.max).then_inc(search_s, 1)
                    dve.wait_ge(search_s, g * 4 + 3)
                    nc.vector.scalar_tensor_tensor(block_f[:, cols_g], got[:, :, SAMPLES], float(SAMPLES), blk2,
                                                   ALU.mult, ALU.add).then_inc(search_s, 1)
                    dve.wait_ge(search_s, g * 4 + 4)
                    nc.vector.tensor_scalar_add(idx[k][:, 0:G], block_f[:, cols_g], 0.0).then_inc(block_idx, 1)
            repeat(dve, PAIRS, group_a, peel=2)
            take_qkv(2 * PAIRS - 1, 1, PAIRS * 16 - 16)
            for k in range(2):
                last_edges(2 * PAIRS - 2 + k, k, PAIRS - 1)

            placed = [0]

            def stage(ins):
                placed[0] += 1
                ins.then_inc(place, 1)
                dve.wait_ge(place, placed[0])

            dve.wait_ge(last_s, 2 * PAIRS)
            stage(nc.vector.tensor_scalar_add(last_f, last_f, -1.0))
            nc.vector.tensor_copy(last_i, last_f).then_inc(last_set, 1)
            stage(nc.vector.tensor_copy(first_i[:, 0:1], dst_f[:, 0:1]))
            stage(nc.vector.tensor_scalar_add(first_i[:, 1:2], dst_f[:, 0:1], 1.0))
            assert placed[0] == FIRSTS_SET
            dve.wait_ge(before_in, 16)
            stage(nc.vector.tensor_copy(before_f, before_i))
            stage(nc.vector.tensor_tensor(has_edges[:], last_f, before_f, ALU.is_gt))
            stage(nc.vector.tensor_scalar(start_f, has_edges[:], -NOWHERE, NOWHERE + 1.0, ALU.mult, ALU.add))
            stage(nc.vector.tensor_tensor(start_i[:], start_f, before_f, ALU.add))
            assert placed[0] == STARTS_SET
            stage(nc.vector.tensor_scalar_max(sum_i[:, 0:NODE_COLS], last_f, 0.0))
            dve.wait_ge(patch_in, 32)
            stage(nc.vector.tensor_copy(patch_f[:, 3:4], start_raw))
            stage(nc.vector.tensor_scalar_add(q_row_i[:], patch_f[:, 3:4], 1.0))
            stage(nc.vector.tensor_copy(patch_f[:, 0:1], patch_raw))
            stage(nc.vector.tensor_copy(patch_f[:, 1:2], chunk_start[:]))
            stage(nc.vector.tensor_scalar_add(patch_f[:, 1:2], patch_f[:, 1:2], float(STEPS)))
            stage(nc.vector.tensor_tensor(patch_f[:, 2:3], patch_f[:, 0:1], patch_f[:, 1:2], ALU.is_ge))
            stage(nc.vector.tensor_copy(patch_i[:, 0:1], patch_f[:, 0:1]))
            stage(nc.vector.scalar_tensor_tensor(patch_i[:, 1:2], patch_f[:, 2:3], NOWHERE, patch_f[:, 0:1],
                                                 ALU.mult, ALU.add))
            assert placed[0] == PLACED

            for k in range(2):
                dve.wait_ge(kv_stored[k], 16 * PAIRS)
            nc.vector.memset(stb[1][:, B - 1, :], 0.0)
            nc.vector.memset(top, -BIG)
            for k in range(2):
                done = nc.vector.memset(penb[k], -BIG)
            done.then_inc(edge_ready, 1)

            def fill(n, k, b):
                before = qb[k][:, b - 1, :] if b else qb[1 - k][:, B - 1, :]
                dve.wait_ge(q_filled, n * B + b)
                nc.vector.scalar_tensor_tensor(qb[k][:, b, :], before, keepb[k][:, b:b + 1], qb[k][:, b, :],
                                               ALU.mult, ALU.add).then_inc(q_filled, 1)

            dve.wait_ge(edge_ready, 1)
            dve.wait_ge(gates_set, 2)
            dve.wait_ge(q_in[0], 16)
            dve.wait_ge(q_first_in, 16)
            nc.vector.tensor_copy(qb[0][:, 0, :], q_first[:]).then_inc(q_filled, 1)
            for b in range(1, B):
                fill(0, 0, b)

            chunked = [0]

            def link(ins):
                chunked[0] += 1
                ins.then_inc(chunk_s, 1)
                dve.wait_ge(chunk_s, chunked[0])

            def chunk_tops():
                link(nc.vector.tensor_tensor(diag8, ident[:].unsqueeze(1).to_broadcast([P, NH, P]),
                                             spread(top[:, :, B], P), ALU.mult))

            def chunk_weights():
                dve.wait_ge(tops_ps, 1)
                link(nc.vector.tensor_tensor(masked, ps[:, 0:2, :].rearrange("p a (h c) -> p (a h) c", c=P),
                                             same_pen[:].unsqueeze(1).to_broadcast([P, NH, P]), ALU.add))
                link(nc.vector.tensor_reduce(carry_max, masked, AX.X, ALU.max))
                link(nc.vector.tensor_tensor(masked, masked, spread(carry_max, P), ALU.subtract))

            def masked_weights():
                dve.wait_ge(weight_s, 1)
                link(nc.vector.tensor_tensor(weight, weight, same_dst[:].unsqueeze(1).to_broadcast([P, NH, P]), ALU.mult))

            PIECES = 4

            def products(n, k, arrived, piece):
                b0, b1 = piece * B // PIECES, (piece + 1) * B // PIECES
                dve.wait_ge(kv_in[k], arrived)
                dve.wait_ge(q_filled, n * B + b1)
                keys = kvb[k][:, b0:b1, 0:HID]
                done = nc.vector.tensor_tensor(keys, keys, qb[k][:, b0:b1, :], ALU.mult)
                if piece == PIECES - 1:
                    done.then_inc(prod_s, 1)

            for piece in range(PIECES):
                products(0, 0, BW, piece)

            AHEAD = 5
            nc.vector.tensor_copy(score[:, :, 0], top[:, :, B]).then_inc(scan_s, 1)

            def batch_b(i, first):
                for k in range(2):
                    n = i * 2 + k
                    other = 1 - k
                    st = stb[k][:, :, 0:SW]
                    dve.wait_ge(prod_s, n + 1)
                    nc.vector.tensor_reduce(score[:, :, 1:CW].rearrange("p h t -> p t h"),
                                            kvb[k][:, :, 0:HID].rearrange("p b (h d) -> p b h d", d=HD), AX.X, ALU.add)\
                        .then_inc(scan_s, 1)
                    last = last_batch(n)
                    if not last:
                        dve.wait_ge(gates_set, n * 2 + 4)
                        if k == 0:
                            dve.wait_ge(q_in[1], i * 16 + 16)
                        else:
                            dve.wait_ge(q_in[0], i * 16 + 32)
                        fill(n + 1, other, 0)
                    dve.wait_ge(scan_s, n * 4 + 1)
                    dve.wait_ge(scan_s, n * 4 + 2)
                    flat = score.rearrange("p h t -> p (h t)")
                    nc.vector.tensor_tensor_scan(run_max, penb[k][:, 0:NH * CW], flat, 0.0, ALU.add, ALU.max)\
                        .then_inc(scan_s, 1)
                    if not last:
                        fill(n + 1, other, 1)
                    dve.wait_ge(scan_s, n * 4 + 3)
                    if not (first and k == 0):
                        dve.wait_ge(top_out, n)
                    nc.vector.tensor_tensor_scan(top.rearrange("p h t -> p (h t)")[:, ::-1],
                                                 penb[k][:, 1:NH * CW + 1][:, ::-1], run_max[:, ::-1], 0.0,
                                                 ALU.add, ALU.max).then_inc(scan_s, 1)
                    if not last:
                        fill(n + 1, other, 2)
                    dve.wait_ge(scan_s, n * 4 + 4)
                    nc.vector.tensor_tensor(dif, score, top, ALU.subtract).then_inc(dif_s, 1)
                    for b in range(3, AHEAD):
                        if not last:
                            fill(n + 1, other, b)
                    if last:
                        chunk_tops()
                    dve.wait_ge(rescale_s, n + 1)
                    nc.vector.tensor_tensor(carried.rearrange("p (h s) -> p h s", s=HS),
                                            stb[other][:, B - 1, 0:SW].rearrange("p (h s) -> p h s", s=HS),
                                            spread(rescale, HS), ALU.mult).then_inc(carried_s, 1)
                    dve.wait_ge(probs_s, n + 1)
                    heads = st.rearrange("p b (h s) -> p b h s", s=HS)
                    nc.vector.tensor_tensor(heads[:, :, :, 0:HD],
                                            kvb[k][:, :, HID:2 * HID].rearrange("p b (h d) -> p b h d", d=HD),
                                            heads[:, :, :, HD:HS].to_broadcast([P, B, NH, HD]), ALU.mult)\
                        .then_inc(weighed_s, 1)
                    dve.wait_ge(weighed_s, n + 1)
                    dve.wait_ge(carried_s, n + 1)
                    for b in range(B):
                        if b:
                            dve.wait_ge(state_s, n * B + b)
                        nc.vector.scalar_tensor_tensor(st[:, b, :], st[:, b - 1, :] if b else carried,
                                                       keepb[k][:, b:b + 1], st[:, b, :], ALU.mult, ALU.add)\
                            .then_inc(state_s, 1)
                        if b + AHEAD < B and not last:
                            fill(n + 1, other, b + AHEAD)
                        elif b == B // 2 and last:
                            chunk_weights()
                        elif b == B - 2 and last:
                            masked_weights()
                        elif b < B - 1 and not last:
                            products(n + 1, other, i * BW + (k + 1) * BW, b + AHEAD - B)
                        if b == B - 1 and not last:
                            nc.vector.tensor_copy(score[:, :, 0], top[:, :, B]).then_inc(scan_s, 1)
            repeat(dve, BPAIRS, batch_b, tail=1)

            dve.wait_ge(patch_row_in, 16)
            link(nc.vector.tensor_tensor(patch_top, patch_row[:, SW:RW], carry_max, ALU.max))
            link(nc.vector.tensor_tensor(patch_low[:, 0, :], patch_row[:, SW:RW], patch_top, ALU.subtract))
            link(nc.vector.tensor_tensor(patch_low[:, 1, :], carry_max, patch_top, ALU.subtract))
            link(nc.vector.tensor_copy(patch_row[:, SW:RW], patch_top))
            dve.wait_ge(patch_exp, 1)
            by_head = patch_row[:, 0:SW].rearrange("p (h s) -> p h s", s=HS)
            link(nc.vector.tensor_tensor(by_head, by_head, spread(patch_w[:, 0, :], HS), ALU.mult))
            dve.wait_ge(carry_ps, 1)
            link(nc.vector.tensor_tensor(patch_add, ps[:, 4, 0:SW].rearrange("p (h s) -> p h s", s=HS),
                                         spread(patch_w[:, 1, :], HS), ALU.mult))
            nc.vector.tensor_tensor(by_head, by_head, patch_add, ALU.add).then_inc(patch_done, 1)

            dve.wait_ge(patch_out, 16)
            for k in range(2):
                nc.vector.tensor_copy(node_idx[k][:], sum_i[:, k * G:(k + 1) * G]).then_inc(sum_idx, 1)

            def loop_scores(g, k, i):
                dve.wait_ge(ng_in[k], i * 48 + 48)
                here = nodes[:, bass.ds(g * G, G), :]
                nc.vector.tensor_tensor(qg[k], here, kvg[k][:, :, 0:HID], ALU.mult).then_inc(attend_s, 1)
                dve.wait_ge(attend_s, g * 9 + 1)
                nc.vector.tensor_reduce(self_e[k], qg[k].rearrange("p j (h d) -> p j h d", d=HD), AX.X, ALU.add)\
                    .then_inc(attend_s, 1)
                dve.wait_ge(attend_s, g * 9 + 2)
                dve.wait_ge(sg_in[k], i * GWAIT + GWAIT)
                tops = sg[k][:, :, SW:RW]
                low = [low_c[k][:, t, :].rearrange("p (j h) -> p j h", h=NH) for t in range(2)]
                nc.vector.tensor_tensor(top_c[k], tops, self_e[k], ALU.max).then_inc(attend_s, 1)
                dve.wait_ge(attend_s, g * 9 + 3)
                nc.vector.tensor_tensor(low[0], tops, top_c[k], ALU.subtract).then_inc(attend_s, 1)
                nc.vector.tensor_tensor(low[1], self_e[k], top_c[k], ALU.subtract).then_inc(low1_s, 1)

            def first_norm(g, k, i):
                dve.wait_ge(ng_in[k], i * 48 + 48)
                settle(dve)
                nc.vector.tensor_tensor(h0g[k], xg[k], spread(nmean0[:, bass.ds(g * G, G)], HID), ALU.add)\
                    .then_inc(centred_s, 1)
                dve.wait_ge(centred_s, g + 1)
                nc.vector.scalar_tensor_tensor(h0g[k], h0g[k], 0.0, spread(rstd0[:, bass.ds(g * G, G)], HID),
                                               ALU.max, ALU.mult).then_inc(h0_s, 1)

            def attend(g, k, i, between):
                n = g + 1
                vals_h = kvg[k][:, :, HID:2 * HID].rearrange("p j (h d) -> p j h d", d=HD)
                w = [w_c[k][:, t, :].rearrange("p (j h) -> p j h", h=NH) for t in range(2)]
                dve.wait_ge(w_cs, n)
                states = sg[k][:, :, 0:SW].rearrange("p j (h s) -> p j h s", s=HS)
                nc.vector.tensor_tensor(states, states, w[0].unsqueeze(3).to_broadcast([P, G, NH, HS]), ALU.mult)\
                    .then_inc(attend_s, 1)
                nc.vector.tensor_tensor(vals_h, vals_h, w[1].unsqueeze(3).to_broadcast([P, G, NH, HD]), ALU.mult)\
                    .then_inc(attend_s, 1)
                first_norm(g, k, i)
                if between:
                    norm_scale(dve, lnC[0], g, rstd2[1 - k], nmr2[1 - k])
                dve.wait_ge(attend_s, g * 9 + 5)
                nc.vector.tensor_tensor(rden[k], states[:, :, :, HD], w[1], ALU.add).then_inc(attend_s, 1)
                dve.wait_ge(attend_s, g * 9 + 6)
                nc.vector.tensor_tensor(vals_h, vals_h, states[:, :, :, 0:HD], ALU.add).then_inc(num_s, 1)
                dve.wait_ge(attend_s, g * 9 + 7)
                nc.vector.reciprocal(rden[k], rden[k]).then_inc(attend_s, 1)
                dve.wait_ge(attend_s, g * 9 + 8)
                nc.vector.tensor_tensor(rden[k], rden[k], spread(has_edges[:, bass.ds(g * G, G)], NH), ALU.mult)\
                    .then_inc(attend_s, 1)
                dve.wait_ge(attend_s, g * 9 + 9)
                dve.wait_ge(num_s, n)
                nc.vector.tensor_tensor(qg[k].rearrange("p j (h d) -> p j h d", d=HD), vals_h,
                                        rden[k].unsqueeze(3).to_broadcast([P, G, NH, HD]), ALU.mult).then_inc(agg_s, 1)
                nc.vector.tensor_copy(node_idx[k][:], sum_i[:, bass.ds((g + 2) * G, G)]).then_inc(sum_idx, 1)

            def add_attention(g, k):
                dve.wait_ge(att_ps, g + 1)
                dve.wait_ge(h0bo_s, g + 1)
                tiles = two_banks(4 * k + 2)[0].rearrange("p (j f) -> p j f", j=G)
                nc.vector.tensor_tensor(h0g[k], tiles, h0g[k], ALU.add).then_inc(x1_s, 1)
                dve.wait_ge(x1_s, g + 1)
                norm_stats(dve, lnC[0], g + 1, [h0g[k][:, j, :] for j in range(G)])

            def add_ffn(g, k):
                dve.wait_ge(ff2_ps, g + 1)
                dve.wait_ge(xb_s, g + 1)
                tiles = two_banks(4 * k + 2)[0].rearrange("p (j f) -> p j f", j=G)
                nc.vector.tensor_tensor(nodes[:, bass.ds(g * G, G), :], tiles, xb[k], ALU.add).then_inc(x2_s, 1)
                dve.wait_ge(x2_s, g + 1)
                settle(dve)
                norm_stats(dve, lnC[1], g + 1, [column(nodes, g * G + j) for j in range(G)])

            def group_c(i, first):
                for k in range(2):
                    g = i * 2 + k
                    if not (first and k == 0):
                        add_attention(g - 1, 1 - k)
                    attend(g, k, i, not (first and k == 0))
                    if not first:
                        add_ffn(g - 2, k)
                    if not last_group(g):
                        loop_scores(g + 1, 1 - k, i + k)
                    if not first:
                        norm_scale(dve, lnC[1], g - 1, rstd3[k], nmr3[k])
            loop_scores(0, 0, 0)
            repeat(dve, PAIRS, group_c, tail=1)
            add_attention(2 * PAIRS - 1, 1)
            norm_scale(dve, lnC[0], 2 * PAIRS, rstd2[1], nmr2[1])
            for k in range(2):
                add_ffn(2 * PAIRS - 2 + k, k)
                norm_scale(dve, lnC[1], 2 * PAIRS - 1 + k, rstd3[k], nmr3[k])

            for k in range(2):
                dve.wait_ge(h2_stored[k], 16 * PAIRS)
            for k in range(2):
                nc.vector.tensor_copy(node_idx[k][:], sum_i[:, k * G:(k + 1) * G]).then_inc(end_idx, 1)
            nc.vector.memset(rows[1][:, B - 1, :], 0.0).then_inc(sum_s, 1)

            def batch_d(i, first):
                for k in range(2):
                    n = i * 2 + k
                    dve.wait_ge(keep1_set, n + 1)
                    dve.wait_ge(rows_in[k], i * BW + BW)
                    for b in range(B):
                        dve.wait_ge(sum_s, n * B + b + 1)
                        before = rows[k][:, b - 1, :] if b else rows[1 - k][:, B - 1, :]
                        nc.vector.scalar_tensor_tensor(rows[k][:, b, :], before, keepd[k][:, b:b + 1], rows[k][:, b, :],
                                                       ALU.mult, ALU.add).then_inc(sum_s, 1)
            repeat(dve, BPAIRS, batch_d)
            dve.wait_ge(row1_in, 16)
            dve.wait_ge(carry1_ps, 1)
            nc.vector.tensor_tensor(patch_row1, patch_row1, ps[:, 1, 0:HID], ALU.add).then_inc(row1_s, 1)

            dve.wait_ge(row1_out, 16)
            nc.vector.tensor_scalar_add(eps1[:], eps1[:], 1.0).then_inc(eps_set, 1)
            dve.wait_ge(eps_set, 1)

            def output(g, k):
                here = nodes[:, bass.ds(g * G, G), :]
                nc.vector.tensor_tensor(here, here, gb2[:].unsqueeze(1).to_broadcast([P, G, HID]), ALU.add)\
                    .then_inc(xb2_s, 1)
                dve.wait_ge(xb2_s, g + 1)
                dve.wait_ge(mlp2_ps, g + 1)
                tiles = two_banks(4 * k)[0].rearrange("p (j f) -> p j f", j=G)
                nc.vector.tensor_tensor(here, tiles, here, ALU.add).then_inc(out_s, 1)

            def group_e(i, first):
                for k in range(2):
                    g = i * 2 + k
                    dve.wait_ge(nsum_in[k], i * GWAIT + GWAIT)
                    nc.vector.tensor_tensor(ng[k], ng[k], spread(has_edges[:, bass.ds(g * G, G)], HID), ALU.mult)\
                        .then_inc(masked_s, 1)
                    nc.vector.tensor_copy(node_idx[k][:], sum_i[:, bass.ds((g + 2) * G, G)]).then_inc(end_idx, 1)
                    dve.wait_ge(h2_in[k], i * 16 + 16)
                    dve.wait_ge(masked_s, g + 1)
                    nc.vector.scalar_tensor_tensor(hg[k], hg[k], eps1[:], ng[k], ALU.mult, ALU.add).then_inc(h_s, 1)
                    if not (first and k == 0):
                        output(g - 1, 1 - k)
            repeat(dve, PAIRS, group_e)
            output(2 * PAIRS - 1, 1)


_INS = ["x", "src", "dst"] + ["L0_gnn_" + n for n in (
    "Wq", "bq", "Wk", "bk", "Wv", "bv", "Wo", "bo", "g1", "b1", "g2", "b2", "W1", "bf1", "W2", "bf2")] + [
    "L1_gnn_" + n for n in ("eps", "W1", "b1", "W2", "b2")]


def kernel(**inputs):
    import numpy as np
    import concourse.bacc as bacc
    from concourse import mybir as mb
    from concourse.bass_utils import run_bass_kernel_spmd

    nc = bacc.Bacc("TRN2", target_bir_lowering=False, num_devices=1)
    arrays, aps = {}, {}
    for name in _INS:
        array = np.ascontiguousarray(inputs[name])
        arrays["in_" + name] = array
        aps[name] = nc.dram_tensor("in_" + name, array.shape, mb.dt.from_np(array.dtype), kind="ExternalInput").ap()
    out = nc.dram_tensor("out", (N, HID), mb.dt.float32, kind="ExternalOutput").ap()
    build(nc, aps, out)
    result = run_bass_kernel_spmd(nc, [arrays], core_ids=[0])
    return result.results[0]["out"]
```

```python
import concourse.bass as bass
from concourse import mybir
from contextlib import ExitStack

F32 = mybir.dt.float32
I32 = mybir.dt.int32
ALU = mybir.AluOpType
ACT = mybir.ActivationFunctionType
AX = mybir.AxisListType

P = 128
N = 12500
E = 200000
HID = 128
NH = 8
HD = HID // NH
FFN = 512
FC = FFN // P
LN_EPS = 1e-5

NODE_COLS = -(-N // P)
NP = P * NODE_COLS
FULL = N // NODE_COLS
REST = N - FULL * NODE_COLS
G = 7
PAIRS = NODE_COLS // (2 * G)
GW = G * HID
HALF = GW // 2

B = 16
BATCHES = -(-E // (P * B))
STEPS = B * BATCHES
EP = P * STEPS
EFULL = E // STEPS
EREST = E - EFULL * STEPS
BPAIRS = BATCHES // 2
SAMPLE = 32
SAMPLES = STEPS // SAMPLE

SORT_TILE = 125
assert E % SORT_TILE == 0 and SORT_TILE <= P

HS = HD + 1
SW = NH * HS
RW = SW + NH
BIG = 1e30
NOWHERE = float(1 << 21)
SCALE = 1.0 / HD ** 0.5

ARENA = 28000
WEIGHTS = 24
FIRST_COLUMNS = 2
COLUMNS_BY = (4, 5, 6, G)
FFN_COLUMNS = 5
QKV_BANKS = 4
ORDER_STEPS = 6
PREP_DIAG, PREP_ALL = 6, 18
FIRSTS_SET, STARTS_SET, PLACED = 3, 7, 16

assert NODE_COLS % (2 * G) == 0 and BATCHES % 2 == 0 and STEPS % SAMPLE == 0


class Carve:

    def __init__(self, tensor):
        self.tensor, self.at = tensor, 0

    def take(self, *shape):
        n = 1
        for s in shape:
            n *= s
        part = self.tensor[:, self.at:self.at + n]
        self.at += n
        assert self.at <= ARENA, self.at
        if len(shape) == 1:
            return part
        names = "abc"[:len(shape)]
        return part.rearrange(f"p ({' '.join(names)}) -> p {' '.join(names)}", **dict(zip(names[1:], shape[1:])))

    def two(self, *shape):
        return [self.take(*shape) for _ in range(2)]


def spread(ap, n):
    return ap.unsqueeze(2).to_broadcast([ap.shape[0], ap.shape[1], n])


def repeat(eng, count, body, peel=1, tail=0):
    for i in range(peel):
        body(i, i == 0)
    with eng.Fori(peel, count - tail) as i:
        body(i, False)
    for i in range(count - tail, count):
        body(i, False)


def build(nc, a, out):
    ctx = ExitStack()
    with ctx:
        def sb(name, shape, dt=F32):
            return ctx.enter_context(nc.sbuf_tensor(name, shape, dt))

        def sem(name):
            return ctx.enter_context(nc.semaphore(name))

        def sem2(name):
            return [sem(f"{name}{k}") for k in range(2)]

        def dram(name, shape, dt=F32):
            return nc.dram_tensor(name, shape, dt).ap()

        x_tail = dram("x_tail", [NODE_COLS, HID])
        kv_tab = dram("kv_tab", [NP, 2 * HID])
        h0_tab = dram("h0_tab", [NP, HID])
        h2_tab = dram("h2_tab", [NP, HID])
        q_edges = dram("q_edges", [EP, HID])
        states0 = dram("states0", [EP, RW])
        states1 = dram("states1", [EP, HID])
        dst_tab = dram("dst_tab", [EP // SAMPLE, SAMPLE], I32)
        count_tab = dram("count_tab", [NP, 1])
        total_tab = dram("total_tab", [P, 1])
        src_sorted, dst_sorted = dram("src_sorted", [E, 1], I32), dram("dst_sorted", [E, 1], I32)
        last_tab = dram("last_tab", [NP + 1, 1], I32)

        def by_node(tab):
            return tab.rearrange("(p j) f -> p j f", j=NODE_COLS)

        def by_step(tab):
            return tab.rearrange("(p t) f -> p t f", t=STEPS)

        nodes = sb("nodes", [P, NODE_COLS, HID])
        src_all = sb("src_all", [P, STEPS + 2 * B], I32)
        keep = sb("keep", [P, STEPS + B])
        pen = sb("pen", [P, STEPS + B])
        ident = sb("ident", [P, P])
        ones = sb("ones", [P, P])
        earlier = sb("earlier", [P, P])
        same_dst = sb("same_dst", [P, P])
        same_pen = sb("same_pen", [P, P])
        has_edges = sb("has_edges", [P, NODE_COLS])
        start_i = sb("start_i", [P, NODE_COLS], I32)
        sum_i = sb("sum_i", [P, NODE_COLS + 2 * G], I32)
        patch_i = sb("patch_i", [P, 2], I32)
        chunk_start = sb("chunk_start", [P, 1], I32)
        first_i = sb("first_i", [P, 2], I32)
        q_first = sb("q_first", [P, HID])
        q_row_i = sb("q_row_i", [P, 1], I32)
        idx = [sb(f"idx{k}", [P, B], I32) for k in range(2)]
        node_idx = [sb(f"node_idx{k}", [P, G], I32) for k in range(2)]
        eps_t = sb("eps_t", [P, 1])
        rstd0 = sb("rstd0", [P, NODE_COLS])
        self_e = sb("self_e", [P, NODE_COLS, NH])
        nmean0 = sb("nmean0", [P, NODE_COLS])
        eps1 = sb("eps1", [P, 1])
        wqkv = sb("wqkv", [P, 3 * HID])
        bqkv = sb("bqkv", [P, 3 * HID])
        wo = sb("wo", [P, HID])
        bo = sb("bo", [P, HID])
        cols = sb("cols", [P, 4])
        w1 = sb("w1", [P, FFN])
        bf1 = sb("bf1", [P, FC])
        w2 = sb("w2", [P, FC, HID])
        bf2 = sb("bf2", [P, HID])
        gw1 = sb("gw1", [P, HID])
        gb1 = sb("gb1", [P, 1])
        gw2 = sb("gw2", [P, HID])
        gb2 = sb("gb2", [P, HID])
        arena = sb("arena", [P, ARENA])
        ps = ctx.enter_context(nc.psum_tensor("ps", [P, 8, 512], F32))

        def two_banks(b):
            flat = ps[:, b:b + 2, :].rearrange("p a b -> p (a b)")
            return flat[:, 0:GW], [flat[:, j * HID:(j + 1) * HID] for j in range(G)]

        def qkv_bank(j):
            return ps[:, 2 + j % QKV_BANKS, 0:3 * HID]

        def halves(b):
            return ps[:, b:b + 2, 0:HALF]

        def column(ap, m):
            return ap[:, bass.ds(m, 1), :].rearrange("p a f -> p (a f)")

        class Norm:
            def __init__(self, tag, carve):
                self.steps = sem(f"{tag}_steps")
                self.std = sem(f"{tag}_std")
                self.stats, self.mean_var, self.dev = carve.take(G, 6), carve.take(G, 2), carve.take(G)

        def norm_stats(dve, ln, n, cols):
            for j in range(G):
                done = nc.vector.bn_stats(ln.stats[:, j, :], cols[j])
            done.then_inc(ln.steps, 1)
            dve.wait_ge(ln.steps, n * 4 - 3)
            settle(dve)
            for j in range(G):
                done = nc.vector.bn_aggr(ln.mean_var[:, j, :], ln.stats[:, j, :])
            done.then_inc(ln.steps, 1)

        def norm_root(act, ln, n):
            act.wait_ge(ln.steps, n * 4 - 2)
            nc.scalar.activation(ln.dev, ln.mean_var[:, :, 1], ACT.Sqrt, bias=eps_t[:]).then_inc(ln.std, 1)

        def norm_scale(dve, ln, n, rstd, nmr):
            dve.wait_ge(ln.std, n)
            settle(dve)
            nc.vector.reciprocal(rstd, ln.dev).then_inc(ln.steps, 1)
            dve.wait_ge(ln.steps, n * 4 - 1)
            nc.vector.scalar_tensor_tensor(nmr, ln.mean_var[:, :, 0], -1.0, rstd, ALU.mult, ALU.mult)\
                .then_inc(ln.steps, 1)

        def norm_act(to, cols, func, rstd, nmr):
            for j in range(G):
                done = nc.scalar.activation(to[:, j, :], cols[j], func, bias=nmr(j), scale=rstd(j))
            return done

        cA = Carve(arena)
        qs_b = cA.two(G, HID)
        zeros = cA.take(B, HID)
        dst_all = cA.take(STEPS).bitcast(I32)
        dst_f = cA.take(STEPS)
        last_row = cA.take(P)
        diag = cA.take(P)
        step_back = cA.take(P)
        back_one = cA.take(P)
        samples = cA.take(SAMPLES + 1)
        deltas = cA.take(SAMPLES + 1)
        row_node_i = cA.take(P).bitcast(I32)
        row_node = cA.take(P)
        node_i = cA.take(NODE_COLS).bitcast(I32)
        node_f = cA.take(NODE_COLS)
        col_i = cA.take(NODE_COLS).bitcast(I32)
        first_less_j = cA.take(NODE_COLS)
        block_f = cA.take(NODE_COLS)
        last_f = cA.take(NODE_COLS)
        last_i = cA.take(NODE_COLS).bitcast(I32)
        before_i = cA.take(NODE_COLS).bitcast(I32)
        before_f = cA.take(NODE_COLS)
        start_f = cA.take(NODE_COLS)
        minus1 = cA.take(1).bitcast(I32)
        chunk_i = cA.take(1).bitcast(I32)
        patch_raw = cA.take(1).bitcast(I32)
        patch_f = cA.take(4)
        starts_ge = cA.two(G, P)
        cmp2 = cA.take(G, SAMPLES)
        cnt2 = cA.take(G)
        blk2 = cA.take(G)
        look = cA.two(G, SAMPLE)
        cmp3 = cA.take(G, SAMPLE)
        cnt3 = cA.take(G)
        start_raw = cA.take(1).bitcast(I32)
        lnA = [Norm(f"lnA{t}", cA) for t in range(2)]
        nmr0, rstd1, nmr1 = cA.take(G), cA.take(G), cA.take(G)
        h0_b = cA.take(G, HID)
        hn_b = cA.take(G, HID)
        hnT = cA.take(GW)
        kv_b = cA.two(G, 2 * HID)
        qk = cA.take(G, HID)

        before_dst = cA.take(1).bitcast(I32)
        before_dst_f = cA.take(1)
        disorder_f = cA.take(1)
        disorder = cA.take(1).bitcast(I32)
        cS = Carve(arena)
        cS.at = cA.at
        tile_dst, tile_src, tile_pos = (cS.take(1).bitcast(I32) for _ in range(3))
        tile_count, tile_sum = cS.take(1), cS.take(1)
        dst_cols = cS.take(E // SORT_TILE).bitcast(I32)
        rank_cols = cS.take(E // SORT_TILE)
        tile_row = cS.take(SORT_TILE).bitcast(I32)
        tile_row_f, tile_dst_f = cS.take(SORT_TILE), cS.take(1)
        same = cS.take(2 * P).rearrange("p (k e) -> p k e", k=2)
        counts = cS.take(NODE_COLS)
        sums = cS.two(NODE_COLS)
        totals = cS.take(P)

        order_s = sem("order_s")
        disorder_ps = sem("disorder_ps")
        edges_sorted = sem("edges_sorted")
        memset_done = sem("memset_done")
        consts = sem("consts")
        masks = sem("masks")
        edges_in = sem("edges_in")
        x_first, x_in = sem("x_first"), sem("x_in")
        x_tail_in = sem("x_tail_in")
        weights_in = sem("weights_in")
        q_zeroed = sem2("q_zeroed")
        prep = sem("prep")
        sample_delta = sem("sample_delta")
        last_rows = sem("last_rows")
        dst_tab_in = sem("dst_tab_in")
        starts = sem("starts")
        sample_row = sem("sample_row")
        search_s = sem("search_s")
        block_idx = sem("block_idx")
        look_in = sem2("look_in")
        count_s = sem("count_s")
        last_s = sem("last_s")
        turns = sem("turns")
        h0_set, hn_set = sem("h0_set"), sem("hn_set")
        hn_T = sem("hn_T")
        hnT_set = sem("hnT_set")
        qkv_ps = sem("qkv_ps")
        kv_set = sem("kv_set")
        qk_s = sem("qk_s")
        kv_stored = sem2("kv_stored")
        last_set = sem("last_set")
        last_stored = sem("last_stored")
        before_in = sem("before_in")
        place = sem("place")
        patch_in = sem("patch_in")
        qs_copied = sem("qs_copied")
        qs_out = sem2("qs_out")
        q_first_in = sem("q_first_in")

        CW = B + 1
        cB = Carve(arena)
        diag8 = cB.take(NH, P)
        masked = cB.take(NH, P)
        weight = cB.take(NH, P)
        weightT = cB.take(NH, P)
        kvb = cB.two(B, 2 * HID)
        qb = cB.two(B, HID)
        stb = cB.two(B, RW)
        score = cB.take(NH, CW)
        run_max = cB.take(NH * CW)
        top = cB.take(NH, CW)
        dif = cB.take(NH, CW)
        penb = cB.two(NH * CW + 1)
        keepb = cB.two(B)
        rescale = cB.take(NH)
        carried = cB.take(SW)
        carry_max = cB.take(NH)
        patch_row = cB.take(RW)
        patch_top = cB.take(NH)
        patch_low = cB.take(2, NH)
        patch_w = cB.take(2, NH)
        patch_add = cB.take(NH, HS)

        edge_ready = sem("edge_ready")
        idx_set = sem("idx_set")
        gates_set = sem("gates_set")
        q_in, kv_in, states_out = sem2("q_in"), sem2("kv_in"), sem2("states_out")
        q_filled = sem("q_filled")
        prod_s, dif_s = sem("prod_s"), sem("dif_s")
        scan_s = sem("scan_s")
        probs_s, rescale_s, top_out = sem("probs_s"), sem("rescale_s"), sem("top_out")
        weighed_s, carried_s = sem("weighed_s"), sem("carried_s")
        state_s = sem("state_s")
        chunk_s = sem("chunk_s")
        tops_ps, weight_s, weightT_ps, weightT_s, carry_ps = (sem(n) for n in (
            "tops_ps", "weight_s", "weightT_ps", "weightT_s", "carry_ps"))
        patch_row_in, patch_exp, patch_done, patch_out = (sem(n) for n in (
            "patch_row_in", "patch_exp", "patch_done", "patch_out"))

        cC = Carve(arena)
        sg = cC.two(G, RW)
        beside = Carve(arena)
        beside.at = cB.at
        xg = beside.two(G, HID)
        vg = beside.two(G, HID)
        h0g = beside.two(G, HID)
        qg = cC.two(G, HID)
        top_c = cC.two(G, NH)
        low_c = cC.two(2, G * NH)
        w_c = cC.two(2, G * NH)
        rden = cC.two(G, NH)
        xT = cC.two(GW)
        gT = cC.two(FC, GW)
        xb = cC.two(G, HID)
        hn2 = cC.take(G, HID)
        gelu_load = cC.take(1)
        h2b = cC.two(G, HID)
        lnC = [Norm(f"lnC{t}", cC) for t in range(2)]
        rstd2, nmr2 = cC.two(G), cC.two(G)
        rstd3, nmr3 = cC.two(G), cC.two(G)
        assert cC.at <= cB.at

        sum_idx = sem("sum_idx")
        sg_in, ng_in = sem2("sg_in"), sem2("ng_in")
        attend_s = sem("attend_s")
        low1_s, w_cs, num_s, agg_s = (sem(n) for n in ("low1_s", "w_cs", "num_s", "agg_s"))
        (aggT_ps, aggT_s, att_ps, x1_s, hn2_s, hnT2_ps, hnT2_s, ff1_ps, gelu_s, ff2_ps, xsum_s, xb_s, x2_s,
         h2_s) = (sem(n) for n in ("aggT_ps", "aggT_s", "att_ps", "x1_s", "hn2_s", "hnT2_ps", "hnT2_s",
                                   "ff1_ps", "gelu_s", "ff2_ps", "xsum_s", "xb_s", "x2_s", "h2_s"))
        xw_in, h0_stored = sem2("xw_in"), sem2("h0_stored")
        centred_s, relu0_s, h0_s = sem("centred_s"), sem("relu0_s"), sem("h0_s")
        h2_stored = sem2("h2_stored")

        cD = Carve(arena)
        rows = cD.two(B, HID)
        keepd = cD.two(B)
        sameT = cD.take(P)
        patch_row1 = cD.take(HID)
        idx1_set, keep1_set = sem("idx1_set"), sem("keep1_set")
        rows_in, sums_out = sem2("rows_in"), sem2("sums_out")
        sum_s = sem("sum_s")
        sameT_ps, sameT_s, carry1_ps, row1_in, row1_s, row1_out = (sem(n) for n in (
            "sameT_ps", "sameT_s", "carry1_ps", "row1_in", "row1_s", "row1_out"))

        cE = Carve(arena)
        cE.at = cD.at
        ng = cE.two(G, HID)
        hg = cE.two(G, HID)
        hT = cE.two(GW)
        rT = cE.two(GW)
        end_idx, eps_set = sem("end_idx"), sem("eps_set")
        nsum_in, h2_in = sem2("nsum_in"), sem2("h2_in")
        masked_s, h_s, hT_ps, hT_s, mlp1_ps, relu_s, mlp2_ps, xb2_s, out_s = (sem(n) for n in (
            "masked_s", "h_s", "hT_ps", "hT_s", "mlp1_ps", "relu_s", "mlp2_ps", "xb2_s", "out_s"))
        out_stored = sem("out_stored")

        x_full = a["x"][0:FULL * NODE_COLS, :].rearrange("(p j) f -> p j f", j=NODE_COLS)
        x_rest = a["x"][FULL * NODE_COLS:N, :].rearrange("(p j) f -> p j f", p=1)
        LAST = (BATCHES - 1) % 2
        BW = 16 * B
        GWAIT = 16 * G

        def settle(eng):
            eng.sem_inc(turns, 1)

        def last_batch(n):
            return isinstance(n, int) and n == BATCHES - 1

        def last_group(g):
            return isinstance(g, int) and g == 2 * PAIRS - 1

        block = ctx.enter_context(nc.Block())

        @block.sync
        def _(sp):
            sp.wait_ge(memset_done, 3)
            sp.dma_start(before_dst[1:EFULL + 1, :],
                         a["dst"][0:EFULL * STEPS].rearrange("(p t) -> p t", t=STEPS)[:, STEPS - 1:STEPS],
                         allow_slow_non_contiguous=True).then_inc(edges_in, 16)
            for to, frm in ((dst_all, a["dst"]), (src_all, a["src"])):
                sp.dma_start(to[0:EFULL, 0:STEPS], frm[0:EFULL * STEPS].rearrange("(p t) -> p t", t=STEPS))\
                    .then_inc(edges_in, 16)
                sp.dma_start(to[EFULL:EFULL + 1, 0:EREST], frm[EFULL * STEPS:E].rearrange("(p t) -> p t", p=1))\
                    .then_inc(edges_in, 16)
            sp.wait_ge(memset_done, 4)
            sp.dma_start(nodes[0:FULL, 0:2 * G, :], x_full[:, 0:2 * G, :]).then_inc(x_first, 16)
            sp.dma_start(nodes[FULL:FULL + 1, 0:2 * G, :], x_rest[:, 0:2 * G, :]).then_inc(x_first, 16)
            sp.dma_start(nodes[0:FULL, 2 * G:NODE_COLS, :], x_full[:, 2 * G:NODE_COLS, :]).then_inc(x_in, 16)
            sp.dma_start(nodes[FULL:FULL + 1, 2 * G:REST, :], x_rest[:, 2 * G:REST, :]).then_inc(x_in, 16)
            sp.wait_ge(memset_done, 5)
            sp.dma_start(x_tail[0:REST, :], a["x"][FULL * NODE_COLS:N, :]).then_inc(x_tail_in, 16)
            sp.dma_start(x_tail[REST:NODE_COLS, :], zeros[0:NODE_COLS - REST, 0, :]).then_inc(x_tail_in, 16)

            def zero_fill(i, first):
                for k in range(2):
                    if not first:
                        sp.wait_ge(q_zeroed[k], i * 16)
                        settle(sp)
                    sp.dma_start(by_step(q_edges)[:, bass.ds((i * 2 + k) * B, B), :], zeros)\
                        .then_inc(q_zeroed[k], 16)
            repeat(sp, BPAIRS, zero_fill)

            def load_x(g, k, to, done):
                sp.dma_start(to[k][0:FULL, :, :], x_full[:, bass.ds(g * G, G), :]).then_inc(done[k], 16)
                sp.dma_start(to[k][FULL:FULL + 1, :, :],
                             x_tail[bass.ds(g * G, G), :].rearrange("(p j) f -> p j f", p=1)).then_inc(done[k], 16)

            def store_h0(g, k):
                sp.wait_ge(h0_s, g + 1)
                settle(sp)
                sp.dma_start(by_node(h0_tab)[:, bass.ds(g * G, G), :], h0g[k]).then_inc(h0_stored[k], 16)

            def group_w(i, first):
                for k in range(2):
                    g = i * 2 + k
                    if not first:
                        sp.wait_ge(centred_s, g - 1)
                        settle(sp)
                    load_x(g, k, xg, xw_in)
                    if not (first and k == 0):
                        store_h0(g - 1, 1 - k)
            sp.wait_ge(x_tail_in, 32)
            sp.wait_ge(edges_sorted, 1)
            repeat(sp, PAIRS, group_w)
            store_h0(2 * PAIRS - 1, 1)

            q_rows = by_step(q_edges)
            for k in range(2):
                sp.wait_ge(qs_out[k], GWAIT * PAIRS)
            sp.wait_ge(edge_ready, 1)
            sp.dma_start(qb[0], q_rows[:, 0:B, :]).then_inc(q_in[0], 16)

            def store_b(n, k):
                sp.wait_ge(state_s, n * B + B)
                settle(sp)
                sp.wait_ge(top_out, n + 1)
                settle(sp)
                sp.dma_start(by_step(states0)[:, bass.ds(n * B, B), :], stb[k]).then_inc(states_out[k], 16)

            def batch_b(i, first):
                for k in range(2):
                    n = i * 2 + k
                    if not last_batch(n):
                        sp.wait_ge(q_filled, n * B + 1)
                        settle(sp)
                        sp.dma_start(qb[1 - k], q_rows[:, bass.ds(n * B + B, B), :]).then_inc(q_in[1 - k], 16)
                    if not (first and k == 0):
                        store_b(n - 1, 1 - k)
            repeat(sp, BPAIRS, batch_b, tail=1)

            for k in range(2):
                sp.wait_ge(h0_stored[k], 16 * PAIRS)

            def group_c(i, first):
                for k in range(2):
                    g = i * 2 + k
                    if not first:
                        sp.wait_ge(xb_s, g - 1)
                        settle(sp)
                        sp.wait_ge(hn2_s, g - 1)
                        settle(sp)
                    load_x(g, k, xg, ng_in)
                    sp.dma_start(vg[k], by_node(kv_tab)[:, bass.ds(g * G, G), HID:2 * HID]).then_inc(ng_in[k], 16)
                    sp.dma_start(h0g[k], by_node(h0_tab)[:, bass.ds(g * G, G), :]).then_inc(ng_in[k], 16)
                    if not (first or isinstance(g, int) and g < 4):
                        store_h2(g - 4, k)

            def store_h2(g, k):
                sp.wait_ge(h2_s, g + 1)
                settle(sp)
                sp.dma_start(by_node(h2_tab)[:, bass.ds(g * G, G), :], h2b[k]).then_inc(h2_stored[k], 16)

            group_c(0, True)
            store_b(BATCHES - 1, LAST)
            group_c(1, False)
            with sp.Fori(2, PAIRS) as i:
                group_c(i, False)
            for g in range(2 * PAIRS - 4, 2 * PAIRS):
                store_h2(g, g % 2)

            def batch_d(i, first):
                for k in range(2):
                    n = i * 2 + k
                    sp.wait_ge(sum_s, n * B + B + 1)
                    settle(sp)
                    sp.dma_start(by_step(states1)[:, bass.ds(n * B, B), :], rows[k]).then_inc(sums_out[k], 16)
            repeat(sp, BPAIRS, batch_d)

            out_full = out[0:FULL * NODE_COLS, :].rearrange("(p j) f -> p j f", j=NODE_COLS)

            def store_out(i):
                sp.wait_ge(out_s, i * 2 + 2)
                settle(sp)
                cols_i = bass.ds(i * 2 * G, 2 * G)
                sp.dma_start(out_full[:, cols_i, :], nodes[0:FULL, cols_i, :]).then_inc(out_stored, 16)

            def group_e(i, first):
                for k in range(2):
                    g = i * 2 + k
                    if not first:
                        sp.wait_ge(hT_ps, g - 1)
                        settle(sp)
                    sp.dma_start(hg[k], by_node(h2_tab)[:, bass.ds(g * G, G), :]).then_inc(h2_in[k], 16)
                if not first:
                    store_out(i - 1)
            repeat(sp, PAIRS, group_e)
            sp.wait_ge(out_s, 2 * PAIRS)
            sp.dma_start(out[FULL * NODE_COLS:N, :].rearrange("(p j) f -> p j f", p=1),
                         nodes[FULL:FULL + 1, 0:REST, :]).then_inc(out_stored, 16)
            store_out(PAIRS - 1)
            sp.wait_ge(out_stored, 16 * (PAIRS + 1))

        @block.gpsimd
        def _(pool):
            def gather(to, tab, at, done):
                pool.indirect_dma_start(to, None, tab, bass.IndirectOffsetOnAxis(ap=at, axis=0)).then_inc(done, 16)

            def scatter(tab, at, frm, done):
                pool.indirect_dma_start(tab, bass.IndirectOffsetOnAxis(ap=at, axis=0), frm, None,
                                        bounds_check=EP - 1, oob_is_err=False).then_inc(done, 16)

            nc.gpsimd.memset(ident[:], 0.0).then_inc(consts, 1)
            nc.gpsimd.memset(back_one, 0.0).then_inc(consts, 1)
            nc.gpsimd.memset(earlier[:], 1.0).then_inc(consts, 1)
            nc.gpsimd.memset(ones[:], 1.0).then_inc(consts, 1)
            nc.gpsimd.memset(eps_t[:], LN_EPS).then_inc(consts, 1)
            nc.gpsimd.memset(minus1, -1).then_inc(consts, 1)
            nc.gpsimd.iota(node_i, [[1, NODE_COLS]], base=0, channel_multiplier=NODE_COLS).then_inc(consts, 1)
            nc.gpsimd.iota(col_i, [[1, NODE_COLS]], base=0, channel_multiplier=0).then_inc(consts, 1)
            nc.gpsimd.iota(row_node_i, [[NODE_COLS, P]], base=0, channel_multiplier=0).then_inc(consts, 1)
            nc.gpsimd.iota(chunk_i, [[1, 1]], base=0, channel_multiplier=1).then_inc(consts, 1)
            nc.gpsimd.iota(chunk_start[:], [[1, 1]], base=0, channel_multiplier=STEPS).then_inc(consts, 1)
            pool.wait_ge(consts, 11)
            nc.gpsimd.affine_select(out=ident[:], in_=ident[:], compare_op=ALU.not_equal, fill=1.0, base=0,
                                    pattern=[[-1, P]], channel_multiplier=1).then_inc(masks, 1)
            nc.gpsimd.affine_select(out=back_one, in_=back_one, compare_op=ALU.not_equal, fill=1.0, base=1,
                                    pattern=[[-1, P]], channel_multiplier=1).then_inc(masks, 1)
            nc.gpsimd.affine_select(out=earlier[:], in_=earlier[:], compare_op=ALU.is_gt, fill=0.0, base=0,
                                    pattern=[[-1, P]], channel_multiplier=1).then_inc(masks, 1)

            def sort_edges():
                row_in, count_in, count_out, src_in, base_in = (sem(f"sort_{n}") for n in (
                    "row_in", "count_in", "count_out", "src_in", "base_in"))
                placed_out = sem2("sort_placed_out")
                sort_s, pos_s = sem("sort_s"), sem("sort_pos_s")
                scan_s, scan_io = sem("sort_scan_s"), sem("sort_scan_io")
                scanned, moved = [0], [0]

                def scan_step(ins):
                    scanned[0] += 1
                    ins.then_inc(scan_s, 1)
                    pool.wait_ge(scan_s, scanned[0])

                def move(to, frm):
                    moved[0] += 16
                    pool.dma_start(to, frm).then_inc(scan_io, 16)
                    pool.wait_ge(scan_io, moved[0])

                T = SORT_TILE
                HALVES = [P >> k for k in range(1, 8)]
                TILE_STEPS = 5 + len(HALVES) + 2
                by_p = count_tab.rearrange("(p j) o -> p (j o)", j=NODE_COLS)
                scan_step(nc.gpsimd.memset(same, 0.0))
                scan_step(nc.gpsimd.memset(counts, 0.0))
                move(by_p, counts)

                with pool.Fori(0, E // T) as i:
                    here = bass.ds(i * T, T)
                    pool.dma_start(tile_row[0:T, :], a["dst"][here].partition_broadcast(T)).then_inc(row_in, 16)
                    pool.dma_start(tile_dst[0:T, :], a["dst"][here].rearrange("(p o) -> p o", o=1)).then_inc(row_in, 16)
                    pool.wait_ge(row_in, i * 32 + 32)
                    settle(pool)
                    pool.indirect_dma_start(tile_count[0:T, :], None, count_tab,
                                            bass.IndirectOffsetOnAxis(ap=tile_dst[0:T, :], axis=0)).then_inc(count_in, 16)
                    nc.gpsimd.tensor_copy(dst_cols[0:T, bass.ds(i, 1)], tile_dst[0:T, :]).then_inc(sort_s, 1)
                    nc.gpsimd.tensor_copy(tile_row_f[0:T, :], tile_row[0:T, :]).then_inc(sort_s, 1)
                    nc.gpsimd.tensor_copy(tile_dst_f[0:T, :], tile_dst[0:T, :]).then_inc(sort_s, 1)
                    pool.wait_ge(sort_s, i * TILE_STEPS + 3)
                    settle(pool)
                    nc.gpsimd.tensor_scalar(same[0:T, 0, 0:T], tile_row_f[0:T, :], tile_dst_f[0:T, :], None, ALU.is_equal)\
                        .then_inc(sort_s, 1)
                    pool.wait_ge(sort_s, i * TILE_STEPS + 4)
                    nc.gpsimd.tensor_tensor(same[0:T, 1, 0:T], same[0:T, 0, 0:T], earlier[0:T, 0:T], ALU.mult)\
                        .then_inc(sort_s, 1)
                    for k, half in enumerate(HALVES):
                        pool.wait_ge(sort_s, i * TILE_STEPS + 5 + k)
                        nc.gpsimd.tensor_tensor(same[0:T, :, 0:half], same[0:T, :, 0:half], same[0:T, :, half:2 * half],
                                                ALU.add).then_inc(sort_s, 1)
                    pool.wait_ge(sort_s, i * TILE_STEPS + TILE_STEPS - 2)
                    settle(pool)
                    pool.wait_ge(count_in, i * 16 + 16)
                    settle(pool)
                    nc.gpsimd.tensor_tensor(rank_cols[0:T, bass.ds(i, 1)], tile_count[0:T, :], same[0:T, 1, 0:1], ALU.add)\
                        .then_inc(sort_s, 1)
                    nc.gpsimd.tensor_tensor(tile_sum[0:T, :], tile_count[0:T, :], same[0:T, 0, 0:1], ALU.add)\
                        .then_inc(sort_s, 1)
                    pool.wait_ge(sort_s, i * TILE_STEPS + TILE_STEPS)
                    settle(pool)
                    pool.indirect_dma_start(count_tab, bass.IndirectOffsetOnAxis(ap=tile_dst[0:T, :], axis=0),
                                            tile_sum[0:T, :], None).then_inc(count_out, 16)
                    pool.wait_ge(count_out, i * 16 + 16)
                    settle(pool)

                move(counts, by_p)
                scan_step(nc.gpsimd.tensor_copy(sums[0], counts))
                now, shift = 0, 1
                while shift < NODE_COLS:
                    scan_step(nc.gpsimd.tensor_copy(sums[1 - now][:, 0:shift], sums[now][:, 0:shift]))
                    scan_step(nc.gpsimd.tensor_tensor(sums[1 - now][:, shift:NODE_COLS], sums[now][:, shift:NODE_COLS],
                                                      sums[now][:, 0:NODE_COLS - shift], ALU.add))
                    now, shift = 1 - now, shift * 2
                move(total_tab, sums[now][:, NODE_COLS - 1:NODE_COLS])
                move(totals, total_tab.rearrange("p o -> (p o)").partition_broadcast(P))
                scan_step(nc.gpsimd.tensor_tensor(totals, totals, earlier[:], ALU.mult))
                for half in HALVES:
                    scan_step(nc.gpsimd.tensor_tensor(totals[:, 0:half], totals[:, 0:half], totals[:, half:2 * half], ALU.add))
                scan_step(nc.gpsimd.tensor_tensor(counts, sums[now], counts, ALU.subtract))
                scan_step(nc.gpsimd.tensor_tensor(counts, counts, totals[:, 0:1].to_broadcast([P, NODE_COLS]), ALU.add))
                move(by_p, counts)

                with pool.Fori(0, E // T) as i:
                    pool.dma_start(tile_src[0:T, :], a["src"][bass.ds(i * T, T)].rearrange("(p o) -> p o", o=1))\
                        .then_inc(src_in, 16)
                    nc.gpsimd.tensor_copy(tile_dst[0:T, :], dst_cols[0:T, bass.ds(i, 1)]).then_inc(pos_s, 1)
                    pool.wait_ge(pos_s, i * 3 + 1)
                    settle(pool)
                    pool.indirect_dma_start(tile_count[0:T, :], None, count_tab,
                                            bass.IndirectOffsetOnAxis(ap=tile_dst[0:T, :], axis=0)).then_inc(base_in, 16)
                    pool.wait_ge(base_in, i * 16 + 16)
                    settle(pool)
                    nc.gpsimd.tensor_tensor(tile_sum[0:T, :], tile_count[0:T, :], rank_cols[0:T, bass.ds(i, 1)], ALU.add)\
                        .then_inc(pos_s, 1)
                    pool.wait_ge(pos_s, i * 3 + 2)
                    settle(pool)
                    nc.gpsimd.tensor_copy(tile_pos[0:T, :], tile_sum[0:T, :]).then_inc(pos_s, 1)
                    pool.wait_ge(pos_s, i * 3 + 3)
                    settle(pool)
                    pool.wait_ge(src_in, i * 16 + 16)
                    settle(pool)
                    for t, (tab, frm) in enumerate(((src_sorted, tile_src), (dst_sorted, tile_dst))):
                        pool.indirect_dma_start(tab, bass.IndirectOffsetOnAxis(ap=tile_pos[0:T, :], axis=0),
                                                frm[0:T, :], None).then_inc(placed_out[t], 16)
                    for t in range(2):
                        pool.wait_ge(placed_out[t], i * 16 + 16)
                        settle(pool)
                for to, tab in ((dst_all, dst_sorted), (src_all, src_sorted)):
                    move(to[0:EFULL, 0:STEPS], tab[0:EFULL * STEPS, :].rearrange("(p t) o -> p (t o)", t=STEPS))
                    move(to[EFULL:EFULL + 1, 0:EREST], tab[EFULL * STEPS:E, :].rearrange("(p t) o -> p (t o)", p=1))
                settle(pool)

            def weight_in(to, frm):
                pool.dma_start(to, frm).then_inc(weights_in, 16)

            def as_column(name):
                return a[name].rearrange("(p o) -> p o", o=1)

            for t, name in enumerate(("g1", "b1", "g2", "b2")):
                weight_in(cols[:, t:t + 1], as_column("L0_gnn_" + name))
            for t, name in enumerate("qkv"):
                weight_in(wqkv[:, t * HID:(t + 1) * HID], a["L0_gnn_W" + name])
                weight_in(bqkv[:, t * HID:(t + 1) * HID], a["L0_gnn_b" + name].partition_broadcast(P))

            pool.wait_ge(order_s, ORDER_STEPS + 1)
            unsorted = pool.value_load(disorder[0:1, 0:1], min_val=0, max_val=1)
            with pool.If(unsorted != 0):
                sort_edges()
            pool.sem_inc(edges_sorted, 1)

            weight_in(wo[:], a["L0_gnn_Wo"])
            weight_in(w1[:], a["L0_gnn_W1"])
            weight_in(w2[:], a["L0_gnn_W2"].rearrange("(c p) f -> p c f", p=P))
            for c in range(FC):
                weight_in(bf1[:, c:c + 1], a["L0_gnn_bf1"][c * P:(c + 1) * P].rearrange("(p o) -> p o", o=1))
            for to, name in ((bo, "L0_gnn_bo"), (bf2, "L0_gnn_bf2"), (gb2, "L1_gnn_b2"), (eps1, "L1_gnn_eps")):
                weight_in(to[:], a[name].partition_broadcast(P))
            weight_in(gw1[:], a["L1_gnn_W1"])
            weight_in(gw2[:], a["L1_gnn_W2"])
            weight_in(gb1[:], as_column("L1_gnn_b1"))

            pool.wait_ge(dst_tab_in, 16)

            def search(i, first):
                for k in range(2):
                    pool.wait_ge(block_idx, i * 2 + k + 1)
                    settle(pool)
                    for j in range(G):
                        gather(look[k][:, j, :].bitcast(I32), dst_tab, idx[k][:, j:j + 1], look_in[k])
            repeat(pool, PAIRS, search)

            pool.wait_ge(place, FIRSTS_SET)
            pool.wait_ge(last_stored, 32)
            gather(patch_raw, last_tab, first_i[:, 1:2], patch_in)
            gather(start_raw, last_tab, first_i[:, 0:1], patch_in)

            for k in range(2):
                pool.wait_ge(kv_stored[k], 16 * PAIRS)
            pool.wait_ge(edge_ready, 1)

            def batch_b(i, first):
                for k in range(2):
                    n = i * 2 + k
                    pool.wait_ge(idx_set, n + 1)
                    if not first:
                        pool.wait_ge(weighed_s, n - 1)
                    settle(pool)
                    for b in range(B):
                        gather(kvb[k][:, b, :], kv_tab, idx[k][:, b:b + 1], kv_in[k])
            batch_b(0, True)

            for k in range(2):
                pool.wait_ge(q_zeroed[k], 16 * BPAIRS)

            def scatter_q(i, first):
                for k in range(2):
                    pool.wait_ge(qs_copied, (i * 2 + k) * 2 + 2)
                    settle(pool)
                    for j in range(G):
                        scatter(q_edges, node_idx[k][:, j:j + 1], qs_b[k][:, j, :], qs_out[k])
            repeat(pool, PAIRS, scatter_q)

            for k in range(2):
                pool.wait_ge(qs_out[k], GWAIT * PAIRS)
            pool.wait_ge(place, PLACED)
            gather(q_first[:], q_edges, q_row_i[:], q_first_in)

            with pool.Fori(1, BPAIRS) as i:
                batch_b(i, False)

            for k in range(2):
                pool.wait_ge(states_out[k], 16 * BPAIRS)
            gather(patch_row, states0, patch_i[:, 0:1], patch_row_in)
            pool.wait_ge(patch_done, 1)
            scatter(states0, patch_i[:, 1:2], patch_row, patch_out)
            pool.wait_ge(patch_out, 16)

            def add_x(g, k):
                pool.wait_ge(x1_s, g + 1)
                nc.gpsimd.tensor_tensor(xb[k], h0g[k], bf2[:].unsqueeze(1).to_broadcast([P, G, HID]), ALU.add)\
                    .then_inc(xsum_s, 1)
                pool.wait_ge(xsum_s, g + 1)
                nc.gpsimd.tensor_tensor(xb[k], xb[k], xg[k], ALU.add).then_inc(xb_s, 1)

            def group_c(i, first):
                for k in range(2):
                    g = i * 2 + k
                    pool.wait_ge(sum_idx, g + 1)
                    if not first:
                        pool.wait_ge(num_s, g - 1)
                    settle(pool)
                    for j in range(G):
                        gather(sg[k][:, j, :], states0, node_idx[k][:, j:j + 1], sg_in[k])
                    if not first:
                        add_x(g - 2, k)
            repeat(pool, PAIRS, group_c)
            add_x(2 * PAIRS - 2, 0)
            add_x(2 * PAIRS - 1, 1)

            for k in range(2):
                pool.wait_ge(h2_stored[k], 16 * PAIRS)

            def batch_d(i, first):
                for k in range(2):
                    n = i * 2 + k
                    pool.wait_ge(idx1_set, n + 1)
                    if not first:
                        pool.wait_ge(sums_out[k], i * 16)
                    settle(pool)
                    for b in range(B):
                        if b == B - 1 and not (first and k == 0):
                            pool.wait_ge(sum_s, (n - 1) * B + 2)
                            settle(pool)
                        gather(rows[k][:, b, :], h2_tab, idx[k][:, b:b + 1], rows_in[k])
            repeat(pool, BPAIRS, batch_d)
            for k in range(2):
                pool.wait_ge(sums_out[k], 16 * BPAIRS)
            gather(patch_row1, states1, patch_i[:, 0:1], row1_in)
            pool.wait_ge(row1_s, 1)
            scatter(states1, patch_i[:, 1:2], patch_row1, row1_out)
            pool.wait_ge(row1_out, 16)

            def group_e(i, first):
                for k in range(2):
                    g = i * 2 + k
                    pool.wait_ge(end_idx, g + 1)
                    if not first:
                        pool.wait_ge(h_s, g - 1)
                    settle(pool)
                    for j in range(G):
                        gather(ng[k][:, j, :], states1, node_idx[k][:, j:j + 1], nsum_in[k])
            repeat(pool, PAIRS, group_e)

        @block.scalar
        def _(act):
            act.wait_ge(edges_sorted, 1)
            act.dma_start(dst_tab.rearrange("(p b) s -> p (b s)", p=P), dst_all).then_inc(dst_tab_in, 16)

            def store_kv(g, k):
                act.wait_ge(kv_set, g * G + G)
                act.dma_start(by_node(kv_tab)[:, bass.ds(g * G, G), :], kv_b[k]).then_inc(kv_stored[k], 16)

            def group_a(i, first):
                for k in range(2):
                    g = i * 2 + k
                    norm_root(act, lnA[0], g + 1)
                    act.wait_ge(lnA[0].steps, g * 4 + 4)
                    settle(act)
                    norm_act(h0_b, [column(nodes, g * G + j) for j in range(G)], ACT.Relu,
                             lambda j: rstd0[:, bass.ds(g * G + j, 1)], lambda j: nmr0[:, j:j + 1])\
                        .then_inc(h0_set, 1)
                    if not (first and k == 0):
                        store_kv(g - 1, 1 - k)
                    norm_root(act, lnA[1], g + 1)
                    act.wait_ge(lnA[1].steps, g * 4 + 4)
                    norm_act(hn_b, [h0_b[:, j, :] for j in range(G)], ACT.Identity,
                             lambda j: rstd1[:, j:j + 1], lambda j: nmr1[:, j:j + 1]).then_inc(hn_set, 1)
                    if first and k == 0:
                        act.wait_ge(weights_in, 16 * WEIGHTS)
                    act.wait_ge(hn_T, g + 1)
                    nc.scalar.activation(hnT, two_banks(0)[0], ACT.Identity, bias=cols[:, 1:2], scale=cols[:, 0:1])\
                        .then_inc(hnT_set, 1)
            repeat(act, PAIRS, group_a)
            store_kv(2 * PAIRS - 1, 1)

            act.wait_ge(last_set, 1)
            act.dma_start(last_tab[0:1, :], minus1[0:1, :]).then_inc(last_stored, 16)
            act.dma_start(last_tab[1:NP + 1, :].rearrange("(p j) o -> p (j o)", j=NODE_COLS), last_i)\
                .then_inc(last_stored, 16)
            act.wait_ge(last_stored, 32)
            act.dma_start(before_i, last_tab[0:NP, :].rearrange("(p j) o -> p (j o)", j=NODE_COLS))\
                .then_inc(before_in, 16)

            for k in range(2):
                nc.scalar.copy(idx[k][:], src_all[:, k * B:(k + 1) * B]).then_inc(idx_set, 1)

            act.wait_ge(place, STARTS_SET)

            def copy_q(i, first):
                for k in range(2):
                    g = (i * 2 + k) * G
                    if not first:
                        act.wait_ge(qs_out[k], i * GWAIT)
                        settle(act)
                    nc.scalar.copy(qs_b[k], nodes[:, bass.ds(g, G), :]).then_inc(qs_copied, 1)
                    nc.scalar.copy(node_idx[k][:], start_i[:, bass.ds(g, G)]).then_inc(qs_copied, 1)
            repeat(act, PAIRS, copy_q)

            act.wait_ge(edge_ready, 1)

            def gates(n, k):
                nc.scalar.copy(keepb[k], keep[:, bass.ds(n * B, B)]).then_inc(gates_set, 1)
                nc.scalar.copy(penb[k][:, 0:NH * CW].rearrange("p (h t) -> p h t", h=NH)[:, :, 1:CW],
                               pen[:, bass.ds(n * B, B)].unsqueeze(1).to_broadcast([P, NH, B])).then_inc(gates_set, 1)
            gates(0, 0)

            def batch_b(i, first):
                for k in range(2):
                    n = i * 2 + k
                    if not (first and k == 0):
                        act.wait_ge(state_s, n * B)
                        settle(act)
                    gates(n + 1, 1 - k)
                    act.wait_ge(prod_s, n + 1)
                    settle(act)
                    nc.scalar.copy(idx[k][:], src_all[:, bass.ds((n + 2) * B, B)]).then_inc(idx_set, 1)
                    act.wait_ge(dif_s, n + 1)
                    if not first:
                        act.wait_ge(states_out[k], i * 16)
                    heads = stb[k][:, :, 0:SW].rearrange("p b (h s) -> p h b s", s=HS)
                    nc.scalar.activation(rescale, dif[:, :, 0], ACT.Exp, scale=SCALE).then_inc(rescale_s, 1)
                    nc.scalar.activation(heads[:, :, :, HD], dif[:, :, 1:CW], ACT.Exp, scale=SCALE)\
                        .then_inc(probs_s, 1)
                    nc.scalar.copy(stb[k][:, :, SW:RW].rearrange("p b h -> p h b"), top[:, :, 1:CW])\
                        .then_inc(top_out, 1)
            repeat(act, BPAIRS, batch_b)

            act.wait_ge(chunk_s, 4)
            nc.scalar.activation(weight, masked, ACT.Exp, scale=SCALE).then_inc(weight_s, 1)
            act.wait_ge(weightT_ps, 1)
            nc.scalar.copy(weightT.rearrange("p h c -> p (h c)"), ps[:, 2:4, :].rearrange("p a b -> p (a b)"))\
                .then_inc(weightT_s, 1)
            act.wait_ge(chunk_s, 9)
            nc.scalar.activation(patch_w, patch_low, ACT.Exp, scale=SCALE).then_inc(patch_exp, 1)

            act.wait_ge(patch_out, 16)

            for k in range(2):
                nc.scalar.copy(idx[k][:], src_all[:, k * B:(k + 1) * B]).then_inc(idx1_set, 1)

            def norm2_T(g, k):
                act.wait_ge(hnT2_ps, g + 1)
                nc.scalar.activation(xT[k], two_banks(4 * k)[0], ACT.Identity, bias=cols[:, 3:4], scale=cols[:, 2:3])\
                    .then_inc(hnT2_s, 1)

            def norm3(g, k, start, stop, stored=None):
                if stored is not None:
                    act.wait_ge(h2_stored[k], stored)
                act.wait_ge(lnC[1].steps, g * 4 + 4)
                settle(act)
                for j in range(start, stop):
                    done = nc.scalar.activation(h2b[k][:, j, :], column(nodes, g * G + j), ACT.Relu,
                                                bias=nmr3[k][:, j:j + 1], scale=rstd3[k][:, j:j + 1])
                if stop == G:
                    done.then_inc(h2_s, 1)

            def gelus(g, k, norm3_too, start=0, stop=FC):
                for c in range(start, stop):
                    j = COLUMNS_BY[c - 1] if c else FIRST_COLUMNS
                    act.wait_ge(ff1_ps, g * FC + c + 1)
                    gelu(g, k, c)
                    if norm3_too and j < COLUMNS_BY[c]:
                        norm3(g - 2, k, j, COLUMNS_BY[c])

            def loop_exp(g, k):
                act.wait_ge(low1_s, g + 1)
                nc.scalar.activation(w_c[k], low_c[k], ACT.Exp, scale=SCALE).then_inc(w_cs, 1)

            def gelu(g, k, c):
                nc.scalar.activation(gT[k][:, c, :].rearrange("p (h f) -> p h f", h=2),
                                     halves(4 * k + 2 - 2 * (c % 2)), ACT.Gelu, bias=bf1[:, c:c + 1]).then_inc(gelu_s, 1)

            def group_c(i, first):
                for k in range(2):
                    g = i * 2 + k
                    if not (first and k == 0):
                        norm2_T(g - 1, 1 - k)
                        gelus(g - 1, 1 - k, not (isinstance(g, int) and g < 3), 0, 1)
                    act.wait_ge(aggT_ps, g + 1)
                    nc.scalar.copy(xT[k], two_banks(4 * k)[0]).then_inc(aggT_s, 1)
                    if not (first and k == 0):
                        gelus(g - 1, 1 - k, not (isinstance(g, int) and g < 3), 1, FC)
                    norm_root(act, lnC[0], g + 1)
                    if not first:
                        norm_root(act, lnC[1], g - 1)
                    if not last_group(g):
                        loop_exp(g + 1, 1 - k)
                    nc.scalar.activation(gelu_load, eps_t[:], ACT.Gelu)
                    if not first:
                        norm3(g - 2, k, 0, FIRST_COLUMNS, None if isinstance(i, int) and i == 1 else i * 16 - 16)
            loop_exp(0, 0)
            repeat(act, PAIRS, group_c, peel=2, tail=1)
            norm2_T(2 * PAIRS - 1, 1)
            gelus(2 * PAIRS - 1, 1, True)
            for k in range(2):
                norm_root(act, lnC[1], 2 * PAIRS - 1 + k)
                norm3(2 * PAIRS - 2 + k, k, 0, G, PAIRS * 16 - 16)

            act.wait_ge(sum_s, 1)

            def batch_d(i, first):
                for k in range(2):
                    n = i * 2 + k
                    if not first:
                        act.wait_ge(sum_s, (n - 1) * B + 1)
                        settle(act)
                    nc.scalar.copy(keepd[k], keep[:, bass.ds(n * B, B)]).then_inc(keep1_set, 1)
                    if not first:
                        nc.scalar.copy(idx[k][:], src_all[:, bass.ds(n * B, B)]).then_inc(idx1_set, 1)
            repeat(act, BPAIRS, batch_d)
            act.wait_ge(sameT_ps, 1)
            nc.scalar.copy(sameT, ps[:, 0, 0:P]).then_inc(sameT_s, 1)

            def group_e(i, first):
                for k in range(2):
                    g = i * 2 + k
                    act.wait_ge(hT_ps, g + 1)
                    nc.scalar.copy(hT[k], two_banks(4 * k)[0]).then_inc(hT_s, 1)
                    act.wait_ge(mlp1_ps, g + 1)
                    nc.scalar.activation(rT[k].rearrange("p (h f) -> p h f", h=2), halves(4 * k + 2), ACT.Relu,
                                         bias=gb1[:]).then_inc(relu_s, 1)
            repeat(act, PAIRS, group_e)

        @block.tensor
        def _(pe):
            pe.wait_ge(order_s, ORDER_STEPS)
            nc.tensor.matmul(ps[:, 6, 0:1], ones[:], disorder_f, start=True, stop=True).then_inc(disorder_ps, 1)
            pe.wait_ge(prep, PREP_DIAG)
            nc.tensor.matmul(ps[:, 6, 0:P], ones[:], diag, start=True, stop=True).then_inc(last_rows, 1)
            nc.tensor.matmul(ps[:, 7, 0:SAMPLES + 1], step_back, samples, start=True, stop=True)\
                .then_inc(sample_delta, 1)
            pe.wait_ge(prep, PREP_ALL)

            def group_a(i, first):
                for k in range(2):
                    g = i * 2 + k
                    pe.wait_ge(starts, g + 1)
                    for j in range(G):
                        done = nc.tensor.matmul(ps[:, 6 + k, j * (SAMPLES + 1):(j + 1) * (SAMPLES + 1)],
                                                starts_ge[k][:, j, :], deltas, start=True, stop=True)
                    done.then_inc(sample_row, 1)
                    pe.wait_ge(hn_set, g + 1)
                    for j in range(G):
                        done = nc.tensor.transpose(two_banks(0)[1][j], hn_b[:, j, :], ident[:])
                    done.then_inc(hn_T, 1)
                    if first and k == 0:
                        pe.wait_ge(weights_in, 16 * WEIGHTS)
                    pe.wait_ge(hnT_set, g + 1)
                    for j in range(G):
                        if j >= QKV_BANKS:
                            pe.wait_ge(kv_set, g * G + j - QKV_BANKS + 1)
                        elif not (first and k == 0):
                            pe.wait_ge(kv_set, (g - 1) * G + (G - 1 - j) // QKV_BANKS * QKV_BANKS + j + 1)
                        nc.tensor.matmul(qkv_bank(j), hnT[:, j * HID:(j + 1) * HID], wqkv[:], start=True, stop=True)\
                            .then_inc(qkv_ps, 1)
            repeat(pe, PAIRS, group_a)

            pe.wait_ge(chunk_s, 1)
            for t in range(2):
                done = nc.tensor.matmul(ps[:, t, :], ones[:], diag8[:, 4 * t:4 * t + 4, :].rearrange("p h c -> p (h c)"),
                                        start=True, stop=True)
            done.then_inc(tops_ps, 1)
            pe.wait_ge(chunk_s, 5)
            for h in range(NH):
                done = nc.tensor.transpose(ps[:, 2 + h // 4, (h % 4) * P:(h % 4 + 1) * P], weight[:, h, :], ident[:])
            done.then_inc(weightT_ps, 1)
            pe.wait_ge(weightT_s, 1)
            pe.wait_ge(state_s, STEPS)
            for h in range(NH):
                done = nc.tensor.matmul(ps[:, 4, h * HS:(h + 1) * HS], weightT[:, h, :],
                                        stb[LAST][:, B - 1, h * HS:(h + 1) * HS], start=True, stop=True)
            done.then_inc(carry_ps, 1)

            def norm_T(g, k):
                pe.wait_ge(hn2_s, g + 1)
                for j in range(G):
                    done = nc.tensor.transpose(two_banks(4 * k)[1][j], hn2[:, j, :], ident[:])
                done.then_inc(hnT2_ps, 1)

            def ffn1(g, k, chunks):
                pe.wait_ge(hnT2_s, g + 1)
                for c in chunks:
                    if c >= 2:
                        pe.wait_ge(gelu_s, g * FC + c - 1)
                    for h in range(2):
                        done = nc.tensor.matmul(halves(4 * k + 2 - 2 * (c % 2))[:, h, :], w1[:, c * P:(c + 1) * P],
                                                xT[k][:, h * HALF:(h + 1) * HALF], start=True, stop=True)
                    done.then_inc(ff1_ps, 1)

            def ffn2(g, k, between):
                pe.wait_ge(gelu_s, g * FC + FC)
                for j in range(G):
                    if between and j == FFN_COLUMNS:
                        norm_T(g + 1, 1 - k)
                    for c in range(FC):
                        done = nc.tensor.matmul(two_banks(4 * k + 2)[1][j], gT[k][:, c, j * HID:(j + 1) * HID], w2[:, c, :],
                                                start=(c == 0), stop=(c == FC - 1))
                done.then_inc(ff2_ps, 1)

            def group_c(i, first):
                for k in range(2):
                    g = i * 2 + k
                    if first and k == 1:
                        norm_T(0, 0)
                    if not (first and k == 0):
                        ffn1(g - 1, 1 - k, range(0, 2))
                    pe.wait_ge(agg_s, g + 1)
                    for j in range(G):
                        done = nc.tensor.transpose(two_banks(4 * k)[1][j], qg[k][:, j, :], ident[:])
                    done.then_inc(aggT_ps, 1)
                    if not (first and k == 0):
                        ffn1(g - 1, 1 - k, range(2, 3))
                    pe.wait_ge(aggT_s, g + 1)
                    if not first:
                        pe.wait_ge(x2_s, g - 1)
                    for j in range(G):
                        done = nc.tensor.matmul(two_banks(4 * k + 2)[1][j], xT[k][:, j * HID:(j + 1) * HID], wo[:],
                                                start=True, stop=True)
                    done.then_inc(att_ps, 1)
                    if not (first and k == 0):
                        ffn1(g - 1, 1 - k, range(3, FC))
                        ffn2(g - 1, 1 - k, True)
            repeat(pe, PAIRS, group_c)
            ffn1(2 * PAIRS - 1, 1, range(FC))
            ffn2(2 * PAIRS - 1, 1, False)

            nc.tensor.transpose(ps[:, 0, 0:P], same_dst[:], ident[:]).then_inc(sameT_ps, 1)
            pe.wait_ge(sameT_s, 1)
            pe.wait_ge(sum_s, STEPS + 1)
            nc.tensor.matmul(ps[:, 1, 0:HID], sameT, rows[LAST][:, B - 1, :], start=True, stop=True)\
                .then_inc(carry1_ps, 1)
            pe.wait_ge(row1_s, 1)

            def group_e(i, first):
                for k in range(2):
                    g = i * 2 + k
                    flat, tiles = two_banks(4 * k)
                    pe.wait_ge(h_s, g + 1)
                    if not first:
                        pe.wait_ge(out_s, g - 1)
                    for j in range(G):
                        done = nc.tensor.transpose(tiles[j], hg[k][:, j, :], ident[:])
                    done.then_inc(hT_ps, 1)
                    pe.wait_ge(hT_s, g + 1)
                    for h in range(2):
                        done = nc.tensor.matmul(halves(4 * k + 2)[:, h, :], gw1[:], hT[k][:, h * HALF:(h + 1) * HALF],
                                                start=True, stop=True)
                    done.then_inc(mlp1_ps, 1)
                    pe.wait_ge(relu_s, g + 1)
                    for j in range(G):
                        done = nc.tensor.matmul(tiles[j], rT[k][:, j * HID:(j + 1) * HID], gw2[:], start=True, stop=True)
                    done.then_inc(mlp2_ps, 1)
            repeat(pe, PAIRS, group_e)

        @block.vector
        def _(dve):
            nc.vector.memset(before_dst, 0).then_inc(memset_done, 1)
            nc.vector.memset(dst_all, N).then_inc(memset_done, 1)
            nc.vector.memset(src_all[:], 0).then_inc(memset_done, 1)
            nc.vector.memset(nodes[FULL // 32 * 32:P, REST:NODE_COLS, :], 0.0).then_inc(memset_done, 1)
            nc.vector.memset(zeros, 0.0).then_inc(memset_done, 1)

            steps = [0]

            def step(ins):
                steps[0] += 1
                ins.then_inc(prep, 1)
                dve.wait_ge(prep, steps[0])

            step(nc.vector.memset(sum_i[:], 0))
            dve.wait_ge(consts, 11)
            dve.wait_ge(masks, 3)
            dve.wait_ge(edges_in, 80)
            looked = [0]

            def look_step(ins):
                looked[0] += 1
                ins.then_inc(order_s, 1)
                dve.wait_ge(order_s, looked[0])

            look_step(nc.vector.tensor_copy(dst_f, dst_all))
            look_step(nc.vector.tensor_copy(before_dst_f, before_dst))
            look_step(nc.vector.tensor_tensor(keep[:, 1:STEPS], dst_f[:, 0:STEPS - 1], dst_f[:, 1:STEPS], ALU.is_gt))
            look_step(nc.vector.tensor_reduce(disorder_f, keep[:, 1:STEPS], AX.X, ALU.add))
            look_step(nc.vector.tensor_tensor(before_dst_f, before_dst_f, dst_f[:, 0:1], ALU.is_gt))
            look_step(nc.vector.tensor_tensor(disorder_f, disorder_f, before_dst_f, ALU.add))
            assert looked[0] == ORDER_STEPS
            dve.wait_ge(disorder_ps, 1)
            nc.vector.tensor_scalar_min(disorder, ps[:, 6, 0:1], 1.0).then_inc(order_s, 1)
            dve.wait_ge(edges_sorted, 1)
            step(nc.vector.tensor_copy(dst_f, dst_all))
            step(nc.vector.tensor_scalar(diag, ident[:], dst_f[:, STEPS - 1:STEPS], None, ALU.mult))
            step(nc.vector.tensor_copy(samples[:, 0:SAMPLES], dst_f[:, 0:STEPS:SAMPLE]))
            step(nc.vector.tensor_copy(samples[:, SAMPLES:SAMPLES + 1], chunk_i))
            step(nc.vector.tensor_tensor(step_back, ident[:], back_one, ALU.subtract))
            assert steps[0] == PREP_DIAG
            step(nc.vector.tensor_copy(node_f, node_i))
            step(nc.vector.tensor_copy(row_node, row_node_i))
            step(nc.vector.tensor_copy(first_less_j, col_i))
            step(nc.vector.tensor_scalar(first_less_j, first_less_j, -1.0, dst_f[:, 0:1], ALU.mult, ALU.add))
            step(nc.vector.memset(first_less_j[0:1, :], -float(NP)))
            step(nc.vector.memset(keep[:], 0.0))
            step(nc.vector.tensor_tensor(keep[:, 1:STEPS], dst_f[:, 1:STEPS], dst_f[:, 0:STEPS - 1], ALU.is_equal))
            step(nc.vector.tensor_scalar(pen[:], keep[:], -1.0, BIG, ALU.add, ALU.mult))
            dve.wait_ge(last_rows, 1)
            step(nc.vector.tensor_scalar(last_row, ps[:, 6, 0:P], dst_f[:, 0:1], None, ALU.is_equal))
            step(nc.vector.tensor_tensor(same_dst[:], last_row, earlier[:], ALU.mult))
            step(nc.vector.tensor_scalar(same_pen[:], same_dst[:], -1.0, BIG, ALU.add, ALU.mult))
            dve.wait_ge(sample_delta, 1)
            step(nc.vector.tensor_copy(deltas, ps[:, 7, 0:SAMPLES + 1]))
            assert steps[0] == PREP_ALL
            dve.wait_ge(x_first, 32)

            def last_edges(g, k, i):
                cols_g = bass.ds(g * G, G)
                dve.wait_ge(look_in[k], i * GWAIT + GWAIT)
                nc.vector.tensor_tensor(cmp3, look[k].bitcast(I32), spread(node_f[:, cols_g], SAMPLE), ALU.is_le)\
                    .then_inc(count_s, 1)
                dve.wait_ge(count_s, g * 2 + 1)
                nc.vector.tensor_reduce(cnt3, cmp3, AX.X, ALU.add).then_inc(count_s, 1)
                dve.wait_ge(count_s, g * 2 + 2)
                nc.vector.scalar_tensor_tensor(last_f[:, cols_g], block_f[:, cols_g], float(SAMPLE), cnt3,
                                               ALU.mult, ALU.add).then_inc(last_s, 1)

            def take_qkv(g, k, stored):
                if stored is not None:
                    dve.wait_ge(kv_stored[k], stored)
                for j in range(G):
                    m = g * G + j
                    dve.wait_ge(qkv_ps, m + 1)
                    nc.vector.tensor_tensor(kv_b[k][:, j, :], qkv_bank(j)[:, HID:3 * HID], bqkv[:, HID:3 * HID], ALU.add)
                    nc.vector.tensor_tensor(column(nodes, m), qkv_bank(j)[:, 0:HID], bqkv[:, 0:HID], ALU.add)\
                        .then_inc(kv_set, 1)

            def loop_products(g, k):
                dve.wait_ge(kv_set, g * G + G)
                nc.vector.tensor_tensor(qk, nodes[:, bass.ds(g * G, G), :], kv_b[k][:, :, 0:HID], ALU.mult)\
                    .then_inc(qk_s, 1)

            def loop_scores(g):
                dve.wait_ge(qk_s, g * 2 + 1)
                settle(dve)
                nc.vector.tensor_reduce(self_e[:, bass.ds(g * G, G), :], qk.rearrange("p j (h d) -> p j h d", d=HD), AX.X,
                                        ALU.add).then_inc(qk_s, 1)

            def group_a(i, first):
                for k in range(2):
                    g = i * 2 + k
                    cols_g = bass.ds(g * G, G)
                    nc.vector.tensor_tensor(starts_ge[k], row_node.unsqueeze(1).to_broadcast([P, G, P]),
                                            spread(first_less_j[:, cols_g], P), ALU.is_ge).then_inc(starts, 1)
                    if first and k == 1:
                        dve.wait_ge(x_in, 32)
                    settle(dve)
                    norm_stats(dve, lnA[0], g + 1, [column(nodes, g * G + j) for j in range(G)])
                    dve.wait_ge(lnA[0].steps, g * 4 + 2)
                    nc.vector.tensor_scalar_mul(nmean0[:, cols_g], lnA[0].mean_var[:, :, 0], -1.0)
                    norm_scale(dve, lnA[0], g + 1, rstd0[:, cols_g], nmr0)
                    if k == 1:
                        take_qkv(g - 1, 0, None if first else i * 16)
                    elif not first:
                        take_qkv(g - 1, 1, None if isinstance(i, int) and i == 1 else i * 16 - 16)
                    dve.wait_ge(h0_set, g + 1)
                    norm_stats(dve, lnA[1], g + 1, [h0_b[:, j, :] for j in range(G)])
                    if not (first and k == 0):
                        loop_products(g - 1, 1 - k)
                    norm_scale(dve, lnA[1], g + 1, rstd1, nmr1)
                    if not (first and k == 0):
                        loop_scores(g - 1)
                    if not first:
                        last_edges(g - 2, k, i - 1)
                    dve.wait_ge(sample_row, g + 1)
                    got = ps[:, 6 + k, 0:G * (SAMPLES + 1)].rearrange("p (j s) -> p j s", j=G)
                    nc.vector.tensor_tensor(cmp2, got[:, :, 0:SAMPLES], spread(node_f[:, cols_g], SAMPLES), ALU.is_le)\
                        .then_inc(search_s, 1)
                    dve.wait_ge(search_s, g * 4 + 1)
                    nc.vector.tensor_reduce(cnt2, cmp2, AX.X, ALU.add).then_inc(search_s, 1)
                    dve.wait_ge(search_s, g * 4 + 2)
                    nc.vector.tensor_scalar(blk2, cnt2, -1.0, 0.0, ALU.add, ALU.max).then_inc(search_s, 1)
                    dve.wait_ge(search_s, g * 4 + 3)
                    nc.vector.scalar_tensor_tensor(block_f[:, cols_g], got[:, :, SAMPLES], float(SAMPLES), blk2,
                                                   ALU.mult, ALU.add).then_inc(search_s, 1)
                    dve.wait_ge(search_s, g * 4 + 4)
                    nc.vector.tensor_scalar_add(idx[k][:, 0:G], block_f[:, cols_g], 0.0).then_inc(block_idx, 1)
            repeat(dve, PAIRS, group_a, peel=2)
            take_qkv(2 * PAIRS - 1, 1, PAIRS * 16 - 16)
            loop_products(2 * PAIRS - 1, 1)
            loop_scores(2 * PAIRS - 1)
            for k in range(2):
                last_edges(2 * PAIRS - 2 + k, k, PAIRS - 1)

            placed = [0]

            def stage(ins):
                placed[0] += 1
                ins.then_inc(place, 1)
                dve.wait_ge(place, placed[0])

            dve.wait_ge(last_s, 2 * PAIRS)
            stage(nc.vector.tensor_scalar_add(last_f, last_f, -1.0))
            nc.vector.tensor_copy(last_i, last_f).then_inc(last_set, 1)
            stage(nc.vector.tensor_copy(first_i[:, 0:1], dst_f[:, 0:1]))
            stage(nc.vector.tensor_scalar_add(first_i[:, 1:2], dst_f[:, 0:1], 1.0))
            assert placed[0] == FIRSTS_SET
            dve.wait_ge(before_in, 16)
            stage(nc.vector.tensor_copy(before_f, before_i))
            stage(nc.vector.tensor_tensor(has_edges[:], last_f, before_f, ALU.is_gt))
            stage(nc.vector.tensor_scalar(start_f, has_edges[:], -NOWHERE, NOWHERE + 1.0, ALU.mult, ALU.add))
            stage(nc.vector.tensor_tensor(start_i[:], start_f, before_f, ALU.add))
            assert placed[0] == STARTS_SET
            stage(nc.vector.tensor_scalar_max(sum_i[:, 0:NODE_COLS], last_f, 0.0))
            dve.wait_ge(patch_in, 32)
            stage(nc.vector.tensor_copy(patch_f[:, 3:4], start_raw))
            stage(nc.vector.tensor_scalar_add(q_row_i[:], patch_f[:, 3:4], 1.0))
            stage(nc.vector.tensor_copy(patch_f[:, 0:1], patch_raw))
            stage(nc.vector.tensor_copy(patch_f[:, 1:2], chunk_start[:]))
            stage(nc.vector.tensor_scalar_add(patch_f[:, 1:2], patch_f[:, 1:2], float(STEPS)))
            stage(nc.vector.tensor_tensor(patch_f[:, 2:3], patch_f[:, 0:1], patch_f[:, 1:2], ALU.is_ge))
            stage(nc.vector.tensor_copy(patch_i[:, 0:1], patch_f[:, 0:1]))
            stage(nc.vector.scalar_tensor_tensor(patch_i[:, 1:2], patch_f[:, 2:3], NOWHERE, patch_f[:, 0:1],
                                                 ALU.mult, ALU.add))
            assert placed[0] == PLACED

            for k in range(2):
                dve.wait_ge(kv_stored[k], 16 * PAIRS)
            nc.vector.memset(stb[1][:, B - 1, :], 0.0)
            nc.vector.memset(top, -BIG)
            for k in range(2):
                done = nc.vector.memset(penb[k], -BIG)
            done.then_inc(edge_ready, 1)

            def group_w(i, first):
                for k in range(2):
                    g = i * 2 + k
                    dve.wait_ge(xw_in[k], i * 32 + 32)
                    if not first:
                        dve.wait_ge(h0_stored[k], i * 16)
                    settle(dve)
                    nc.vector.tensor_tensor(h0g[k], xg[k], spread(nmean0[:, bass.ds(g * G, G)], HID), ALU.add)\
                        .then_inc(centred_s, 1)
                    dve.wait_ge(centred_s, g + 1)
                    nc.vector.scalar_tensor_tensor(h0g[k], h0g[k], 0.0, spread(rstd0[:, bass.ds(g * G, G)], HID),
                                                   ALU.max, ALU.mult).then_inc(relu0_s, 1)
                    dve.wait_ge(relu0_s, g + 1)
                    nc.vector.tensor_tensor(h0g[k], h0g[k], bo[:].unsqueeze(1).to_broadcast([P, G, HID]), ALU.add)\
                        .then_inc(h0_s, 1)
            repeat(dve, PAIRS, group_w)

            def fill(n, k, b):
                before = qb[k][:, b - 1, :] if b else qb[1 - k][:, B - 1, :]
                dve.wait_ge(q_filled, n * B + b)
                nc.vector.scalar_tensor_tensor(qb[k][:, b, :], before, keepb[k][:, b:b + 1], qb[k][:, b, :],
                                               ALU.mult, ALU.add).then_inc(q_filled, 1)

            dve.wait_ge(edge_ready, 1)
            dve.wait_ge(gates_set, 2)
            dve.wait_ge(q_in[0], 16)
            dve.wait_ge(q_first_in, 16)
            nc.vector.tensor_copy(qb[0][:, 0, :], q_first[:]).then_inc(q_filled, 1)
            for b in range(1, B):
                fill(0, 0, b)

            chunked = [0]

            def link(ins):
                chunked[0] += 1
                ins.then_inc(chunk_s, 1)
                dve.wait_ge(chunk_s, chunked[0])

            def chunk_tops():
                link(nc.vector.tensor_tensor(diag8, ident[:].unsqueeze(1).to_broadcast([P, NH, P]),
                                             spread(top[:, :, B], P), ALU.mult))

            def chunk_weights():
                dve.wait_ge(tops_ps, 1)
                link(nc.vector.tensor_tensor(masked, ps[:, 0:2, :].rearrange("p a (h c) -> p (a h) c", c=P),
                                             same_pen[:].unsqueeze(1).to_broadcast([P, NH, P]), ALU.add))
                link(nc.vector.tensor_reduce(carry_max, masked, AX.X, ALU.max))
                link(nc.vector.tensor_tensor(masked, masked, spread(carry_max, P), ALU.subtract))

            def masked_weights():
                dve.wait_ge(weight_s, 1)
                link(nc.vector.tensor_tensor(weight, weight, same_dst[:].unsqueeze(1).to_broadcast([P, NH, P]), ALU.mult))

            PIECES = 4

            def products(n, k, arrived, piece):
                b0, b1 = piece * B // PIECES, (piece + 1) * B // PIECES
                dve.wait_ge(kv_in[k], arrived)
                dve.wait_ge(q_filled, n * B + b1)
                keys = kvb[k][:, b0:b1, 0:HID]
                done = nc.vector.tensor_tensor(keys, keys, qb[k][:, b0:b1, :], ALU.mult)
                if piece == PIECES - 1:
                    done.then_inc(prod_s, 1)

            for piece in range(PIECES):
                products(0, 0, BW, piece)

            AHEAD = 5
            nc.vector.tensor_copy(score[:, :, 0], top[:, :, B]).then_inc(scan_s, 1)

            def batch_b(i, first):
                for k in range(2):
                    n = i * 2 + k
                    other = 1 - k
                    st = stb[k][:, :, 0:SW]
                    dve.wait_ge(prod_s, n + 1)
                    nc.vector.tensor_reduce(score[:, :, 1:CW].rearrange("p h t -> p t h"),
                                            kvb[k][:, :, 0:HID].rearrange("p b (h d) -> p b h d", d=HD), AX.X, ALU.add)\
                        .then_inc(scan_s, 1)
                    last = last_batch(n)
                    if not last:
                        dve.wait_ge(gates_set, n * 2 + 4)
                        if k == 0:
                            dve.wait_ge(q_in[1], i * 16 + 16)
                        else:
                            dve.wait_ge(q_in[0], i * 16 + 32)
                        fill(n + 1, other, 0)
                    dve.wait_ge(scan_s, n * 4 + 1)
                    dve.wait_ge(scan_s, n * 4 + 2)
                    flat = score.rearrange("p h t -> p (h t)")
                    nc.vector.tensor_tensor_scan(run_max, penb[k][:, 0:NH * CW], flat, 0.0, ALU.add, ALU.max)\
                        .then_inc(scan_s, 1)
                    if not last:
                        fill(n + 1, other, 1)
                    dve.wait_ge(scan_s, n * 4 + 3)
                    if not (first and k == 0):
                        dve.wait_ge(top_out, n)
                    nc.vector.tensor_tensor_scan(top.rearrange("p h t -> p (h t)")[:, ::-1],
                                                 penb[k][:, 1:NH * CW + 1][:, ::-1], run_max[:, ::-1], 0.0,
                                                 ALU.add, ALU.max).then_inc(scan_s, 1)
                    if not last:
                        fill(n + 1, other, 2)
                    dve.wait_ge(scan_s, n * 4 + 4)
                    nc.vector.tensor_tensor(dif, score, top, ALU.subtract).then_inc(dif_s, 1)
                    for b in range(3, AHEAD):
                        if not last:
                            fill(n + 1, other, b)
                    if last:
                        chunk_tops()
                    dve.wait_ge(rescale_s, n + 1)
                    nc.vector.tensor_tensor(carried.rearrange("p (h s) -> p h s", s=HS),
                                            stb[other][:, B - 1, 0:SW].rearrange("p (h s) -> p h s", s=HS),
                                            spread(rescale, HS), ALU.mult).then_inc(carried_s, 1)
                    dve.wait_ge(probs_s, n + 1)
                    heads = st.rearrange("p b (h s) -> p b h s", s=HS)
                    nc.vector.tensor_tensor(heads[:, :, :, 0:HD],
                                            kvb[k][:, :, HID:2 * HID].rearrange("p b (h d) -> p b h d", d=HD),
                                            heads[:, :, :, HD:HS].to_broadcast([P, B, NH, HD]), ALU.mult)\
                        .then_inc(weighed_s, 1)
                    dve.wait_ge(weighed_s, n + 1)
                    dve.wait_ge(carried_s, n + 1)
                    for b in range(B):
                        if b:
                            dve.wait_ge(state_s, n * B + b)
                        nc.vector.scalar_tensor_tensor(st[:, b, :], st[:, b - 1, :] if b else carried,
                                                       keepb[k][:, b:b + 1], st[:, b, :], ALU.mult, ALU.add)\
                            .then_inc(state_s, 1)
                        if b + AHEAD < B and not last:
                            fill(n + 1, other, b + AHEAD)
                        elif b == B // 2 and last:
                            chunk_weights()
                        elif b == B - 2 and last:
                            masked_weights()
                        elif b < B - 1 and not last:
                            products(n + 1, other, i * BW + (k + 1) * BW, b + AHEAD - B)
                        if b == B - 1 and not last:
                            nc.vector.tensor_copy(score[:, :, 0], top[:, :, B]).then_inc(scan_s, 1)
            repeat(dve, BPAIRS, batch_b, tail=1)

            dve.wait_ge(patch_row_in, 16)
            link(nc.vector.tensor_tensor(patch_top, patch_row[:, SW:RW], carry_max, ALU.max))
            link(nc.vector.tensor_tensor(patch_low[:, 0, :], patch_row[:, SW:RW], patch_top, ALU.subtract))
            link(nc.vector.tensor_tensor(patch_low[:, 1, :], carry_max, patch_top, ALU.subtract))
            link(nc.vector.tensor_copy(patch_row[:, SW:RW], patch_top))
            dve.wait_ge(patch_exp, 1)
            by_head = patch_row[:, 0:SW].rearrange("p (h s) -> p h s", s=HS)
            link(nc.vector.tensor_tensor(by_head, by_head, spread(patch_w[:, 0, :], HS), ALU.mult))
            dve.wait_ge(carry_ps, 1)
            link(nc.vector.tensor_tensor(patch_add, ps[:, 4, 0:SW].rearrange("p (h s) -> p h s", s=HS),
                                         spread(patch_w[:, 1, :], HS), ALU.mult))
            nc.vector.tensor_tensor(by_head, by_head, patch_add, ALU.add).then_inc(patch_done, 1)

            dve.wait_ge(patch_out, 16)
            for k in range(2):
                nc.vector.tensor_copy(node_idx[k][:], sum_i[:, k * G:(k + 1) * G]).then_inc(sum_idx, 1)

            def loop_maxima(g, k, i):
                loop = self_e[:, bass.ds(g * G, G), :]
                dve.wait_ge(sg_in[k], i * GWAIT + GWAIT)
                tops = sg[k][:, :, SW:RW]
                low = [low_c[k][:, t, :].rearrange("p (j h) -> p j h", h=NH) for t in range(2)]
                nc.vector.tensor_tensor(top_c[k], tops, loop, ALU.max).then_inc(attend_s, 1)
                dve.wait_ge(attend_s, g * 7 + 1)
                nc.vector.tensor_tensor(low[0], tops, top_c[k], ALU.subtract).then_inc(attend_s, 1)
                nc.vector.tensor_tensor(low[1], loop, top_c[k], ALU.subtract).then_inc(low1_s, 1)

            def norm2(g, k, used):
                norm_scale(dve, lnC[0], g + 1, rstd2[k], nmr2[k])
                dve.wait_ge(lnC[0].steps, g * 4 + 4)
                if used is not None:
                    dve.wait_ge(hnT2_ps, used)
                settle(dve)
                for j in range(G):
                    done = nc.vector.tensor_scalar(hn2[:, j, :], h0g[k][:, j, :], rstd2[k][:, j:j + 1], nmr2[k][:, j:j + 1],
                                                   ALU.mult, ALU.add)
                done.then_inc(hn2_s, 1)

            def attend(g, k, i, between):
                n = g + 1
                vals_h = vg[k].rearrange("p j (h d) -> p j h d", d=HD)
                w = [w_c[k][:, t, :].rearrange("p (j h) -> p j h", h=NH) for t in range(2)]
                if between:
                    norm2(g - 1, 1 - k, None if isinstance(i, int) and i == 0 else g - 1)
                if not (isinstance(g, int) and g < 3):
                    norm_scale(dve, lnC[1], g - 2, rstd3[1 - k], nmr3[1 - k])
                dve.wait_ge(w_cs, n)
                dve.wait_ge(ng_in[k], i * 64 + 64)
                states = sg[k][:, :, 0:SW].rearrange("p j (h s) -> p j h s", s=HS)
                nc.vector.tensor_tensor(states, states, w[0].unsqueeze(3).to_broadcast([P, G, NH, HS]), ALU.mult)\
                    .then_inc(attend_s, 1)
                nc.vector.tensor_tensor(vals_h, vals_h, w[1].unsqueeze(3).to_broadcast([P, G, NH, HD]), ALU.mult)\
                    .then_inc(attend_s, 1)
                dve.wait_ge(attend_s, g * 7 + 3)
                nc.vector.tensor_tensor(rden[k], states[:, :, :, HD], w[1], ALU.add).then_inc(attend_s, 1)
                dve.wait_ge(attend_s, g * 7 + 4)
                nc.vector.tensor_tensor(vals_h, vals_h, states[:, :, :, 0:HD], ALU.add).then_inc(num_s, 1)
                dve.wait_ge(attend_s, g * 7 + 5)
                nc.vector.reciprocal(rden[k], rden[k]).then_inc(attend_s, 1)
                dve.wait_ge(attend_s, g * 7 + 6)
                nc.vector.tensor_tensor(rden[k], rden[k], spread(has_edges[:, bass.ds(g * G, G)], NH), ALU.mult)\
                    .then_inc(attend_s, 1)
                dve.wait_ge(attend_s, g * 7 + 7)
                dve.wait_ge(num_s, n)
                nc.vector.tensor_tensor(qg[k].rearrange("p j (h d) -> p j h d", d=HD), vals_h,
                                        rden[k].unsqueeze(3).to_broadcast([P, G, NH, HD]), ALU.mult).then_inc(agg_s, 1)
                nc.vector.tensor_copy(node_idx[k][:], sum_i[:, bass.ds((g + 2) * G, G)]).then_inc(sum_idx, 1)

            def add_attention(g, k):
                dve.wait_ge(att_ps, g + 1)
                tiles = two_banks(4 * k + 2)[0].rearrange("p (j f) -> p j f", j=G)
                nc.vector.tensor_tensor(h0g[k], tiles, h0g[k], ALU.add).then_inc(x1_s, 1)
                dve.wait_ge(x1_s, g + 1)
                norm_stats(dve, lnC[0], g + 1, [h0g[k][:, j, :] for j in range(G)])

            def add_ffn(g, k):
                dve.wait_ge(ff2_ps, g + 1)
                dve.wait_ge(xb_s, g + 1)
                tiles = two_banks(4 * k + 2)[0].rearrange("p (j f) -> p j f", j=G)
                nc.vector.tensor_tensor(nodes[:, bass.ds(g * G, G), :], tiles, xb[k], ALU.add).then_inc(x2_s, 1)
                dve.wait_ge(x2_s, g + 1)
                settle(dve)
                norm_stats(dve, lnC[1], g + 1, [column(nodes, g * G + j) for j in range(G)])

            def group_c(i, first):
                for k in range(2):
                    g = i * 2 + k
                    if not (first and k == 0):
                        add_attention(g - 1, 1 - k)
                    attend(g, k, i, not (first and k == 0))
                    if not first:
                        add_ffn(g - 2, k)
                    if not last_group(g):
                        loop_maxima(g + 1, 1 - k, i + k)
            loop_maxima(0, 0, 0)
            repeat(dve, PAIRS, group_c, peel=2, tail=1)
            add_attention(2 * PAIRS - 1, 1)
            norm2(2 * PAIRS - 1, 1, 2 * PAIRS - 1)
            norm_scale(dve, lnC[1], 2 * PAIRS - 2, rstd3[1], nmr3[1])
            for k in range(2):
                add_ffn(2 * PAIRS - 2 + k, k)
                norm_scale(dve, lnC[1], 2 * PAIRS - 1 + k, rstd3[k], nmr3[k])

            for k in range(2):
                dve.wait_ge(h2_stored[k], 16 * PAIRS)
            for k in range(2):
                nc.vector.tensor_copy(node_idx[k][:], sum_i[:, k * G:(k + 1) * G]).then_inc(end_idx, 1)
            nc.vector.memset(rows[1][:, B - 1, :], 0.0).then_inc(sum_s, 1)

            def batch_d(i, first):
                for k in range(2):
                    n = i * 2 + k
                    dve.wait_ge(keep1_set, n + 1)
                    dve.wait_ge(rows_in[k], i * BW + BW)
                    for b in range(B):
                        dve.wait_ge(sum_s, n * B + b + 1)
                        before = rows[k][:, b - 1, :] if b else rows[1 - k][:, B - 1, :]
                        nc.vector.scalar_tensor_tensor(rows[k][:, b, :], before, keepd[k][:, b:b + 1], rows[k][:, b, :],
                                                       ALU.mult, ALU.add).then_inc(sum_s, 1)
            repeat(dve, BPAIRS, batch_d)
            dve.wait_ge(row1_in, 16)
            dve.wait_ge(carry1_ps, 1)
            nc.vector.tensor_tensor(patch_row1, patch_row1, ps[:, 1, 0:HID], ALU.add).then_inc(row1_s, 1)

            dve.wait_ge(row1_out, 16)
            nc.vector.tensor_scalar_add(eps1[:], eps1[:], 1.0).then_inc(eps_set, 1)
            dve.wait_ge(eps_set, 1)

            def output(g, k):
                here = nodes[:, bass.ds(g * G, G), :]
                nc.vector.tensor_tensor(here, here, gb2[:].unsqueeze(1).to_broadcast([P, G, HID]), ALU.add)\
                    .then_inc(xb2_s, 1)
                dve.wait_ge(xb2_s, g + 1)
                dve.wait_ge(mlp2_ps, g + 1)
                tiles = two_banks(4 * k)[0].rearrange("p (j f) -> p j f", j=G)
                nc.vector.tensor_tensor(here, tiles, here, ALU.add).then_inc(out_s, 1)

            def group_e(i, first):
                for k in range(2):
                    g = i * 2 + k
                    dve.wait_ge(nsum_in[k], i * GWAIT + GWAIT)
                    nc.vector.tensor_tensor(ng[k], ng[k], spread(has_edges[:, bass.ds(g * G, G)], HID), ALU.mult)\
                        .then_inc(masked_s, 1)
                    nc.vector.tensor_copy(node_idx[k][:], sum_i[:, bass.ds((g + 2) * G, G)]).then_inc(end_idx, 1)
                    dve.wait_ge(h2_in[k], i * 16 + 16)
                    dve.wait_ge(masked_s, g + 1)
                    nc.vector.scalar_tensor_tensor(hg[k], hg[k], eps1[:], ng[k], ALU.mult, ALU.add).then_inc(h_s, 1)
                    if not (first and k == 0):
                        output(g - 1, 1 - k)
            repeat(dve, PAIRS, group_e)
            output(2 * PAIRS - 1, 1)


_INS = ["x", "src", "dst"] + ["L0_gnn_" + n for n in (
    "Wq", "bq", "Wk", "bk", "Wv", "bv", "Wo", "bo", "g1", "b1", "g2", "b2", "W1", "bf1", "W2", "bf2")] + [
    "L1_gnn_" + n for n in ("eps", "W1", "b1", "W2", "b2")]


def kernel(**inputs):
    import numpy as np
    import concourse.bacc as bacc
    from concourse import mybir as mb
    from concourse.bass_utils import run_bass_kernel_spmd

    nc = bacc.Bacc("TRN2", target_bir_lowering=False, num_devices=1)
    arrays, aps = {}, {}
    for name in _INS:
        array = np.ascontiguousarray(inputs[name])
        arrays["in_" + name] = array
        aps[name] = nc.dram_tensor("in_" + name, array.shape, mb.dt.from_np(array.dtype), kind="ExternalInput").ap()
    out = nc.dram_tensor("out", (N, HID), mb.dt.float32, kind="ExternalOutput").ap()
    build(nc, aps, out)
    result = run_bass_kernel_spmd(nc, [arrays], core_ids=[0])
    return result.results[0]["out"]
```
